# Optimizing a Trainium2 kernel written in Bass

```python
import numpy as np
import jax
import jax.numpy as jnp

def _softmax(x, axis=-1):
    return jax.nn.softmax(x, axis=axis)

def _gelu(x):
    return jax.nn.gelu(x, approximate=True)

def _silu(x):
    return jax.nn.silu(x)

def _sigmoid(x):
    return jax.nn.sigmoid(x)

def _layernorm(x, axis=-1, eps=1e-05):
    m = jnp.mean(x, axis=axis, keepdims=True)
    v = jnp.var(x, axis=axis, keepdims=True)
    return (x - m) / jnp.sqrt(v + eps)

def _scatter_add(tgt, idx, src, axis=0):
    return tgt.at[idx].add(src)

def _segment_sum(src, seg, n):
    return jax.ops.segment_sum(src, seg, n)
kernel_name = 'mk_lm_tower_d1_tok_ids768_r4_ff0b1b'

def setup_inputs(seed: int=0):
    np.random.seed(seed)
    _w = jnp.asarray

    def _rec_inputs():
        import jax
        import jax.numpy as jnp
        _rk = jax.random.key(seed)
        x = jax.random.randint(jax.random.fold_in(_rk, 1), (8, 256), 0, 8000, jnp.int32)
        return x
    x = _rec_inputs()

    def _L0_tok_setup():
        import jax, jax.numpy as jnp
        import numpy as np
        V, S, D, H = (8000, 256, 192, 768)
        EPS = 1e-05

        def pos_encoding(seq_len, dim, dtype=jnp.float32):
            pos = jnp.arange(seq_len, dtype=dtype)[:, None]
            i = jnp.arange(dim, dtype=dtype)[None, :]
            ang = pos / jnp.power(jnp.asarray(10000.0, dtype), i / dim)
            even = (jnp.arange(dim) % 2 == 0)[None, :]
            return jnp.where(even, jnp.sin(ang), jnp.cos(ang))

        def layernorm2d(x, w, b):
            m = jnp.mean(x, axis=(-2, -1), keepdims=True)
            v = jnp.mean((x - m) ** 2, axis=(-2, -1), keepdims=True)
            return (x - m) / jnp.sqrt(v + EPS) * w + b
        key = jax.random.key(seed)
        ks = jax.random.split(key, 16)
        sc = 0.02
        emb = jax.random.normal(ks[0], (V, D), jnp.float32) * sc
        emb = emb.at[0].set(0.0)
        inp = {'x': jax.random.randint(ks[1], (8, S), 0, V), 'emb': emb, 'Wq': jax.random.normal(ks[2], (D, H), jnp.float32) * sc, 'bq': jnp.zeros((H,), jnp.float32), 'Wk': jax.random.normal(ks[3], (D, H), jnp.float32) * sc, 'bk': jnp.zeros((H,), jnp.float32), 'Wv': jax.random.normal(ks[4], (D, H), jnp.float32) * sc, 'bv': jnp.zeros((H,), jnp.float32), 'Wo': jax.random.normal(ks[5], (H, D), jnp.float32) * sc, 'bo': jnp.zeros((D,), jnp.float32), 'W1': jax.random.normal(ks[6], (D, H), jnp.float32) * sc, 'b1': jnp.zeros((H,), jnp.float32), 'W2': jax.random.normal(ks[7], (H, D), jnp.float32) * sc, 'b2': jnp.zeros((D,), jnp.float32), 'ln1_w': jnp.ones((S, D), jnp.float32), 'ln1_b': jnp.zeros((S, D), jnp.float32), 'ln2_w': jnp.ones((S, D), jnp.float32), 'ln2_b': jnp.zeros((S, D), jnp.float32)}
        return inp
    _L0_tok_all = _L0_tok_setup()
    _L0_tok_in = {k: v for k, v in _L0_tok_all.items() if k in ('emb', 'Wq', 'bq', 'Wk', 'bk', 'Wv', 'bv', 'Wo', 'bo', 'W1', 'b1', 'W2', 'b2', 'ln1_w', 'ln1_b', 'ln2_w', 'ln2_b')}
    del _L0_tok_all

    def _L0_attn_setup():
        import jax, jax.numpy as jnp
        import numpy as np
        import math
        DIM = 192
        NUM_HEADS = 12
        HEAD_DIM = DIM // NUM_HEADS
        EPS = 1e-06

        def rms_norm(x, w):
            xf = x.astype(jnp.float32)
            var = jnp.mean(xf * xf, axis=-1, keepdims=True)
            return (xf * jax.lax.rsqrt(var + EPS) * w).astype(x.dtype)
        key = jax.random.key(seed)
        ks = jax.random.split(key, 6)
        B, N, C = (4, 512, DIM)
        return {'x': jax.random.normal(ks[0], (B, N, C), dtype=jnp.float32), 'qkv_w': jax.random.normal(ks[1], (3 * C, C), dtype=jnp.float32) * C ** (-0.5), 'qkv_b': jax.random.normal(ks[2], (3 * C,), dtype=jnp.float32) * 0.02, 'proj_w': jax.random.normal(ks[3], (C, C), dtype=jnp.float32) * C ** (-0.5), 'proj_b': jax.random.normal(ks[4], (C,), dtype=jnp.float32) * 0.02, 'q_norm_w': jnp.ones((HEAD_DIM,), dtype=jnp.float32), 'k_norm_w': jnp.ones((HEAD_DIM,), dtype=jnp.float32)}
    _L0_attn_all = _L0_attn_setup()
    _L0_attn_in = {k: v for k, v in _L0_attn_all.items() if k in ('qkv_w', 'qkv_b', 'proj_w', 'proj_b', 'q_norm_w', 'k_norm_w')}
    del _L0_attn_all

    def _L0_ffn_setup():
        import jax, jax.numpy as jnp
        import numpy as np
        DIM = 192
        GROUP = 64
        E1, S1, E2 = (8, 16, 4)
        MULT = 4
        HID = int(DIM * MULT * 2 / 3)
        B, N = (4, 1024)

        def _l2norm(t, eps=1e-06):
            return t * jax.lax.rsqrt(jnp.sum(t * t, axis=-1, keepdims=True) + eps)

        def _forward(x, gamma_in, slots1, gamma2, w_slot2, w1, b1, w2, b2):
            b, n, d = x.shape
            G, g = (n // GROUP, GROUP)
            scale = d ** 0.5
            xn = _l2norm(x) * scale * gamma_in
            xg = xn.reshape(b, G, g, d)
            phi = _l2norm(slots1) * scale
            logits1 = jnp.einsum('bGgd,esd->bGges', xg, phi)
            disp1 = jax.nn.softmax(logits1, axis=2)
            comb1 = jax.nn.softmax(logits1.reshape(b, G, g, E1 * S1), -1)
            slots = jnp.einsum('bGgd,bGges->bGesd', xg, disp1)
            yn = _l2norm(slots) * scale * gamma2[None, None, :, None, :]
            ns = S1 // E2
            m = S1 // ns
            means = yn.reshape(b, G, E1, m, ns, d).mean(axis=4)
            se2 = jnp.einsum('bGkmd,kdf->bGkmf', means, w_slot2)
            se2 = se2.reshape(b, G, E1, m, E2, d).transpose(0, 1, 2, 4, 3, 5)
            se2 = _l2norm(se2) * scale
            logits2 = jnp.einsum('bGksd,bGkemd->bGksem', yn, se2)
            disp2 = jax.nn.softmax(logits2, axis=3)
            comb2 = jax.nn.softmax(logits2.reshape(b, G, E1, S1, E2 * m), -1)
            slots2 = jnp.einsum('bGksd,bGksem->bGkemd', yn, disp2)
            u = jnp.einsum('bGkemd,kedh->bGkemh', slots2, w1) + b1[None, None, :, :, None, :]
            v, gate = jnp.split(u, 2, axis=-1)
            act = v * jax.nn.gelu(gate)
            o = jnp.einsum('bGkemh,kehd->bGkemd', act, w2) + b2[None, None, :, :, None, :]
            out2 = jnp.einsum('bGkpd,bGksp->bGksd', o.reshape(b, G, E1, E2 * m, d), comb2)
            out = jnp.einsum('bGPd,bGgP->bGgd', out2.reshape(b, G, E1 * S1, d), comb1)
            return out.reshape(b, n, d)
        key = jax.random.key(seed)
        ks = jax.random.split(key, 8)
        p = lambda k, shape, s=0.02: jax.random.normal(k, shape, dtype=jnp.float32) * s
        return {'x': jax.random.normal(ks[0], (B, N, DIM), dtype=jnp.float32), 'gamma_in': jnp.ones((DIM,), jnp.float32), 'slots1': p(ks[1], (E1, S1, DIM), 1.0 / DIM ** 0.5), 'gamma2': jnp.ones((E1, DIM), jnp.float32), 'w_slot2': p(ks[2], (E1, DIM, E2 * DIM)), 'w1': p(ks[3], (E1, E2, DIM, 2 * HID)), 'b1': jnp.zeros((E1, E2, 2 * HID), jnp.float32), 'w2': p(ks[4], (E1, E2, HID, DIM)), 'b2': jnp.zeros((E1, E2, DIM), jnp.float32)}
    _L0_ffn_all = _L0_ffn_setup()
    _L0_ffn_in = {k: v for k, v in _L0_ffn_all.items() if k in ('gamma_in', 'slots1', 'gamma2', 'w_slot2', 'w1', 'b1', 'w2', 'b2')}
    del _L0_ffn_all
    return {'x': x, 'L0_tok_emb': _L0_tok_in['emb'], 'L0_tok_Wq': _L0_tok_in['Wq'], 'L0_tok_bq': _L0_tok_in['bq'], 'L0_tok_Wk': _L0_tok_in['Wk'], 'L0_tok_bk': _L0_tok_in['bk'], 'L0_tok_Wv': _L0_tok_in['Wv'], 'L0_tok_bv': _L0_tok_in['bv'], 'L0_tok_Wo': _L0_tok_in['Wo'], 'L0_tok_bo': _L0_tok_in['bo'], 'L0_tok_W1': _L0_tok_in['W1'], 'L0_tok_b1': _L0_tok_in['b1'], 'L0_tok_W2': _L0_tok_in['W2'], 'L0_tok_b2': _L0_tok_in['b2'], 'L0_tok_ln1_w': _L0_tok_in['ln1_w'], 'L0_tok_ln1_b': _L0_tok_in['ln1_b'], 'L0_tok_ln2_w': _L0_tok_in['ln2_w'], 'L0_tok_ln2_b': _L0_tok_in['ln2_b'], 'L0_attn_qkv_w': _L0_attn_in['qkv_w'], 'L0_attn_qkv_b': _L0_attn_in['qkv_b'], 'L0_attn_proj_w': _L0_attn_in['proj_w'], 'L0_attn_proj_b': _L0_attn_in['proj_b'], 'L0_attn_q_norm_w': _L0_attn_in['q_norm_w'], 'L0_attn_k_norm_w': _L0_attn_in['k_norm_w'], 'L0_ffn_gamma_in': _L0_ffn_in['gamma_in'], 'L0_ffn_slots1': _L0_ffn_in['slots1'], 'L0_ffn_gamma2': _L0_ffn_in['gamma2'], 'L0_ffn_w_slot2': _L0_ffn_in['w_slot2'], 'L0_ffn_w1': _L0_ffn_in['w1'], 'L0_ffn_b1': _L0_ffn_in['b1'], 'L0_ffn_w2': _L0_ffn_in['w2'], 'L0_ffn_b2': _L0_ffn_in['b2']}

def reference(x, L0_tok_emb, L0_tok_Wq, L0_tok_bq, L0_tok_Wk, L0_tok_bk, L0_tok_Wv, L0_tok_bv, L0_tok_Wo, L0_tok_bo, L0_tok_W1, L0_tok_b1, L0_tok_W2, L0_tok_b2, L0_tok_ln1_w, L0_tok_ln1_b, L0_tok_ln2_w, L0_tok_ln2_b, L0_attn_qkv_w, L0_attn_qkv_b, L0_attn_proj_w, L0_attn_proj_b, L0_attn_q_norm_w, L0_attn_k_norm_w, L0_ffn_gamma_in, L0_ffn_slots1, L0_ffn_gamma2, L0_ffn_w_slot2, L0_ffn_w1, L0_ffn_b1, L0_ffn_w2, L0_ffn_b2):
    import jax
    import jax.numpy as jnp

    def _L0_tok_ref(x, emb, Wq, bq, Wk, bk, Wv, bv, Wo, bo, W1, b1, W2, b2, ln1_w, ln1_b, ln2_w, ln2_b):
        import jax, jax.numpy as jnp
        import numpy as np
        V, S, D, H = (8000, 256, 192, 768)
        EPS = 1e-05

        def pos_encoding(seq_len, dim, dtype=jnp.float32):
            pos = jnp.arange(seq_len, dtype=dtype)[:, None]
            i = jnp.arange(dim, dtype=dtype)[None, :]
            ang = pos / jnp.power(jnp.asarray(10000.0, dtype), i / dim)
            even = (jnp.arange(dim) % 2 == 0)[None, :]
            return jnp.where(even, jnp.sin(ang), jnp.cos(ang))

        def layernorm2d(x, w, b):
            m = jnp.mean(x, axis=(-2, -1), keepdims=True)
            v = jnp.mean((x - m) ** 2, axis=(-2, -1), keepdims=True)
            return (x - m) / jnp.sqrt(v + EPS) * w + b
        y = emb[x]
        y = y + pos_encoding(y.shape[1], y.shape[2], y.dtype)
        q = y @ Wq + bq
        k = y @ Wk + bk
        v = y @ Wv + bv
        attn = jax.nn.softmax(jnp.einsum('bsh,bth->bst', q, k), axis=-1)
        a = jnp.einsum('bst,bth->bsh', attn, v) @ Wo + bo
        y = layernorm2d(y + a, ln1_w, ln1_b)
        f = jax.nn.gelu((y @ W1 + b1) @ W2 + b2, approximate=False)
        y = layernorm2d(y + f, ln2_w, ln2_b)
        return y

    def _L0_attn_ref(x, qkv_w, qkv_b, proj_w, proj_b, q_norm_w, k_norm_w):
        import jax, jax.numpy as jnp
        import numpy as np
        import math
        DIM = 192
        NUM_HEADS = 12
        HEAD_DIM = DIM // NUM_HEADS
        EPS = 1e-06

        def rms_norm(x, w):
            xf = x.astype(jnp.float32)
            var = jnp.mean(xf * xf, axis=-1, keepdims=True)
            return (xf * jax.lax.rsqrt(var + EPS) * w).astype(x.dtype)
        B, N, C = x.shape
        H, D = (NUM_HEADS, C // NUM_HEADS)
        qkv = x @ qkv_w.T + qkv_b
        qkv = qkv.reshape(B, N, 3, H, D).transpose(2, 0, 3, 1, 4)
        q, k, v = (qkv[0], qkv[1], qkv[2])
        q = rms_norm(q, q_norm_w)
        k = rms_norm(k, k_norm_w)
        scale = 1.0 / math.sqrt(D)
        w = jnp.einsum('bhnd,bhmd->bhnm', q.astype(jnp.float32), k.astype(jnp.float32)) * scale
        w = jax.nn.softmax(w, axis=-1).astype(v.dtype)
        out = jnp.einsum('bhnm,bhmd->bhnd', w, v)
        out = out.transpose(0, 2, 1, 3).reshape(B, N, C)
        return out @ proj_w.T + proj_b

    def _L0_ffn_ref(x, gamma_in, slots1, gamma2, w_slot2, w1, b1, w2, b2):
        import jax, jax.numpy as jnp
        import numpy as np
        DIM = 192
        GROUP = 64
        E1, S1, E2 = (8, 16, 4)
        MULT = 4
        HID = int(DIM * MULT * 2 / 3)
        B, N = (4, 1024)

        def _l2norm(t, eps=1e-06):
            return t * jax.lax.rsqrt(jnp.sum(t * t, axis=-1, keepdims=True) + eps)

        def _forward(x, gamma_in, slots1, gamma2, w_slot2, w1, b1, w2, b2):
            b, n, d = x.shape
            G, g = (n // GROUP, GROUP)
            scale = d ** 0.5
            xn = _l2norm(x) * scale * gamma_in
            xg = xn.reshape(b, G, g, d)
            phi = _l2norm(slots1) * scale
            logits1 = jnp.einsum('bGgd,esd->bGges', xg, phi)
            disp1 = jax.nn.softmax(logits1, axis=2)
            comb1 = jax.nn.softmax(logits1.reshape(b, G, g, E1 * S1), -1)
            slots = jnp.einsum('bGgd,bGges->bGesd', xg, disp1)
            yn = _l2norm(slots) * scale * gamma2[None, None, :, None, :]
            ns = S1 // E2
            m = S1 // ns
            means = yn.reshape(b, G, E1, m, ns, d).mean(axis=4)
            se2 = jnp.einsum('bGkmd,kdf->bGkmf', means, w_slot2)
            se2 = se2.reshape(b, G, E1, m, E2, d).transpose(0, 1, 2, 4, 3, 5)
            se2 = _l2norm(se2) * scale
            logits2 = jnp.einsum('bGksd,bGkemd->bGksem', yn, se2)
            disp2 = jax.nn.softmax(logits2, axis=3)
            comb2 = jax.nn.softmax(logits2.reshape(b, G, E1, S1, E2 * m), -1)
            slots2 = jnp.einsum('bGksd,bGksem->bGkemd', yn, disp2)
            u = jnp.einsum('bGkemd,kedh->bGkemh', slots2, w1) + b1[None, None, :, :, None, :]
            v, gate = jnp.split(u, 2, axis=-1)
            act = v * jax.nn.gelu(gate)
            o = jnp.einsum('bGkemh,kehd->bGkemd', act, w2) + b2[None, None, :, :, None, :]
            out2 = jnp.einsum('bGkpd,bGksp->bGksd', o.reshape(b, G, E1, E2 * m, d), comb2)
            out = jnp.einsum('bGPd,bGgP->bGgd', out2.reshape(b, G, E1 * S1, d), comb1)
            return out.reshape(b, n, d)
        return _forward(x, gamma_in, slots1, gamma2, w_slot2, w1, b1, w2, b2)
    h = _L0_tok_ref(x, L0_tok_emb, L0_tok_Wq, L0_tok_bq, L0_tok_Wk, L0_tok_bk, L0_tok_Wv, L0_tok_bv, L0_tok_Wo, L0_tok_bo, L0_tok_W1, L0_tok_b1, L0_tok_W2, L0_tok_b2, L0_tok_ln1_w, L0_tok_ln1_b, L0_tok_ln2_w, L0_tok_ln2_b)
    h = h + _L0_attn_ref(_layernorm(h, axis=-1), L0_attn_qkv_w, L0_attn_qkv_b, L0_attn_proj_w, L0_attn_proj_b, L0_attn_q_norm_w, L0_attn_k_norm_w)
    h = h + _L0_ffn_ref(_layernorm(h, axis=-1), L0_ffn_gamma_in, L0_ffn_slots1, L0_ffn_gamma2, L0_ffn_w_slot2, L0_ffn_w1, L0_ffn_b1, L0_ffn_w2, L0_ffn_b2)
    return h

_drawn_inputs = setup_inputs


def setup_inputs(seed=0):
    import zlib

    import numpy as np

    out = dict(_drawn_inputs(seed))
    spreads = {'L0_tok_bq': (0.0, 0.8),
     'L0_tok_bk': (0.0, 2.0),
     'L0_tok_bv': (0.0, 0.1),
     'L0_tok_bo': (0.0, 0.1),
     'L0_tok_b1': (0.0, 0.268),
     'L0_tok_b2': (0.0, 0.1),
     'L0_tok_ln1_w': (1.0, 0.2),
     'L0_tok_ln1_b': (0.0, 0.1),
     'L0_tok_ln2_w': (1.0, 0.2),
     'L0_tok_ln2_b': (0.0, 0.1),
     'L0_attn_q_norm_w': (1.0, 0.6),
     'L0_attn_k_norm_w': (1.0, 0.6),
     'L0_ffn_gamma_in': (1.0, 0.2),
     'L0_ffn_gamma2': (1.0, 0.6),
     'L0_ffn_b1': (0.0, 0.8),
     'L0_ffn_b2': (0.0, 0.321)}
    factors = {'L0_tok_Wq': 2.898,
     'L0_attn_qkv_b': 3.488,
     'L0_attn_proj_b': 3.487,
     'L0_ffn_w1': 3.956,
     'L0_ffn_w2': 3.782}
    for name, (base, spread) in spreads.items():
        noise = np.random.default_rng([zlib.crc32(name.encode()), seed]).standard_normal(out[name].shape)
        drawn = base * np.exp(spread * noise) if base else spread * noise
        out[name] = jnp.asarray(drawn.astype(out[name].dtype))
    for name, factor in factors.items():
        out[name] = (out[name] * factor).astype(out[name].dtype)
    return out
```

```python
from contextlib import ExitStack

import numpy as np

import concourse.bass as bass
from concourse import mybir

ALU = mybir.AluOpType
ACT = mybir.ActivationFunctionType
AX = mybir.AxisListType
F32 = mybir.dt.float32
BF16 = mybir.dt.bfloat16
U32 = mybir.dt.uint32

P = 128
BATCH, SEQ, DIM = 8, 256, 192
HALF = DIM // 2
AUG = HALF + 1
TILES = BATCH * SEQ // P
TPS = SEQ // P
TOK_HID = 768
HC = TOK_HID // P
HEADS, HDIM = 12, 16
GROUP = 64
GPS = SEQ // GROUP
NGROUPS = BATCH * GPS
E1, S1, E2 = 8, 16, 4
MEAN = 4
HID = 512
SLOTS = E1 * S1
W = 2
STEPS = BATCH // W
ROOT = float(DIM) ** 0.5
MASKED = -1.0e30
FRONT_OPERANDS = ("qkv_t", "proj_t", "ln_w1", "ln_b1", "ln_w2", "ln_b2", "pos", "qk_weights")
MOE_OPERANDS = ("gamma_in", "gamma2", "b2")
N_OPERANDS = len(FRONT_OPERANDS) + len(MOE_OPERANDS)
ds = bass.ds
EXP_LN = "natural_log_exp_and_others"


def pos_encoding():
    pos = np.arange(SEQ, dtype=np.float32)[:, None]
    i = np.arange(DIM, dtype=np.float32)[None, :]
    ang = pos / np.power(np.float32(10000.0), i / np.float32(DIM))
    return np.where((np.arange(DIM) % 2 == 0)[None, :], np.sin(ang), np.cos(ang)).astype(np.float32)


class Shared:

    def __init__(self):
        self.t = {}
        self.spent = []

    def stage_semaphore(self, stage, semaphore):
        s = stage.enter_context(semaphore)
        self.spent.append(s)
        return s


def clear_spent(nc, g):
    with nc.Block() as block:
        @block.sync
        def _(sp):
            for s in g.spent:
                sp.sem_clear(s)
    g.spent = []


def fold_weights(nc, g):
    with ExitStack() as ctx:
        sb = lambda name, shape, dt=F32: ctx.enter_context(nc.sbuf_tensor(name, shape, dt))
        sem = lambda name: g.stage_semaphore(ctx, nc.semaphore(name))
        wq_t = sb("wq_t", [P, HC, DIM + 1])
        wk_t = sb("wk_t", [P, HC, DIM + 1])
        wv_t = sb("wv_t", [P, HC, DIM + 1])
        w1_t = sb("w1_t", [P, HC, DIM + 1])
        wo = sb("wo", [P, HC, DIM])
        w2 = sb("w2", [P, HC, DIM])
        tail_bias = sb("tail_bias", [1, 2, DIM])
        last_row = sb("last_row", [1, AUG])
        slots_raw = sb("slots_raw", [P, DIM])
        slots_sq = sb("slots_sq", [P, DIM])
        slots_ss = sb("slots_ss", [P, 1])
        slots_ln = sb("slots_ln", [P, 1])
        slots_rn = sb("slots_rn", [P, 1])
        loaded_qk = sem("loaded_qk")
        loaded_v = sem("loaded_v")
        loaded_1 = sem("loaded_1")
        loaded_bias = sem("loaded_bias")
        loaded_slots = sem("loaded_slots")
        zeroed = sem("zeroed")
        row_set = sem("row_set")
        folded = sem("folded")
        slots_squared = sem("slots_squared")
        slots_logged = sem("slots_logged")
        slots_rooted = sem("slots_rooted")
        slots_normed = sem("slots_normed")
        slots_turned = sem("slots_turned")
        ident_zeroed = sem("ident_zeroed")
        masks_zeroed = sem("masks_zeroed")
        block = ctx.enter_context(nc.Block())

        @block.sync
        def _(sp):
            sp.dma_start(wq_t[:, :, :], g.d["wq_t"]).then_inc(loaded_qk, 16)
            sp.dma_start(wv_t[:, :, :], g.d["wv_t"]).then_inc(loaded_v, 16)
            sp.dma_start(w1_t[:, :, :], g.d["w1_t"]).then_inc(loaded_1, 16)
            sp.dma_start(tail_bias[:, :, :], g.d["tail_bias"]).then_inc(loaded_bias, 16)
            for name in FRONT_OPERANDS + MOE_OPERANDS:
                sp.dma_start(g.t[name], g.d[name]).then_inc(g.operands_loaded, 16)
            sp.wait_ge(g.operands_loaded, 16 * N_OPERANDS)

        @block.gpsimd
        def _(pool):
            pool.dma_start(g.ids[:, :], g.d["ids"]).then_inc(g.ids_loaded, 16)
            pool.wait_ge(g.ids_loaded, 16)
            for t in range(TILES):
                pool.indirect_dma_start(g.h[:, t, :], None, g.d["emb"],
                                        bass.IndirectOffsetOnAxis(ap=g.ids[:, t:t + 1], axis=0)
                                        ).then_inc(g.gathered, 16)
            nc.gpsimd.memset(g.ident[:, :], 0.0).then_inc(ident_zeroed, 1)
            nc.gpsimd.memset(g.average[:, :], 1.0 / MEAN).then_inc(masks_zeroed, 1)
            nc.gpsimd.memset(g.block_mask[:, :], 0.0).then_inc(masks_zeroed, 1)
            pool.wait_ge(ident_zeroed, 1)
            nc.gpsimd.affine_select(out=g.ident[:, :], in_=g.ident[:, :], compare_op=ALU.not_equal, fill=1.0,
                                    base=0, pattern=[[-1, P]], channel_multiplier=1).then_inc(g.ident_made, 1)
            pool.wait_ge(masks_zeroed, 2)
            nc.gpsimd.affine_select(out=g.average[:, :], in_=g.average[:, :], compare_op=ALU.is_ge, fill=0.0,
                                    base=0, pattern=[[-MEAN, P // MEAN]], channel_multiplier=1
                                    ).then_inc(masks_zeroed, 1)
            nc.gpsimd.affine_select(out=g.block_mask[:, :], in_=g.block_mask[:, :], compare_op=ALU.is_ge,
                                    fill=MASKED, base=0, pattern=[[-S1, E1], [0, S1]], channel_multiplier=1
                                    ).then_inc(masks_zeroed, 1)
            pool.wait_ge(masks_zeroed, 4)
            nc.gpsimd.affine_select(out=g.average[:, :], in_=g.average[:, :], compare_op=ALU.is_ge, fill=0.0,
                                    base=MEAN - 1, pattern=[[MEAN, P // MEAN]], channel_multiplier=-1
                                    ).then_inc(g.masks_made, 1)
            nc.gpsimd.affine_select(out=g.block_mask[:, :], in_=g.block_mask[:, :], compare_op=ALU.is_ge,
                                    fill=MASKED, base=S1 - 1, pattern=[[S1, E1], [0, S1]],
                                    channel_multiplier=-1).then_inc(g.masks_made, 1)

        @block.scalar
        def _(act):
            act.dma_start(wk_t[:, :, :], g.d["wk_t"]).then_inc(loaded_qk, 16)
            act.dma_start(wo[:, :, :], g.d["wo"]).then_inc(loaded_v, 16)
            act.dma_start(w2[:, :, :], g.d["w2"]).then_inc(loaded_1, 16)
            act.dma_start(slots_raw[:, :], g.d["slots1"]).then_inc(loaded_slots, 16)
            nc.scalar.preload_act_table_set(EXP_LN)
            act.wait_ge(loaded_slots, 16)
            nc.scalar.activation(slots_sq[:, :], slots_raw[:, :], ACT.Square,
                                 accum_out=slots_ss[:, :]).then_inc(slots_squared, 1)
            act.wait_ge(slots_squared, 1)
            act.wait_ge(g.consts_set, 1)
            nc.scalar.activation(slots_ln[:, :], slots_ss[:, :], ACT.Ln, bias=g.eps6[:, :]
                                 ).then_inc(slots_logged, 1)
            act.wait_ge(slots_logged, 1)
            nc.scalar.activation(slots_rn[:, :], slots_ln[:, :], ACT.Exp, scale=-0.5).then_inc(slots_rooted, 1)

        @block.tensor
        def _(pe):
            pe.wait_ge(loaded_qk, 32)
            for c in range(2):
                for j in range(HC):
                    last = nc.tensor.matmul(g.ps[c][0:AUG, 0:DIM + 1], wk_t[:, j, c * HALF:c * HALF + AUG],
                                            wq_t[:, j, :], start=(j == 0), stop=(j == HC - 1))
                last.then_inc(folded, 1)
            pe.wait_ge(zeroed, 1)
            pe.wait_ge(row_set, 1)
            pe.wait_ge(loaded_bias, 16)
            for n, (lhs, rhs, loaded) in enumerate(((wv_t, wo, loaded_v), (w1_t, w2, loaded_1))):
                pe.wait_ge(loaded, 32)
                for c in range(2):
                    bank = g.ps[2 + 2 * n + c]
                    for j in range(HC):
                        last = nc.tensor.matmul(bank[0:AUG, 0:DIM], lhs[:, j, c * HALF:c * HALF + AUG],
                                                rhs[:, j, :], start=(j == 0), stop=(c == 0 and j == HC - 1))
                    if c == 1:
                        last = nc.tensor.matmul(bank[0:AUG, 0:DIM], last_row[:, :], tail_bias[:, n, :],
                                                start=False, stop=True)
                    last.then_inc(folded, 1)
            pe.wait_ge(slots_normed, 1)
            pe.wait_ge(g.ident_made, 1)
            for c in range(2):
                last = nc.tensor.transpose(g.ps[6][0:HALF, c * P:(c + 1) * P],
                                           slots_raw[:, c * HALF:(c + 1) * HALF], g.ident[:, :])
            last.then_inc(slots_turned, 1)

        @block.vector
        def _(dve):
            nc.vector.memset(g.eps6[:, :], 1e-6)
            nc.vector.memset(g.eps5[:, :], 1e-5)
            nc.vector.memset(g.eps_norms[:, :], 1e-11 / DIM)
            nc.vector.memset(g.eps_dim[:, :], 1e-6 / DIM)
            nc.vector.memset(g.rms_eps[:, :], 1e-6).then_inc(g.consts_set, 1)
            nc.vector.memset(last_row[:, :], 0.0).then_inc(zeroed, 1)
            nc.vector.memset(g.mean_all[:, :], 1.0 / P).then_inc(g.consts_set, 1)
            dve.wait_ge(zeroed, 1)
            nc.vector.memset(last_row[:, HALF:AUG], 1.0).then_inc(row_set, 1)
            for s in range(W):
                nc.vector.memset(g.xt[s][HALF:AUG, :, :], 1.0).then_inc(g.ones_set, 1)
            for n, fold in enumerate((g.qk_fold, g.vo_fold, g.mlp_fold)):
                for c in range(2):
                    dve.wait_ge(folded, 2 * n + c + 1)
                    nc.vector.tensor_copy(fold[:, c, :], g.ps[2 * n + c][0:AUG, 0:fold.shape[2]]
                                          ).then_inc(g.folds_ready, 1)
            dve.wait_ge(slots_rooted, 1)
            nc.vector.tensor_scalar(slots_raw[:, :], slots_raw[:, :], slots_rn[:, :], ROOT, ALU.mult, ALU.mult
                                    ).then_inc(slots_normed, 1)
            dve.wait_ge(slots_turned, 1)
            nc.vector.tensor_copy(g.phi_t[:, :, :], g.ps[6][0:HALF, 0:2 * P].rearrange("p (c n) -> p c n", c=2)
                                  ).then_inc(g.folds_ready, 1)


def token_mixer(nc, g):
    with ExitStack() as ctx:
        def sb(name, shape, dt=F32):
            return [ctx.enter_context(nc.sbuf_tensor(f"{name}{s}", shape, dt)) for s in range(W)]

        sem = lambda name: g.stage_semaphore(ctx, nc.semaphore(name))
        y = sb("y", [P, TPS, DIM])
        key_t = sb("key_t", [AUG, 2, SEQ])
        value = sb("value", [P, TPS, DIM])
        prob = sb("prob", [P, TPS, SEQ])
        prob_t = sb("prob_t", [P, TPS, SEQ])
        neg_max = sb("neg_max", [P, TPS])
        row_sum = sb("row_sum", [P, TPS])
        inv_sum = sb("inv_sum", [P, TPS])
        f_out = sb("f_out", [P, TPS, DIM])
        bn = sb("bn", [P, TPS, 6])
        stat = sb("stat", [P, 2])
        neg_var = sb("neg_var", [P, 1])
        log_var = sb("log_var", [P, 1])
        rstd = sb("rstd", [P, 1])
        shift = sb("shift", [P, 1])
        tok = {n: sem("tok_" + n) for n in (
            "placed", "turned", "turned_kept", "keys", "keys_kept", "values", "values_kept", "scores",
            "maxed", "exped", "inverted", "probs_turned", "probs_kept", "mixed", "added", "stats1",
            "stats2", "stats3", "stats_summed", "var_ready", "logged", "rooted", "shifted", "scaled",
            "weighted", "normed", "fed", "gelued", "fed_added")}

        def at(i, s, per=1, n=1):
            return (W * i + s) * per + n

        def nth(i, s, which):
            return W * (2 * i + which) + s + 1

        block = ctx.enter_context(nc.Block())

        def norm_stats_pe(pe, i, s, which):
            pe.wait_ge(tok["stats3"], nth(i, s, which))
            nc.tensor.matmul(g.ps[4 * s + 2][:, 0:2], g.mean_all[:, :], stat[s][:, :], start=True, stop=True
                             ).then_inc(tok["stats_summed"], 1)

        @block.tensor
        def _(pe):
            pe.wait_ge(g.consts_set, 2)
            with pe.Fori(0, STEPS) as i:
                for s in range(W):
                    pe.wait_ge(tok["placed"], at(i, s))
                    for c in range(2):
                        for t in range(TPS):
                            last = nc.tensor.transpose(
                                g.ps[4 * s][0:HALF, c * SEQ + t * P:c * SEQ + (t + 1) * P],
                                y[s][:, t, c * HALF:(c + 1) * HALF], g.ident[:, :])
                    last.then_inc(tok["turned"], 1)
                for s in range(W):
                    pe.wait_ge(tok["turned_kept"], nth(i, s, 0))
                    for a in range(2):
                        for c in range(2):
                            k = HALF + c
                            last = nc.tensor.matmul(
                                g.ps[4 * s + 1][0:AUG, a * SEQ:(a + 1) * SEQ],
                                g.qk_fold[0:k, c, a * HALF:a * HALF + AUG], g.xt[s][0:k, c, :],
                                start=(c == 0), stop=(c == 1))
                    last.then_inc(tok["keys"], 1)
                for s in range(W):
                    for t in range(TPS):
                        for c in range(2):
                            k = HALF + c
                            last = nc.tensor.matmul(
                                g.ps[4 * s + 2][:, t * DIM:(t + 1) * DIM], g.xt[s][0:k, c, t * P:(t + 1) * P],
                                g.vo_fold[0:k, c, :], start=(c == 0), stop=(c == 1))
                    last.then_inc(tok["values"], 1)
                for s in range(W):
                    pe.wait_ge(tok["keys_kept"], at(i, s))
                    for t in range(TPS):
                        for c in range(2):
                            k = HALF + c
                            last = nc.tensor.matmul(
                                g.ps[4 * s + 3][:, t * SEQ:(t + 1) * SEQ], g.xt[s][0:k, c, t * P:(t + 1) * P],
                                key_t[s][0:k, c, :], start=(c == 0), stop=(c == 1))
                    last.then_inc(tok["scores"], 1)
                for s in range(W):
                    pe.wait_ge(tok["exped"], at(i, s, 2, 2))
                    for m in range(TPS):
                        for t in range(TPS):
                            last = nc.tensor.transpose(
                                g.ps[4 * s][:, m * SEQ + t * P:m * SEQ + (t + 1) * P],
                                prob[s][:, t, m * P:(m + 1) * P], g.ident[:, :])
                    last.then_inc(tok["probs_turned"], 1)
                for s in range(W):
                    pe.wait_ge(tok["probs_kept"], at(i, s))
                    pe.wait_ge(tok["values_kept"], at(i, s))
                    for t in range(TPS):
                        for m in range(TPS):
                            last = nc.tensor.matmul(
                                g.ps[4 * s + 1][:, t * DIM:(t + 1) * DIM], prob_t[s][:, m, t * P:(t + 1) * P],
                                value[s][:, m, :], start=(m == 0), stop=(m == TPS - 1))
                    last.then_inc(tok["mixed"], 1)
                for s in range(W):
                    norm_stats_pe(pe, i, s, 0)
                for s in range(W):
                    pe.wait_ge(tok["normed"], nth(i, s, 0))
                    for c in range(2):
                        for t in range(TPS):
                            last = nc.tensor.transpose(
                                g.ps[4 * s + 3][0:HALF, c * SEQ + t * P:c * SEQ + (t + 1) * P],
                                y[s][:, t, c * HALF:(c + 1) * HALF], g.ident[:, :])
                    last.then_inc(tok["turned"], 1)
                for s in range(W):
                    pe.wait_ge(tok["turned_kept"], nth(i, s, 1))
                    for t in range(TPS):
                        for c in range(2):
                            k = HALF + c
                            last = nc.tensor.matmul(
                                g.ps[4 * s][:, t * DIM:(t + 1) * DIM], g.xt[s][0:k, c, t * P:(t + 1) * P],
                                g.mlp_fold[0:k, c, :], start=(c == 0), stop=(c == 1))
                    last.then_inc(tok["fed"], 1)
                for s in range(W):
                    norm_stats_pe(pe, i, s, 1)

        @block.scalar
        def _(act):
            act.wait_ge(g.consts_set, 2)

            def turned_copy(i, s, which, bank):
                act.wait_ge(tok["turned"], nth(i, s, which))
                nc.scalar.copy(g.xt[s][0:HALF, :, :], g.ps[bank][0:HALF, :].rearrange("p (c n) -> p c n", c=2)
                               ).then_inc(tok["turned_kept"], 1)

            def root(i, s, which):
                n = nth(i, s, which)
                act.wait_ge(tok["var_ready"], n)
                nc.scalar.activation(log_var[s][:, :], neg_var[s][:, :], ACT.Ln, bias=g.eps5[:, :], scale=-1.0
                                     ).then_inc(tok["logged"], 1)
                act.wait_ge(tok["logged"], n)
                nc.scalar.activation(rstd[s][:, :], log_var[s][:, :], ACT.Exp, scale=-0.5
                                     ).then_inc(tok["rooted"], 1)

            with act.Fori(0, STEPS) as i:
                nc.scalar.preload_act_table_set(EXP_LN)
                for s in range(W):
                    turned_copy(i, s, 0, 4 * s)
                for s in range(W):
                    act.wait_ge(tok["values"], at(i, s))
                    nc.scalar.copy(value[s][:, :, :],
                                   g.ps[4 * s + 2][:, 0:TPS * DIM].rearrange("p (t n) -> p t n", t=TPS)
                                   ).then_inc(tok["values_kept"], 1)
                for s in range(W):
                    act.wait_ge(tok["maxed"], at(i, s))
                    for t in range(TPS):
                        nc.scalar.activation(prob[s][:, t, :], g.ps[4 * s + 3][:, t * SEQ:(t + 1) * SEQ], ACT.Exp,
                                             bias=neg_max[s][:, t:t + 1], accum_out=row_sum[s][:, t:t + 1]
                                             ).then_inc(tok["exped"], 1)
                for s in range(W):
                    root(i, s, 0)
                for s in range(W):
                    turned_copy(i, s, 1, 4 * s + 3)
                for s in range(W):
                    act.wait_ge(tok["fed"], at(i, s))
                    nc.scalar.activation(f_out[s][:, :, :],
                                         g.ps[4 * s][:, 0:TPS * DIM].rearrange("p (t n) -> p t n", t=TPS),
                                         ACT.Gelu).then_inc(tok["gelued"], 1)
                nc.scalar.preload_act_table_set(EXP_LN)
                for s in range(W):
                    root(i, s, 1)

        @block.vector
        def _(dve):
            dve.wait_ge(g.gathered, 16 * TILES)
            dve.wait_ge(g.operands_loaded, 16 * N_OPERANDS)

            def stats(i, s, which, added):
                n = nth(i, s, which)
                dve.wait_ge(tok["added"], added)
                for t in range(TPS):
                    nc.vector.bn_stats(bn[s][:, t, :], y[s][:, t, :]).then_inc(tok["stats1"], 1)
                dve.wait_ge(tok["stats1"], 2 * n)
                nc.vector.nop(nofuse=True)
                nc.vector.bn_aggr(stat[s][:, :], bn[s][:, :, :]).then_inc(tok["stats2"], 1)
                dve.wait_ge(tok["stats2"], n)
                nc.vector.scalar_tensor_tensor(out=stat[s][:, 1:2], in0=stat[s][:, 0:1], scalar=stat[s][:, 0:1],
                                               in1=stat[s][:, 1:2], op0=ALU.mult, op1=ALU.add
                                               ).then_inc(tok["stats3"], 1)

            def variance(i, s, which):
                n = nth(i, s, which)
                dve.wait_ge(tok["stats_summed"], n)
                nc.vector.tensor_copy(stat[s][:, :], g.ps[4 * s + 2][:, 0:2]).then_inc(tok["shifted"], 1)
                dve.wait_ge(tok["shifted"], 2 * n - 1)
                nc.vector.scalar_tensor_tensor(out=neg_var[s][:, :], in0=stat[s][:, 0:1], scalar=stat[s][:, 0:1],
                                               in1=stat[s][:, 1:2], op0=ALU.mult, op1=ALU.subtract
                                               ).then_inc(tok["var_ready"], 1)
                dve.wait_ge(tok["rooted"], n)
                nc.vector.scalar_tensor_tensor(out=shift[s][:, :], in0=stat[s][:, 0:1], scalar=-1.0,
                                               in1=rstd[s][:, :], op0=ALU.mult, op1=ALU.mult
                                               ).then_inc(tok["shifted"], 1)
                dve.wait_ge(tok["shifted"], 2 * n)
                nc.vector.tensor_scalar(y[s][:, :, :], y[s][:, :, :], rstd[s][:, :], shift[s][:, :],
                                        ALU.mult, ALU.add).then_inc(tok["scaled"], 1)

            def weigh(i, s, which, weight, bias, out):
                n = nth(i, s, which)
                dve.wait_ge(tok["scaled"], n)
                nc.vector.tensor_tensor(y[s][:, :, :], y[s][:, :, :], weight, ALU.mult
                                        ).then_inc(tok["weighted"], 1)
                dve.wait_ge(tok["weighted"], n)
                nc.vector.tensor_tensor(out, y[s][:, :, :], bias, ALU.add).then_inc(tok["normed"], 1)

            with dve.Fori(0, STEPS) as i:
                dve.wait_ge(tok["normed"], 2 * W * i)
                for s in range(W):
                    nc.vector.tensor_tensor(y[s][:, :, :], g.h[:, ds(TPS * (W * i + s), TPS), :], g.t["pos"],
                                            ALU.add).then_inc(tok["placed"], 1)
                for s in range(W):
                    dve.wait_ge(tok["keys"], at(i, s))
                    nc.vector.tensor_copy(key_t[s][:, :, :],
                                          g.ps[4 * s + 1][0:AUG, :].rearrange("p (c n) -> p c n", c=2)
                                          ).then_inc(tok["keys_kept"], 1)
                for s in range(W):
                    dve.wait_ge(tok["scores"], at(i, s))
                    nc.vector.tensor_reduce(neg_max[s][:, :],
                                            g.ps[4 * s + 3][:, :].rearrange("p (t n) -> p t n", t=TPS),
                                            AX.X, ALU.max, negate=True).then_inc(tok["maxed"], 1)
                for s in range(W):
                    dve.wait_ge(tok["probs_turned"], at(i, s))
                    nc.vector.tensor_copy(prob_t[s][:, :, :],
                                          g.ps[4 * s][:, :].rearrange("p (m n) -> p m n", m=TPS)
                                          ).then_inc(tok["probs_kept"], 1)
                    nc.vector.reciprocal(inv_sum[s][:, :], row_sum[s][:, :]).then_inc(tok["inverted"], 1)
                for s in range(W):
                    dve.wait_ge(tok["mixed"], at(i, s))
                    dve.wait_ge(tok["inverted"], at(i, s))
                    for t in range(TPS):
                        nc.vector.scalar_tensor_tensor(
                            out=y[s][:, t, :], in0=g.ps[4 * s + 1][:, t * DIM:(t + 1) * DIM],
                            scalar=inv_sum[s][:, t:t + 1], in1=y[s][:, t, :], op0=ALU.mult, op1=ALU.add
                            ).then_inc(tok["added"], 1)
                for s in range(W):
                    stats(i, s, 0, at(i, s, 2, 2))
                for s in range(W):
                    variance(i, s, 0)
                for s in range(W):
                    weigh(i, s, 0, g.t["ln_w1"], g.t["ln_b1"], y[s][:, :, :])
                for s in range(W):
                    dve.wait_ge(tok["gelued"], at(i, s))
                    nc.vector.tensor_tensor(y[s][:, :, :], y[s][:, :, :], f_out[s][:, :, :], ALU.add
                                            ).then_inc(tok["fed_added"], 1)
                for s in range(W):
                    dve.wait_ge(tok["fed_added"], at(i, s))
                    stats(i, s, 1, at(i, s, 2, 2))
                for s in range(W):
                    variance(i, s, 1)
                for s in range(W):
                    weigh(i, s, 1, g.t["ln_w2"], g.t["ln_b2"], g.h[:, ds(TPS * (W * i + s), TPS), :])


def attention(nc, g):
    QUADS, QH = 3, 4
    PARTS = 6
    KS = PARTS * HDIM
    KM = KS + 2 * QH
    QK = 2 * TPS * HEADS
    SUM = HDIM
    with ExitStack() as ctx:
        sb = lambda name, shape, dt=F32: ctx.enter_context(nc.sbuf_tensor(name, shape, dt))
        sem = lambda name: g.stage_semaphore(ctx, nc.semaphore("att_" + name))
        q_t = [sb(f"q_t{s}", [KM, HEADS, SEQ], BF16) for s in range(2)]
        k_t = [sb(f"k_t{s}", [KM, HEADS, SEQ], BF16) for s in range(2)]
        val = [sb(f"val{s}", [P, TPS, HEADS, 32]) for s in range(2)]
        bn = sb("att_bn", [P, TPS, 6])
        mv = sb("att_mv", [P, TPS, 2])
        log_v = sb("att_log", [P, TPS])
        rstd = sb("att_rstd", [P, TPS])
        x = sb("att_x", [P, TPS, DIM])
        sq = sb("att_sq", [P, TPS, 2 * DIM])
        ss = sb("att_ss", [P, QK])
        log_s = sb("att_log_s", [P, QK])
        rms = sb("att_rms", [P, QK])
        weight = sb("att_weight", [P, HDIM])
        qk = sb("att_qk", [P, QK, HDIM])
        rem = sb("att_rem", [P, QK, HDIM])
        rem2 = sb("att_rem2", [P, QK, HDIM])
        stack = sb("att_stack", [P, QK, PARTS, HDIM], BF16)
        neg_max = sb("att_max", [P, QH, TPS])
        max_rem = sb("att_max_rem", [P, TPS, QH])
        max_bf = sb("att_max_bf", [P, TPS, 2, QH], BF16)
        ident_b = sb("att_ident", [P, P], BF16)
        prob = [sb(f"att_prob{u}", [P, 2, TPS, SEQ]) for u in range(2)]
        out_t = sb("att_out_t", [P, QUADS, SEQ])
        inv = sb("att_inv", [P, TPS, HEADS])
        mixed = sb("att_mixed", [P, TPS, HEADS, HDIM])
        x_t, mixed_t = g.xt
        preset = sem("preset")
        val_cleared = sem("val_cleared")
        picks_cleared = sem("picks_cleared")
        picks_set = sem("picks_set")
        S = {n: sem(n) for n in (
            "stats", "mean_var", "logged", "rooted", "normed", "x_turned", "x_kept", "qk_made", "v_made",
            "v_kept", "squared", "summed", "rms_logged", "rms_rooted", "scaled", "weighted", "part1",
            "rem1", "part2", "rem2", "part3", "copied", "filled", "fill_kept_v", "fill_kept_s",
            "max_scored", "maxed", "max_hi", "max_rem", "max_lo", "max_turned", "max_kept",
            "scored", "exped", "mixed", "out_kept", "out_turned", "inverted", "divided", "mixed_turned",
            "mixed_kept", "projected", "added", "weight_made")}
        block = ctx.enter_context(nc.Block())
        O_BANKS = (4, 5)
        flat = lambda a, b, rows=P: g.psum[0:rows, a:b, :].rearrange("p b n -> p (b n)")

        def schedule(eng, front, body, finish):
            front(0, 0, None)
            body(0, 0, first=True, last=False)
            with eng.Fori(0, (BATCH - 2) // 2) as i:
                body(2 * i + 1, 1, first=False, last=False)
                body(2 * i + 2, 0, first=False, last=False)
            body(BATCH - 1, 1, first=False, last=True)
            finish(BATCH - 1, 1)


        @block.tensor
        def _(pe):
            pe.wait_ge(preset, 5)

            def turn_x(n):
                pe.wait_ge(S["normed"], 2 * n + 2)
                for c in range(2):
                    for t in range(TPS):
                        last = nc.tensor.transpose(
                            g.ps[6][0:HALF, c * SEQ + t * P:c * SEQ + (t + 1) * P],
                            x[:, t, c * HALF:(c + 1) * HALF], g.ident[:, :])
                last.then_inc(S["x_turned"], 1)

            def make_qk(n):
                pe.wait_ge(S["x_kept"], n + 1)
                for t in range(TPS):
                    for c in range(2):
                        k = HALF + c
                        last = nc.tensor.matmul(g.ps[7 - t][:, 0:2 * DIM], x_t[0:k, c, t * P:(t + 1) * P],
                                                g.t["qkv_t"][0:k, c, 0:2 * DIM], start=(c == 0), stop=(c == 1))
                    last.then_inc(S["qk_made"], 1)

            def make_v(n):
                pe.wait_ge(S["scaled"], 2 * n + 2)
                for t in range(TPS):
                    for c in range(2):
                        k = HALF + c
                        last = nc.tensor.matmul(g.ps[7][:, t * DIM:(t + 1) * DIM],
                                                x_t[0:k, c, t * P:(t + 1) * P],
                                                g.t["qkv_t"][0:k, c, 2 * DIM:3 * DIM],
                                                start=(c == 0), stop=(c == 1))
                last.then_inc(S["v_made"], 1)

            def fill(n, f):
                if f == 0:
                    pe.wait_ge(S["copied"], n + 1)
                    pe.wait_ge(S["v_kept"], n + 1)
                if f == 1:
                    pe.wait_ge(S["v_kept"], n + 1)
                if f >= 2:
                    if f % 2 == 0:
                        pe.wait_ge(S["fill_kept_v"], 3 * n + f // 2)
                    else:
                        pe.wait_ge(S["fill_kept_s"], 3 * n + f // 2)
                bank = g.ps[6 + f % 2].bitcast(BF16)
                which, quad = f // QUADS, f % QUADS
                for h in range(QH):
                    for t in range(TPS):
                        row = (t * 2 + which) * HEADS + quad * QH + h
                        last = nc.tensor.transpose(
                            bank[0:KS, h * SEQ + t * P:h * SEQ + (t + 1) * P],
                            stack[:, row, :, :].rearrange("p a b -> p (a b)"), ident_b[:, :])
                last.then_inc(S["filled"], 1)

            def front(n, s, slot):
                if slot in (None, (0, 2)):
                    turn_x(n)
                if slot in (None, (1, 0)):
                    make_qk(n)
                if slot in (None, (2, 0)):
                    make_v(n)
                if slot in (None, (2, 1)):
                    for f in range(3):
                        fill(n, f)
                if slot in (None, (2, 2)):
                    for f in range(3, 6):
                        fill(n, f)

            def max_scores(n, s, q, u):
                count = QUADS * n + q
                if u == 0:
                    if q == 0:
                        pe.wait_ge(S["fill_kept_v"], 3 * n + 3)
                        pe.wait_ge(S["fill_kept_s"], 3 * n + 3)
                    pe.wait_ge(S["max_kept"], count)
                else:
                    pe.wait_ge(S["maxed"], 2 * count + 1)
                for hh in range(2):
                    h = QH * q + 2 * u + hh
                    for t in range(TPS):
                        last = nc.tensor.matmul(g.ps[hh][:, t * SEQ:(t + 1) * SEQ],
                                                q_t[s][0:KS, h, t * P:(t + 1) * P], k_t[s][0:KS, h, :],
                                                start=True, stop=True)
                last.then_inc(S["max_scored"], 1)

            def turn_max(n, q):
                count = QUADS * n + q
                pe.wait_ge(S["max_lo"], count + 1)
                for t in range(TPS):
                    last = nc.tensor.transpose(g.ps[0].bitcast(BF16)[KS:KM, t * P:(t + 1) * P],
                                               max_bf[:, t, :, :].rearrange("p a b -> p (a b)"), ident_b[:, :])
                last.then_inc(S["max_turned"], 1)

            def scores(n, s, q, u):
                count = 2 * (QUADS * n + q) + u
                if u == 0:
                    pe.wait_ge(S["max_kept"], QUADS * n + q + 1)
                pe.wait_ge(S["exped"], count)
                for hh in range(2):
                    h = QH * q + 2 * u + hh
                    for m in range(TPS):
                        last = nc.tensor.matmul(g.ps[2 + hh][:, m * SEQ:(m + 1) * SEQ],
                                                k_t[s][:, h, m * P:(m + 1) * P], q_t[s][:, h, :],
                                                start=True, stop=True)
                last.then_inc(S["scored"], 1)

            def mix(n, s, q):
                pe.wait_ge(S["exped"], 2 * (QUADS * n + q) + 2)
                if q == 0:
                    pe.wait_ge(S["mixed_kept"], n)
                    pe.wait_ge(S["added"], n)
                bank = g.ps[O_BANKS[q // 2]]
                for m in range(TPS):
                    for j in range(QH):
                        last = nc.tensor.matmul(
                            bank[32 * j:32 * j + 32, (q % 2) * SEQ:(q % 2 + 1) * SEQ],
                            val[s][:, m, QH * q + j, :], prob[j // 2][:, j % 2, m, :],
                            start=(m == 0), stop=(m == TPS - 1))
                last.then_inc(S["mixed"], 1)

            def turn_out(n):
                pe.wait_ge(S["out_kept"], n + 1)
                for t in range(TPS):
                    for q in range(QUADS):
                        last = nc.tensor.transpose(g.ps[O_BANKS[t]][:, q * P:(q + 1) * P],
                                                   out_t[:, q, t * P:(t + 1) * P], g.ident[:, :])
                last.then_inc(S["out_turned"], 1)

            def turn_mixed(n):
                pe.wait_ge(S["divided"], n + 1)
                flat_mixed = mixed[:, :, :, :].rearrange("p t h d -> p t (h d)")
                for c in range(2):
                    for t in range(TPS):
                        last = nc.tensor.transpose(
                            g.ps[4][0:HALF, c * SEQ + t * P:c * SEQ + (t + 1) * P],
                            flat_mixed[:, t, c * HALF:(c + 1) * HALF], g.ident[:, :])
                last.then_inc(S["mixed_turned"], 1)

            def project(n):
                pe.wait_ge(S["mixed_kept"], n + 1)
                for t in range(TPS):
                    for c in range(2):
                        k = HALF + c
                        last = nc.tensor.matmul(g.ps[5][:, t * DIM:(t + 1) * DIM],
                                                mixed_t[0:k, c, t * P:(t + 1) * P],
                                                g.t["proj_t"][0:k, c, :], start=(c == 0), stop=(c == 1))
                last.then_inc(S["projected"], 1)

            def body(n, s, first, last):
                for q in range(QUADS):
                    pn, ps_, pq = (n, s, q - 1) if q else (n - 1, 1 - s, QUADS - 1)
                    prev = q or not first
                    max_scores(n, s, q, 0)
                    if prev:
                        scores(pn, ps_, pq, 0)
                    if q == 1 and not first:
                        turn_out(n - 1)
                    if not last:
                        front(n + 1, 1 - s, (q, 0))
                    max_scores(n, s, q, 1)
                    if prev:
                        scores(pn, ps_, pq, 1)
                    if q == 1 and not first:
                        turn_mixed(n - 1)
                    if not last:
                        front(n + 1, 1 - s, (q, 1))
                    turn_max(n, q)
                    if q == 1 and not first:
                        project(n - 1)
                    if prev:
                        mix(pn, ps_, pq)
                    if not last:
                        front(n + 1, 1 - s, (q, 2))

            def finish(n, s):
                for u in range(2):
                    scores(n, s, QUADS - 1, u)
                mix(n, s, QUADS - 1)
                turn_out(n)
                turn_mixed(n)
                project(n)

            schedule(pe, front, body, finish)


        @block.scalar
        def _(act):
            nc.scalar.preload_act_table_set(EXP_LN)
            act.wait_ge(g.consts_set, 2)

            def root_var(n):
                act.wait_ge(S["mean_var"], 2 * n + 2)
                nc.scalar.activation(log_v[:, :], mv[:, :, 1], ACT.Ln, bias=g.eps5[:, :]).then_inc(S["logged"], 1)
                act.wait_ge(S["logged"], n + 1)
                nc.scalar.activation(rstd[:, :], log_v[:, :], ACT.Exp, scale=-0.5).then_inc(S["rooted"], 1)

            def keep_x(n):
                act.wait_ge(S["x_turned"], n + 1)
                nc.scalar.copy(x_t[0:HALF, :, :], g.ps[6][0:HALF, :].rearrange("p (c n) -> p c n", c=2)
                               ).then_inc(S["x_kept"], 1)

            def square(n):
                for t in range(TPS):
                    act.wait_ge(S["qk_made"], 2 * n + t + 1)
                    nc.scalar.activation(sq[:, t, :], g.ps[7 - t][:, 0:2 * DIM], ACT.Square
                                         ).then_inc(S["squared"], 1)

            def root_rms(n):
                act.wait_ge(S["summed"], n + 1)
                nc.scalar.activation(log_s[:, :], ss[:, :], ACT.Ln, scale=1.0 / HDIM, bias=g.rms_eps[:, :]
                                     ).then_inc(S["rms_logged"], 1)
                act.wait_ge(S["rms_logged"], n + 1)
                nc.scalar.activation(rms[:, :], log_s[:, :], ACT.Exp, scale=-0.5).then_inc(S["rms_rooted"], 1)

            def keep_v(n, s):
                act.wait_ge(S["v_made"], n + 1)
                nc.scalar.copy(val[s][:, :, :, 0:HDIM].rearrange("p t h d -> p (t h) d"),
                               g.ps[7][:, 0:TPS * DIM].rearrange("p (g d) -> p g d", d=HDIM)
                               ).then_inc(S["v_kept"], 1)

            def keep_fill(n, s, f):
                act.wait_ge(S["filled"], 6 * n + f + 1)
                dst = (q_t if f < QUADS else k_t)[s]
                nc.scalar.copy(dst[0:KS, (f % QUADS) * QH:(f % QUADS + 1) * QH, :],
                               g.ps[6 + f % 2].bitcast(BF16)[0:KS, :].rearrange("p (h n) -> p h n", h=QH)
                               ).then_inc(S["fill_kept_s"], 1)

            def front(n, s, slot):
                if slot in (None, (0, 0)):
                    root_var(n)
                if slot in (None, (0, 2)):
                    keep_x(n)
                if slot in (None, (1, 0)):
                    square(n)
                if slot in (None, (1, 1)):
                    root_rms(n)
                if slot in (None, (2, 0)):
                    keep_v(n, s)
                if slot in (None, (2, 1)):
                    keep_fill(n, s, 1)
                if slot in (None, (2, 2)):
                    keep_fill(n, s, 3)
                    keep_fill(n, s, 5)

            def expo(n, q, u):
                count = 2 * (QUADS * n + q) + u
                act.wait_ge(S["scored"], count + 1)
                act.wait_ge(S["mixed"], QUADS * n + q)
                nc.scalar.activation(prob[u][:, :, :, :].rearrange("p a b n -> p (a b n)"), flat(2, 4), ACT.Exp
                                     ).then_inc(S["exped"], 1)

            def keep_out(n):
                act.wait_ge(S["mixed"], QUADS * n + QUADS)
                nc.scalar.copy(out_t[:, :, :].rearrange("p q n -> p (q n)"), flat(4, 6)[:, 0:QUADS * SEQ]
                               ).then_inc(S["out_kept"], 1)

            def keep_mixed(n):
                act.wait_ge(S["mixed_turned"], n + 1)
                nc.scalar.copy(mixed_t[0:HALF, :, :], g.ps[4][0:HALF, :].rearrange("p (c n) -> p c n", c=2)
                               ).then_inc(S["mixed_kept"], 1)

            def body(n, s, first, last):
                for q in range(QUADS):
                    pn, pq = (n, q - 1) if q else (n - 1, QUADS - 1)
                    prev = q or not first
                    if q == 1 and not first:
                        keep_out(n - 1)
                    if prev:
                        expo(pn, pq, 0)
                    if not last:
                        front(n + 1, 1 - s, (q, 0))
                    if prev:
                        expo(pn, pq, 1)
                    if q == 1 and not first:
                        keep_mixed(n - 1)
                    if not last:
                        front(n + 1, 1 - s, (q, 1))
                        front(n + 1, 1 - s, (q, 2))

            def finish(n, s):
                for u in range(2):
                    expo(n, QUADS - 1, u)
                keep_out(n)
                keep_mixed(n)

            schedule(act, front, body, finish)


        @block.vector
        def _(dve):
            nc.vector.tensor_copy(ident_b[:, :], g.ident[:, :]).then_inc(preset, 1)
            for s in range(2):
                nc.vector.memset(val[s][:, :, :, HDIM:], 0.0).then_inc(val_cleared, 1)
            dve.wait_ge(val_cleared, 2)
            for s in range(2):
                nc.vector.memset(val[s][:, :, :, SUM:SUM + 1], 1.0).then_inc(preset, 1)

            def norm_stats(n):
                dve.wait_ge(S["rooted"], n)
                for t in range(TPS):
                    nc.vector.nop(nofuse=True)
                    nc.vector.bn_stats(bn[:, t, :], g.h[:, ds(TPS * n + t, 1), :].rearrange("p a n -> p (a n)")
                                       ).then_inc(S["stats"], 1)
                dve.wait_ge(S["stats"], 2 * n + 2)
                nc.vector.nop(nofuse=True)
                for t in range(TPS):
                    nc.vector.bn_aggr(mv[:, t, :], bn[:, t, :]).then_inc(S["mean_var"], 1)

            def norm(n):
                dve.wait_ge(S["rooted"], n + 1)
                dve.wait_ge(S["x_turned"], n)
                for t in range(TPS):
                    nc.vector.tensor_scalar(x[:, t, :], g.h[:, ds(TPS * n + t, 1), :].rearrange("p a n -> p (a n)"),
                                            mv[:, t, 0:1], rstd[:, t:t + 1], ALU.subtract, ALU.mult
                                            ).then_inc(S["normed"], 1)

            def sum_squares(n):
                dve.wait_ge(S["squared"], 2 * n + 2)
                nc.vector.tensor_reduce(ss[:, :], sq[:, :, :].rearrange("p t (g d) -> p (t g) d", d=HDIM),
                                        AX.X, ALU.add).then_inc(S["summed"], 1)

            def scale(n):
                dve.wait_ge(S["rms_rooted"], n + 1)
                dve.wait_ge(S["rem2"], n)
                for t in range(TPS):
                    r = rms[:, t * 24:(t + 1) * 24]
                    nc.vector.tensor_tensor(qk[:, t * 24:(t + 1) * 24, :],
                                            g.ps[7 - t][:, 0:2 * DIM].rearrange("p (g d) -> p g d", d=HDIM),
                                            r.unsqueeze(2).broadcast_to((P, 24, HDIM)), ALU.mult
                                            ).then_inc(S["scaled"], 1)

            def split(n):
                dve.wait_ge(S["weighted"], 2 * n + 2)
                dve.wait_ge(S["filled"], 6 * n)
                nc.vector.tensor_copy(stack[:, :, 0, :], qk[:, :, :]).then_inc(S["part1"], 1)
                dve.wait_ge(S["part1"], n + 1)
                nc.vector.tensor_tensor(rem[:, :, :], qk[:, :, :], stack[:, :, 0, :], ALU.subtract
                                        ).then_inc(S["rem1"], 1)
                dve.wait_ge(S["rem1"], n + 1)
                nc.vector.tensor_copy(stack[:, :, 1, :], rem[:, :, :]).then_inc(S["part2"], 1)
                dve.wait_ge(S["part2"], n + 1)
                nc.vector.tensor_tensor(rem2[:, :, :], rem[:, :, :], stack[:, :, 1, :], ALU.subtract
                                        ).then_inc(S["rem2"], 1)
                dve.wait_ge(S["rem2"], n + 1)
                for k, slot in ((0, 5), (1, 4)):
                    for t in range(TPS):
                        g0 = (2 * t + k) * HEADS
                        nc.vector.tensor_copy(stack[:, g0:g0 + HEADS, slot, :], rem2[:, g0:g0 + HEADS, :]
                                              ).then_inc(S["part3"], 1)

            def keep_fill(n, s, f):
                dve.wait_ge(S["filled"], 6 * n + f + 1)
                dst = (q_t if f < QUADS else k_t)[s]
                nc.vector.tensor_copy(dst[0:KS, (f % QUADS) * QH:(f % QUADS + 1) * QH, :],
                                      g.ps[6 + f % 2].bitcast(BF16)[0:KS, :].rearrange("p (h n) -> p h n", h=QH)
                                      ).then_inc(S["fill_kept_v"], 1)

            def front(n, s, slot):
                if slot in (None, (0, 0)):
                    norm_stats(n)
                if slot in (None, (0, 1)):
                    norm(n)
                if slot in (None, (1, 0)):
                    sum_squares(n)
                if slot in (None, (1, 1)):
                    scale(n)
                if slot in (None, (1, 2)):
                    split(n)
                if slot in (None, (2, 1)):
                    keep_fill(n, s, 0)
                    keep_fill(n, s, 2)
                if slot in (None, (2, 2)):
                    keep_fill(n, s, 4)

            def row_max(n, q, u):
                count = QUADS * n + q
                dve.wait_ge(S["max_scored"], 2 * count + u + 1)
                if u == 0:
                    dve.wait_ge(S["max_hi"], count)
                    dve.wait_ge(S["max_rem"], count)
                nc.vector.tensor_reduce(neg_max[:, 2 * u:2 * u + 2, :].rearrange("p a b -> p (a b)"),
                                        flat(0, 2).rearrange("p (g n) -> p g n", n=SEQ), AX.X, ALU.max,
                                        negate=True).then_inc(S["maxed"], 1)

            def split_max(n, q):
                count = QUADS * n + q
                by_tile = neg_max[:, :, :].rearrange("p h t -> p t h")
                dve.wait_ge(S["maxed"], 2 * count + 2)
                dve.wait_ge(S["max_turned"], count)
                nc.vector.tensor_copy(max_bf[:, :, 0, :], by_tile).then_inc(S["max_hi"], 1)
                dve.wait_ge(S["max_hi"], count + 1)
                dve.wait_ge(S["max_lo"], count)
                nc.vector.tensor_tensor(max_rem[:, :, :], by_tile, max_bf[:, :, 0, :], ALU.subtract
                                        ).then_inc(S["max_rem"], 1)
                dve.wait_ge(S["max_rem"], count + 1)
                nc.vector.tensor_copy(max_bf[:, :, 1, :], max_rem[:, :, :]).then_inc(S["max_lo"], 1)

            def keep_max(n, s, q):
                count = QUADS * n + q
                dve.wait_ge(S["max_turned"], count + 1)
                nc.vector.tensor_copy(q_t[s][KS:KM, QH * q:QH * (q + 1), :],
                                      g.ps[0].bitcast(BF16)[KS:KM, 0:SEQ].unsqueeze(1).broadcast_to((2 * QH, QH, SEQ))
                                      ).then_inc(S["max_kept"], 1)

            def divide(n):
                by_head = g.psum[:, 4:6, 0:QUADS * P].rearrange("p t (h c) -> p t h c", c=32)
                dve.wait_ge(S["out_turned"], n + 1)
                dve.wait_ge(S["divided"], n)
                nc.vector.reciprocal(inv[:, :, :], by_head[:, :, :, SUM]).then_inc(S["inverted"], 1)
                dve.wait_ge(S["inverted"], n + 1)
                dve.wait_ge(S["mixed_turned"], n)
                nc.vector.tensor_tensor(mixed[:, :, :, :], by_head[:, :, :, 0:HDIM],
                                        inv[:, :, :].unsqueeze(3).broadcast_to((P, TPS, HEADS, HDIM)), ALU.mult
                                        ).then_inc(S["divided"], 1)

            def add(n):
                dve.wait_ge(S["projected"], n + 1)
                state = g.h[:, ds(TPS * n, TPS), :]
                nc.vector.tensor_tensor(state, state,
                                        g.ps[5][:, 0:TPS * DIM].rearrange("p (t d) -> p t d", t=TPS), ALU.add
                                        ).then_inc(S["added"], 1)

            def body(n, s, first, last):
                for q in range(QUADS):
                    row_max(n, q, 0)
                    if q == 1 and not first:
                        divide(n - 1)
                    if not last:
                        front(n + 1, 1 - s, (q, 0))
                    row_max(n, q, 1)
                    split_max(n, q)
                    if not last:
                        front(n + 1, 1 - s, (q, 1))
                    keep_max(n, s, q)
                    if q == 1 and not first:
                        add(n - 1)
                    if not last:
                        front(n + 1, 1 - s, (q, 2))

            def finish(n, s):
                divide(n)
                add(n)

            schedule(dve, front, body, finish)


        @block.gpsimd
        def _(pool):
            nc.gpsimd.tensor_tensor(weight[:, :], g.t["qk_weights"][:, 0, :], g.t["qk_weights"][:, 1, :], ALU.mult
                                    ).then_inc(S["weight_made"], 1)
            pool.wait_ge(S["weight_made"], 1)
            nc.gpsimd.tensor_scalar(weight[:, :], weight[:, :], float(HDIM) ** -0.5, None, ALU.mult
                                    ).then_inc(S["weight_made"], 1)
            pool.wait_ge(S["weight_made"], 2)
            for s in range(2):
                nc.gpsimd.memset(k_t[s][KS:KM, :, :], 0.0).then_inc(picks_cleared, 1)
            pool.wait_ge(picks_cleared, 2)
            for r in range(2):
                for s in range(2):
                    rows = k_t[s][KS:KM, :, :].rearrange("p (q h) n -> p q h n", h=QH)
                    nc.gpsimd.affine_select(out=rows, in_=rows, compare_op=ALU.not_equal, fill=1.0,
                                            base=-QH * r, pattern=[[0, QUADS], [-1, QH], [0, SEQ]],
                                            channel_multiplier=1).then_inc(preset if r else picks_set, 1)
                if r == 0:
                    pool.wait_ge(picks_set, 2)

            def weigh(n):
                for t in range(TPS):
                    pool.wait_ge(S["scaled"], 2 * n + t + 1)
                    q_part = qk[:, 2 * t * HEADS:(2 * t + 1) * HEADS, :]
                    nc.gpsimd.tensor_tensor(q_part, q_part,
                                            weight[:, :].unsqueeze(1).broadcast_to((P, HEADS, HDIM)), ALU.mult
                                            ).then_inc(S["weighted"], 1)

            def repeat(n):
                pool.wait_ge(S["part3"], 4 * n + 4)
                pool.wait_ge(S["filled"], 6 * n)
                nc.gpsimd.nop(nofuse=True)
                for k, to, of in ((0, 2, 0), (0, 3, 1), (0, 4, 0), (1, 2, 1), (1, 3, 0), (1, 5, 0)):
                    for t in range(TPS):
                        g0 = (2 * t + k) * HEADS
                        last = nc.gpsimd.tensor_copy(stack[:, g0:g0 + HEADS, to, :],
                                                     stack[:, g0:g0 + HEADS, of, :])
                last.then_inc(S["copied"], 1)

            def front(n, s, slot):
                if slot is None:
                    weigh(n)
                    repeat(n)

            def body(n, s, first, last):
                if not last:
                    front(n + 1, 1 - s, None)

            schedule(pool, front, body, lambda n, s: None)


def first_slots(nc, g):
    with ExitStack() as ctx:
        def sb(name, shape, dt=F32):
            return [ctx.enter_context(nc.sbuf_tensor(f"fs_{name}{s}", shape, dt)) for s in range(W)]

        sem = lambda name: g.stage_semaphore(ctx, nc.semaphore("fs_" + name))
        bn = sb("bn", [P, TPS, 6])
        mv = sb("mv", [P, TPS, 2])
        log_v = sb("log_v", [P, TPS])
        factor = sb("factor", [P, TPS])
        x = sb("x", [P, TPS, DIM])
        neg_slot = sb("neg_slot", [P, GPS])
        neg_tok = sb("neg_tok", [P, TPS])
        disp_t = sb("disp_t", [P, SEQ])
        disp_sum = sb("disp_sum", [P, GPS])
        comb = sb("comb", [P, TPS, P])
        comb_sum = sb("comb_sum", [P, TPS])
        comb_inv = sb("comb_inv", [P, TPS])
        disp = sb("disp", [P, TPS, P])
        square = sb("square", [P, DIM])
        slot_ss = sb("slot_ss", [P, GPS])
        eps_part = sb("eps_part", [P, GPS])
        slot_var = sb("slot_var", [P, GPS])
        slot_log = sb("slot_log", [P, GPS])
        slot_fac = sb("slot_fac", [P, GPS])
        yn = sb("yn", [P, GPS, DIM])
        S = {n: sem(n) for n in (
            "stats", "mean_var", "logged", "rooted", "centred", "weighted", "turned", "kept", "logits",
            "slot_maxed", "tok_maxed", "disp_exped", "comb_exped", "inverted", "combined", "disp_turned",
            "comb_turned", "disp_kept", "comb_kept", "slots_made", "squared", "eps_made", "var_made",
            "slot_logged", "slot_rooted", "slots_normed", "stored", "means_made", "means_kept")}
        at = lambda i, s, per=1: (W * i + s + 1) * per
        block = ctx.enter_context(nc.Block())

        @block.tensor
        def _(pe):
            with pe.Fori(0, STEPS) as i:
                for s in range(W):
                    pe.wait_ge(S["weighted"], at(i, s))
                    for c in range(2):
                        for t in range(TPS):
                            last = nc.tensor.transpose(
                                g.ps[4 * s][0:HALF, c * SEQ + t * P:c * SEQ + (t + 1) * P],
                                x[s][:, t, c * HALF:(c + 1) * HALF], g.ident[:, :])
                    last.then_inc(S["turned"], 1)
                for s in range(W):
                    pe.wait_ge(S["kept"], at(i, s))
                    bank = g.ps[4 * s + 1]
                    for c in range(2):
                        nc.tensor.matmul(bank[:, 0:SEQ], g.phi_t[:, c, :], g.xt[s][0:HALF, c, :],
                                         start=(c == 0), stop=(c == 1))
                    for t in range(TPS):
                        for c in range(2):
                            last = nc.tensor.matmul(bank[:, SEQ + t * P:SEQ + (t + 1) * P],
                                                    g.xt[s][0:HALF, c, t * P:(t + 1) * P], g.phi_t[:, c, :],
                                                    start=(c == 0), stop=(c == 1))
                    last.then_inc(S["logits"], 1)
                for s in range(W):
                    pe.wait_ge(S["disp_exped"], at(i, s, GPS))
                    for t in range(TPS):
                        last = nc.tensor.transpose(g.ps[4 * s + 2][:, t * P:(t + 1) * P],
                                                   disp_t[s][:, t * P:(t + 1) * P], g.ident[:, :])
                    last.then_inc(S["disp_turned"], 1)
                for s in range(W):
                    pe.wait_ge(S["combined"], at(i, s))
                    for t in range(TPS):
                        last = nc.tensor.transpose(g.ps[4 * s + 3][:, t * P:(t + 1) * P], comb[s][:, t, :],
                                                   g.ident[:, :])
                    last.then_inc(S["comb_turned"], 1)
                for s in range(W):
                    pe.wait_ge(S["disp_kept"], at(i, s))
                    pe.wait_ge(S["comb_kept"], at(i, s))
                    for gr in range(GPS):
                        rows, t = slice(GROUP * (gr % 2), GROUP * (gr % 2 + 1)), gr // 2
                        last = nc.tensor.matmul(g.ps[4 * s + 3 * (gr % 2)][:, t * DIM:(t + 1) * DIM],
                                                disp[s][rows, t, :], x[s][rows, t, :], start=True, stop=True)
                    last.then_inc(S["slots_made"], 1)
                for s in range(W):
                    pe.wait_ge(S["slots_normed"], at(i, s, GPS))
                    for c in range(2):
                        for gr in range(GPS):
                            m0 = (c * GPS + gr) * (P // MEAN)
                            last = nc.tensor.matmul(g.ps[4 * s + 1][0:HALF, m0:m0 + P // MEAN],
                                                    yn[s][:, gr, c * HALF:(c + 1) * HALF], g.average[:, :],
                                                    start=True, stop=True)
                    last.then_inc(S["means_made"], 1)

        @block.scalar
        def _(act):
            nc.scalar.preload_act_table_set(EXP_LN)
            act.wait_ge(g.consts_set, 2)
            with act.Fori(0, STEPS) as i:
                for s in range(W):
                    act.wait_ge(S["mean_var"], at(i, s, TPS))
                    nc.scalar.activation(log_v[s][:, :], mv[s][:, :, 1], ACT.Ln, scale=1.0 + 1e-6 / DIM,
                                         bias=g.eps_norms[:, :]).then_inc(S["logged"], 1)
                    act.wait_ge(S["logged"], at(i, s))
                    nc.scalar.activation(factor[s][:, :], log_v[s][:, :], ACT.Exp, scale=-0.5
                                         ).then_inc(S["rooted"], 1)
                for s in range(W):
                    act.wait_ge(S["turned"], at(i, s))
                    nc.scalar.copy(g.xt[s][0:HALF, :, :], g.ps[4 * s][0:HALF, :].rearrange("p (c n) -> p c n", c=2)
                                   ).then_inc(S["kept"], 1)
                for s in range(W):
                    act.wait_ge(S["slot_maxed"], at(i, s))
                    act.wait_ge(S["tok_maxed"], at(i, s))
                    for gr in range(GPS):
                        cols = slice(gr * GROUP, (gr + 1) * GROUP)
                        nc.scalar.activation(disp_t[s][:, cols], g.ps[4 * s + 1][:, cols], ACT.Exp,
                                             bias=neg_slot[s][:, gr:gr + 1], accum_out=disp_sum[s][:, gr:gr + 1]
                                             ).then_inc(S["disp_exped"], 1)
                    for t in range(TPS):
                        nc.scalar.activation(comb[s][:, t, :], g.ps[4 * s + 1][:, SEQ + t * P:SEQ + (t + 1) * P],
                                             ACT.Exp, bias=neg_tok[s][:, t:t + 1],
                                             accum_out=comb_sum[s][:, t:t + 1]).then_inc(S["comb_exped"], 1)
                for s in range(W):
                    act.wait_ge(S["disp_turned"], at(i, s))
                    nc.scalar.copy(disp[s][:, :, :], g.ps[4 * s + 2][:, 0:SEQ].rearrange("p (t n) -> p t n", t=TPS)
                                   ).then_inc(S["disp_kept"], 1)
                for s in range(W):
                    act.wait_ge(S["slots_made"], at(i, s))
                    for gr in range(GPS):
                        t = gr // 2
                        act.wait_ge(S["squared"], at(i, s, GPS) - GPS + gr)
                        nc.scalar.activation(square[s][:, :],
                                             g.ps[4 * s + 3 * (gr % 2)][:, t * DIM:(t + 1) * DIM], ACT.Square,
                                             accum_out=slot_ss[s][:, gr:gr + 1]).then_inc(S["squared"], 1)
                for s in range(W):
                    act.wait_ge(S["var_made"], at(i, s))
                    nc.scalar.activation(slot_log[s][:, :], slot_var[s][:, :], ACT.Ln, scale=1.0 / DIM
                                         ).then_inc(S["slot_logged"], 1)
                    act.wait_ge(S["slot_logged"], at(i, s))
                    nc.scalar.activation(slot_fac[s][:, :], slot_log[s][:, :], ACT.Exp, scale=-0.5
                                         ).then_inc(S["slot_rooted"], 1)

        @block.vector
        def _(dve):
            with dve.Fori(0, STEPS) as i:
                for s in range(W):
                    dve.wait_ge(S["rooted"], W * i)
                    for t in range(TPS):
                        nc.vector.nop(nofuse=True)
                        row = g.h[:, ds(TPS * (W * i + s) + t, 1), :].rearrange("p a n -> p (a n)")
                        nc.vector.bn_stats(bn[s][:, t, :], row).then_inc(S["stats"], 1)
                    dve.wait_ge(S["stats"], at(i, s, TPS))
                    nc.vector.nop(nofuse=True)
                    for t in range(TPS):
                        nc.vector.bn_aggr(mv[s][:, t, :], bn[s][:, t, :]).then_inc(S["mean_var"], 1)
                for s in range(W):
                    dve.wait_ge(S["rooted"], at(i, s))
                    dve.wait_ge(S["slots_made"], W * i)
                    for t in range(TPS):
                        row = g.h[:, ds(TPS * (W * i + s) + t, 1), :].rearrange("p a n -> p (a n)")
                        nc.vector.tensor_scalar(x[s][:, t, :], row, mv[s][:, t, 0:1], factor[s][:, t:t + 1],
                                                ALU.subtract, ALU.mult).then_inc(S["centred"], 1)
                for s in range(W):
                    dve.wait_ge(S["centred"], at(i, s, TPS))
                    nc.vector.tensor_tensor(x[s][:, :, :], x[s][:, :, :],
                                            g.t["gamma_in"].unsqueeze(1).broadcast_to((P, TPS, DIM)), ALU.mult
                                            ).then_inc(S["weighted"], 1)
                for s in range(W):
                    dve.wait_ge(S["logits"], at(i, s))
                    nc.vector.tensor_reduce(neg_slot[s][:, :],
                                            g.ps[4 * s + 1][:, 0:SEQ].rearrange("p (g n) -> p g n", g=GPS),
                                            AX.X, ALU.max, negate=True).then_inc(S["slot_maxed"], 1)
                    nc.vector.tensor_reduce(neg_tok[s][:, :],
                                            g.ps[4 * s + 1][:, SEQ:].rearrange("p (t n) -> p t n", t=TPS),
                                            AX.X, ALU.max, negate=True).then_inc(S["tok_maxed"], 1)
                for s in range(W):
                    dve.wait_ge(S["comb_exped"], at(i, s, TPS))
                    nc.vector.reciprocal(comb_inv[s][:, :], comb_sum[s][:, :]).then_inc(S["inverted"], 1)
                    dve.wait_ge(S["inverted"], at(i, s))
                    nc.vector.tensor_tensor(comb[s][:, :, :], comb[s][:, :, :],
                                            comb_inv[s][:, :].unsqueeze(2).broadcast_to((P, TPS, P)), ALU.mult
                                            ).then_inc(S["combined"], 1)
                for s in range(W):
                    dve.wait_ge(S["comb_turned"], at(i, s))
                    nc.vector.nop(nofuse=True)
                    nc.vector.tensor_copy(g.comb_t[:, ds((W * i + s) * SEQ, SEQ)], g.ps[4 * s + 3][:, 0:SEQ]
                                          ).then_inc(S["comb_kept"], 1)
                for s in range(W):
                    nc.vector.scalar_tensor_tensor(out=eps_part[s][:, :], in0=disp_sum[s][:, :], scalar=1e-6,
                                                   in1=disp_sum[s][:, :], op0=ALU.mult, op1=ALU.mult
                                                   ).then_inc(S["eps_made"], 1)
                    dve.wait_ge(S["eps_made"], at(i, s))
                    dve.wait_ge(S["squared"], at(i, s, GPS))
                    nc.vector.tensor_tensor(slot_var[s][:, :], slot_ss[s][:, :], eps_part[s][:, :], ALU.add
                                            ).then_inc(S["var_made"], 1)
                for s in range(W):
                    dve.wait_ge(S["slot_rooted"], at(i, s))
                    dve.wait_ge(S["stored"], W * i + s)
                    for gr in range(GPS):
                        t = gr // 2
                        nc.vector.scalar_tensor_tensor(
                            out=yn[s][:, gr, :], in0=g.ps[4 * s + 3 * (gr % 2)][:, t * DIM:(t + 1) * DIM],
                            scalar=slot_fac[s][:, gr:gr + 1], in1=g.t["gamma2"], op0=ALU.mult, op1=ALU.mult
                            ).then_inc(S["slots_normed"], 1)
                for s in range(W):
                    dve.wait_ge(S["means_made"], at(i, s))
                    nc.vector.nop(nofuse=True)
                    for c in range(2):
                        nc.vector.tensor_copy(
                            g.means_t[:, c, :, ds((W * i + s) * GPS, GPS), :],
                            g.ps[4 * s + 1][0:HALF, c * P:(c + 1) * P].rearrange("p (g k m) -> p k g m", g=GPS, k=E1)
                            ).then_inc(S["means_kept"], 1)

        @block.gpsimd
        def _(pool):
            with pool.Fori(0, STEPS) as i:
                for s in range(W):
                    pool.wait_ge(S["slots_normed"], at(i, s, GPS))
                    nc.gpsimd.nop(nofuse=True)
                    nc.gpsimd.tensor_copy(g.yn[:, ds((W * i + s) * GPS, GPS), :], yn[s][:, :, :]
                                          ).then_inc(S["stored"], 1)


def second_slots(nc, g):
    with ExitStack() as ctx:
        def sb(name, shape, dt=F32):
            return [ctx.enter_context(nc.sbuf_tensor(f"ss_{name}{s}", shape, dt)) for s in range(W)]

        sem = lambda name: g.stage_semaphore(ctx, nc.semaphore("ss_" + name))
        weight = sb("weight", [HALF, 2, E2 * DIM])
        mean_k = sb("mean_k", [HALF, 2, P])
        square = sb("square", [P, DIM])
        ss = sb("ss", [P, E2])
        log_s = sb("log_s", [P, E2])
        factor = sb("factor", [P, E2])
        se = sb("se", [P, E2, DIM])
        loaded = [sem(f"loaded{s}") for s in range(W)]
        S = {n: sem(n) for n in ("means", "made", "squared", "logged", "rooted", "normed", "turned",
                                 "kept_v", "kept_s")}
        at = lambda i, s, per=1: (W * i + s + 1) * per
        block = ctx.enter_context(nc.Block())

        @block.sync
        def _(sp):
            with sp.Fori(0, E1 // W) as i:
                for s in range(W):
                    sp.wait_ge(S["made"], W * i)
                    sp.dma_start(weight[s][:, :, :],
                                 g.d["w_slot2"][ds(W * i + s, 1)].rearrange("a p c n -> (a p) c n")
                                 ).then_inc(loaded[s], 16)

        @block.gpsimd
        def _(pool):
            with pool.Fori(0, E1 // W) as i:
                for s in range(W):
                    pool.wait_ge(S["made"], W * i)
                    nc.gpsimd.nop(nofuse=True)
                    nc.gpsimd.tensor_copy(mean_k[s][:, :, :].unsqueeze(2),
                                          g.means_t[:, :, ds(W * i + s, 1), :, :].rearrange(
                                              "p c k g m -> p c k (g m)")).then_inc(S["means"], 1)

        @block.tensor
        def _(pe):
            with pe.Fori(0, E1 // W) as i:
                for s in range(W):
                    pe.wait_ge(loaded[s], 16 * (i + 1))
                    pe.wait_ge(S["means"], at(i, s))
                    for b in range(2):
                        for c in range(2):
                            last = nc.tensor.matmul(g.ps[4 * s + b][:, 0:2 * DIM], mean_k[s][:, c, :],
                                                    weight[s][:, c, b * 2 * DIM:(b + 1) * 2 * DIM],
                                                    start=(c == 0), stop=(c == 1))
                    last.then_inc(S["made"], 1)
                for s in range(W):
                    pe.wait_ge(S["normed"], at(i, s))
                    pe.wait_ge(S["kept_v"], W * i)
                    pe.wait_ge(S["kept_s"], W * i)
                    for c in range(2):
                        for e in range(E2):
                            last = nc.tensor.transpose(g.ps[4 * s + 2 + c][0:HALF, e * P:(e + 1) * P],
                                                       se[s][:, e, c * HALF:(c + 1) * HALF], g.ident[:, :])
                    last.then_inc(S["turned"], 1)

        def dest(i, s, c):
            return g.se2_t[:, c, :, ds((W * i + s) * E2 * MEAN, E2 * MEAN)].rearrange(
                "p g (e m) -> p e g m", e=E2)

        def source(s, c):
            return g.ps[4 * s + 2 + c][0:HALF, :].rearrange("p (e g m) -> p e g m", e=E2, m=MEAN)

        @block.scalar
        def _(act):
            nc.scalar.preload_act_table_set(EXP_LN)
            with act.Fori(0, E1 // W) as i:
                for s in range(W):
                    act.wait_ge(S["made"], at(i, s))
                    for e in range(E2):
                        act.wait_ge(S["squared"], at(i, s, E2) - E2 + e)
                        nc.scalar.activation(square[s][:, :],
                                             g.ps[4 * s + e // 2][:, (e % 2) * DIM:(e % 2 + 1) * DIM], ACT.Square,
                                             accum_out=ss[s][:, e:e + 1]).then_inc(S["squared"], 1)
                for s in range(W):
                    act.wait_ge(S["squared"], at(i, s, E2))
                    nc.scalar.activation(log_s[s][:, :], ss[s][:, :], ACT.Ln, scale=1.0 / DIM,
                                         bias=g.eps_dim[:, :]).then_inc(S["logged"], 1)
                    act.wait_ge(S["logged"], at(i, s))
                    nc.scalar.activation(factor[s][:, :], log_s[s][:, :], ACT.Exp, scale=-0.5
                                         ).then_inc(S["rooted"], 1)
                for s in range(W):
                    act.wait_ge(S["turned"], at(i, s))
                    nc.scalar.nop(nofuse=True)
                    nc.scalar.copy(dest(i, s, 1), source(s, 1)).then_inc(S["kept_s"], 1)

        @block.vector
        def _(dve):
            with dve.Fori(0, E1 // W) as i:
                for s in range(W):
                    dve.wait_ge(S["rooted"], at(i, s))
                    nc.vector.tensor_tensor(
                        se[s][:, :, :].rearrange("p (b e) d -> p b e d", b=2),
                        g.psum[:, 4 * s:4 * s + 2, 0:2 * DIM].rearrange("p b (e d) -> p b e d", e=2),
                        factor[s][:, :].rearrange("p (b e) -> p b e", b=2).unsqueeze(3).broadcast_to(
                            (P, 2, 2, DIM)), ALU.mult).then_inc(S["normed"], 1)
                for s in range(W):
                    dve.wait_ge(S["turned"], at(i, s))
                    nc.vector.nop(nofuse=True)
                    nc.vector.tensor_copy(dest(i, s, 0), source(s, 0)).then_inc(S["kept_v"], 1)


def second_dispatch(nc, g):
    with ExitStack() as ctx:
        def sb(name, shape, dt=F32):
            return [ctx.enter_context(nc.sbuf_tensor(f"sd_{name}{s}", shape, dt)) for s in range(W)]

        sem = lambda name: g.stage_semaphore(ctx, nc.semaphore("sd_" + name))
        yn = sb("yn", [P, GPS, DIM])
        yn_t = sb("yn_t", [HALF, 2, GPS * P])
        logits = sb("logits", [P, GPS, P])
        neg_row = sb("neg_row", [P, GPS])
        neg_col = sb("neg_col", [P, GPS])
        sum_row = sb("sum_row", [P, GPS])
        sum_col = sb("sum_col", [P, GPS])
        inv_row = sb("inv_row", [P, GPS])
        inv_col = sb("inv_col", [P, GPS])
        comb = sb("comb", [P, GPS, P])
        disp_t = sb("disp_t", [P, GPS, P])
        disp = sb("disp", [P, GPS, P])
        S = {n: sem(n) for n in (
            "fetched", "yn_turned", "yn_kept_s", "yn_kept_v", "logits_made", "masked", "row_maxed",
            "row_exped", "row_inverted", "combined", "logits_turned", "col_maxed", "col_exped",
            "col_inverted", "dispatched", "disp_turned", "disp_kept", "weights_made", "weights_kept",
            "inputs_made", "inputs_kept_s", "inputs_kept_v")}
        at = lambda i, s, per=1: (W * i + s + 1) * per
        block = ctx.enter_context(nc.Block())
        cols4 = lambda bank: bank.rearrange("p (g n) -> p g n", g=GPS)

        @block.gpsimd
        def _(pool):
            with pool.Fori(0, STEPS) as i:
                for s in range(W):
                    pool.wait_ge(S["inputs_made"], W * i)
                    nc.gpsimd.nop(nofuse=True)
                    nc.gpsimd.tensor_copy(yn[s][:, :, :], g.yn[:, ds((W * i + s) * GPS, GPS), :]
                                          ).then_inc(S["fetched"], 1)

        @block.tensor
        def _(pe):
            with pe.Fori(0, STEPS) as i:
                for s in range(W):
                    pe.wait_ge(S["fetched"], at(i, s))
                    pe.wait_ge(S["disp_kept"], W * i)
                    pe.wait_ge(S["weights_kept"], W * i)
                    for c in range(2):
                        for gr in range(GPS):
                            last = nc.tensor.transpose(g.ps[4 * s + c][0:HALF, gr * P:(gr + 1) * P],
                                                       yn[s][:, gr, c * HALF:(c + 1) * HALF], g.ident[:, :])
                    last.then_inc(S["yn_turned"], 1)
                for s in range(W):
                    pe.wait_ge(S["yn_kept_s"], at(i, s))
                    pe.wait_ge(S["yn_kept_v"], at(i, s))
                    pe.wait_ge(S["inputs_kept_v"], W * i)
                    pe.wait_ge(S["inputs_kept_s"], W * i)
                    for gr in range(GPS):
                        for c in range(2):
                            last = nc.tensor.matmul(
                                g.ps[4 * s + 2][:, gr * P:(gr + 1) * P], yn_t[s][:, c, gr * P:(gr + 1) * P],
                                g.se2_t[:, c, ds((W * i + s) * GPS + gr, 1), :].rearrange("p a n -> p (a n)"),
                                start=(c == 0), stop=(c == 1))
                    last.then_inc(S["logits_made"], 1)
                for s in range(W):
                    pe.wait_ge(S["masked"], at(i, s))
                    for gr in range(GPS):
                        last = nc.tensor.transpose(g.ps[4 * s + 3][:, gr * P:(gr + 1) * P], logits[s][:, gr, :],
                                                   g.ident[:, :])
                    last.then_inc(S["logits_turned"], 1)
                for s in range(W):
                    pe.wait_ge(S["combined"], at(i, s))
                    for gr in range(GPS):
                        last = nc.tensor.matmul(
                            g.ps[4 * s + 1][:, gr * GROUP:(gr + 1) * GROUP], comb[s][:, gr, :],
                            g.comb_t[:, ds((W * i + s) * SEQ + gr * GROUP, GROUP)], start=True, stop=True)
                    last.then_inc(S["weights_made"], 1)
                for s in range(W):
                    pe.wait_ge(S["dispatched"], at(i, s))
                    for gr in range(GPS):
                        last = nc.tensor.transpose(g.ps[4 * s][:, gr * P:(gr + 1) * P], disp_t[s][:, gr, :],
                                                   g.ident[:, :])
                    last.then_inc(S["disp_turned"], 1)
                for s in range(W):
                    pe.wait_ge(S["disp_kept"], at(i, s))
                    for c in range(2):
                        for gr in range(GPS):
                            last = nc.tensor.matmul(g.ps[4 * s + 2 + c][0:HALF, gr * P:(gr + 1) * P],
                                                    yn[s][:, gr, c * HALF:(c + 1) * HALF], disp[s][:, gr, :],
                                                    start=True, stop=True)
                    last.then_inc(S["inputs_made"], 1)

        def inputs(i, s, c):
            out = g.slots2_t[0:HALF, c, :, ds((W * i + s) * GPS * MEAN, GPS * MEAN)].rearrange(
                "p k (g m) -> p k g m", m=MEAN)
            return out, g.ps[4 * s + 2 + c][0:HALF, :].rearrange("p (g k m) -> p k g m", g=GPS, m=MEAN)

        @block.scalar
        def _(act):
            nc.scalar.preload_act_table_set(EXP_LN)
            with act.Fori(0, STEPS) as i:
                for s in range(W):
                    act.wait_ge(S["yn_turned"], at(i, s))
                    nc.scalar.copy(yn_t[s][:, 0, :], g.ps[4 * s][0:HALF, :]).then_inc(S["yn_kept_s"], 1)
                for s in range(W):
                    act.wait_ge(S["row_maxed"], at(i, s))
                    for gr in range(GPS):
                        nc.scalar.activation(comb[s][:, gr, :], logits[s][:, gr, :], ACT.Exp,
                                             bias=neg_row[s][:, gr:gr + 1], accum_out=sum_row[s][:, gr:gr + 1]
                                             ).then_inc(S["row_exped"], 1)
                for s in range(W):
                    act.wait_ge(S["col_maxed"], at(i, s))
                    for gr in range(GPS):
                        nc.scalar.activation(disp_t[s][:, gr, :], g.ps[4 * s + 3][:, gr * P:(gr + 1) * P], ACT.Exp,
                                             bias=neg_col[s][:, gr:gr + 1], accum_out=sum_col[s][:, gr:gr + 1]
                                             ).then_inc(S["col_exped"], 1)
                for s in range(W):
                    act.wait_ge(S["disp_turned"], at(i, s))
                    nc.scalar.copy(disp[s][:, :, :], cols4(g.ps[4 * s])).then_inc(S["disp_kept"], 1)
                for s in range(W):
                    act.wait_ge(S["inputs_made"], at(i, s))
                    nc.scalar.nop(nofuse=True)
                    out, of = inputs(i, s, 1)
                    nc.scalar.copy(out, of).then_inc(S["inputs_kept_s"], 1)

        @block.vector
        def _(dve):
            nc.vector.memset(g.slots2_t[HALF:AUG, 1, :, :], 1.0).then_inc(g.input_ones, 1)
            with dve.Fori(0, STEPS) as i:
                for s in range(W):
                    dve.wait_ge(S["yn_turned"], at(i, s))
                    nc.vector.tensor_copy(yn_t[s][:, 1, :], g.ps[4 * s + 1][0:HALF, :]
                                          ).then_inc(S["yn_kept_v"], 1)
                for s in range(W):
                    dve.wait_ge(S["logits_made"], at(i, s))
                    nc.vector.tensor_tensor(logits[s][:, :, :], cols4(g.ps[4 * s + 2]),
                                            g.block_mask[:, :].unsqueeze(1).broadcast_to((P, GPS, P)), ALU.add
                                            ).then_inc(S["masked"], 1)
                    dve.wait_ge(S["masked"], at(i, s))
                    nc.vector.tensor_reduce(neg_row[s][:, :], logits[s][:, :, :], AX.X, ALU.max, negate=True
                                            ).then_inc(S["row_maxed"], 1)
                for s in range(W):
                    dve.wait_ge(S["logits_turned"], at(i, s))
                    nc.vector.tensor_reduce(neg_col[s][:, :], cols4(g.ps[4 * s + 3]), AX.X, ALU.max, negate=True
                                            ).then_inc(S["col_maxed"], 1)
                for s in range(W):
                    dve.wait_ge(S["row_exped"], at(i, s, GPS))
                    nc.vector.reciprocal(inv_row[s][:, :], sum_row[s][:, :]).then_inc(S["row_inverted"], 1)
                    dve.wait_ge(S["row_inverted"], at(i, s))
                    nc.vector.tensor_tensor(comb[s][:, :, :], comb[s][:, :, :],
                                            inv_row[s][:, :].unsqueeze(2).broadcast_to((P, GPS, P)), ALU.mult
                                            ).then_inc(S["combined"], 1)
                for s in range(W):
                    dve.wait_ge(S["col_exped"], at(i, s, GPS))
                    nc.vector.reciprocal(inv_col[s][:, :], sum_col[s][:, :]).then_inc(S["col_inverted"], 1)
                    dve.wait_ge(S["col_inverted"], at(i, s))
                    nc.vector.tensor_tensor(disp_t[s][:, :, :], disp_t[s][:, :, :],
                                            inv_col[s][:, :].unsqueeze(2).broadcast_to((P, GPS, P)), ALU.mult
                                            ).then_inc(S["dispatched"], 1)
                for s in range(W):
                    dve.wait_ge(S["weights_made"], at(i, s))
                    nc.vector.nop(nofuse=True)
                    nc.vector.tensor_copy(g.mix_t[:, ds((W * i + s) * SEQ, SEQ)], g.ps[4 * s + 1][:, 0:SEQ]
                                          ).then_inc(S["weights_kept"], 1)
                for s in range(W):
                    dve.wait_ge(S["inputs_made"], at(i, s))
                    nc.vector.nop(nofuse=True)
                    out, of = inputs(i, s, 0)
                    nc.vector.tensor_copy(out, of).then_inc(S["inputs_kept_v"], 1)


def load_expert(sp, g, k, e):
    sp.dma_start(g.w1[e][:, :, :], g.d["w1"][ds(k, 1), e].rearrange("a p c n -> (a p) c n")
                 ).then_inc(g.w1_loaded[e], 16)
    sp.dma_start(g.w2[e][:, :, :], g.d["w2e"][ds(k, 1), e].rearrange("a p c n -> (a p) c n")
                 ).then_inc(g.w2_loaded[e], 16)


def experts(nc, g):
    HB = HID // P
    with ExitStack() as ctx:
        def sb(name, shape, dt=F32):
            return [ctx.enter_context(nc.sbuf_tensor(f"ex_{name}{u}", shape, dt)) for u in range(2)]

        sem = lambda name: g.stage_semaphore(ctx, nc.semaphore("ex_" + name))
        gelu = sb("gelu", [P, HID])
        act_t = sb("act_t", [P, HID])
        rows = sb("rows", [P, DIM])
        S = {n: sem(n) for n in ("gates", "values", "gelued", "acted", "made", "kept")}
        written = [sem(f"written{e}") for e in range(E2)]
        gathered = sem("gathered")
        block = ctx.enter_context(nc.Block())
        gate_bank, value_bank, out_bank = (lambda e: g.ps[4 * (e % 2)], lambda e: g.ps[4 * (e % 2) + 1],
                                           lambda e: g.ps[4 * (e % 2) + 2])

        @block.sync
        def _(sp):
            for e in range(E2):
                load_expert(sp, g, 0, e)
            with sp.Fori(1, E1) as k:
                for e in range(E2):
                    sp.wait_ge(S["values"], E2 * (k - 1) + e + 1)
                    sp.wait_ge(S["made"], E2 * (k - 1) + e + 1)
                    load_expert(sp, g, k, e)

        @block.tensor
        def _(pe):
            pe.wait_ge(g.input_ones, 1)

            def hidden(k, e):
                n = E2 * k + e
                pe.wait_ge(g.w1_loaded[e], 16 * (k + 1))
                x = lambda c: g.slots2_t[0:HALF + c, c, ds(n, 1), :].rearrange("p a n -> p (a n)")
                for bank, first, done, free in ((gate_bank(e), HID, "gates", "gelued"),
                                                (value_bank(e), 0, "values", "acted")):
                    if e >= 2:
                        pe.wait_ge(S[free], n - 1)
                    else:
                        pe.wait_ge(S[free], E2 * k)
                    for j in range(HB):
                        for c in range(2):
                            last = nc.tensor.matmul(
                                bank[:, j * P:(j + 1) * P],
                                g.w1[e][0:HALF + c, c, first + j * P:first + (j + 1) * P], x(c),
                                start=(c == 0), stop=(c == 1))
                    last.then_inc(S[done], 1)

            def output(k, e):
                n = E2 * k + e
                pe.wait_ge(S["acted"], n + 1)
                pe.wait_ge(g.w2_loaded[e], 16 * (k + 1))
                if e >= 2:
                    pe.wait_ge(S["kept"], n - 1)
                else:
                    pe.wait_ge(S["kept"], E2 * k)
                for j in range(HB):
                    last = nc.tensor.matmul(out_bank(e)[:, 0:DIM], act_t[e % 2][:, j * P:(j + 1) * P],
                                            g.w2[e][:, j, :], start=(j == 0), stop=(j == HB - 1))
                last.then_inc(S["made"], 1)

            with pe.Fori(0, E1) as k:
                hidden(k, 0)
                for e in range(1, E2):
                    hidden(k, e)
                    output(k, e - 1)
                output(k, E2 - 1)

        @block.scalar
        def _(act):
            def gate(k, e):
                n = E2 * k + e
                act.wait_ge(S["gates"], n + 1)
                if e >= 2:
                    act.wait_ge(S["acted"], n - 1)
                else:
                    act.wait_ge(S["acted"], E2 * k)
                nc.scalar.activation(gelu[e % 2][:, :], gate_bank(e)[:, :], ACT.Gelu_apprx_tanh
                                     ).then_inc(S["gelued"], 1)

            def keep(k, e):
                n = E2 * k + e
                act.wait_ge(S["made"], n + 1)
                if e >= 2:
                    act.wait_ge(written[e - 2], 16 * (k + 1))
                else:
                    act.wait_ge(written[e + 2], 16 * k)
                nc.scalar.copy(rows[e % 2][:, :], out_bank(e)[:, 0:DIM]).then_inc(S["kept"], 1)
                act.wait_ge(S["kept"], n + 1)
                act.dma_start(g.scratch[ds(k, 1), e].rearrange("a p n -> (a p) n"), rows[e % 2][:, :]
                              ).then_inc(written[e], 16)

            with act.Fori(0, E1) as k:
                gate(k, 0)
                for e in range(1, E2):
                    gate(k, e)
                    keep(k, e - 1)
                keep(k, E2 - 1)

        @block.vector
        def _(dve):
            with dve.Fori(0, E1) as k:
                for e in range(E2):
                    n = E2 * k + e
                    dve.wait_ge(S["gelued"], n + 1)
                    dve.wait_ge(S["values"], n + 1)
                    if e >= 2:
                        dve.wait_ge(S["made"], n - 1)
                    else:
                        dve.wait_ge(S["made"], E2 * k)
                    nc.vector.tensor_tensor(act_t[e % 2][:, :], value_bank(e)[:, :], gelu[e % 2][:, :], ALU.mult
                                            ).then_inc(S["acted"], 1)

        @block.gpsimd
        def _(pool):
            for k in range(E1):
                for e in range(E2):
                    p0 = (k * E2 + e) * MEAN
                    pool.wait_ge(written[e], 16 * (k + 1))
                    pool.dma_start(g.yn[p0:p0 + MEAN, :, :],
                                   g.scratch[k, e].rearrange("(g m) d -> m g d", m=MEAN)).then_inc(gathered, 16)
            pool.wait_ge(gathered, 16 * E1 * E2)


def combine(nc, g):
    with ExitStack() as ctx:
        def sb(name, shape, dt=F32):
            return [ctx.enter_context(nc.sbuf_tensor(f"co_{name}{s}", shape, dt)) for s in range(W)]

        sem = lambda name: g.stage_semaphore(ctx, nc.semaphore("co_" + name))
        rows = sb("rows", [P, GPS, DIM])
        mix = sb("mix", [P, SEQ])
        final = sb("final", [P, TPS, DIM])
        S = {n: sem(n) for n in ("biased", "fetched", "mixed", "added")}
        stored = [sem(f"stored{s}") for s in range(W)]
        at = lambda i, s, per=1: (W * i + s + 1) * per
        block = ctx.enter_context(nc.Block())

        @block.vector
        def _(dve):
            with dve.Fori(0, STEPS) as i:
                for s in range(W):
                    dve.wait_ge(S["mixed"], W * i)
                    nc.vector.tensor_tensor(rows[s][:, :, :], g.yn[:, ds((W * i + s) * GPS, GPS), :],
                                            g.t["b2"].unsqueeze(1).broadcast_to((P, GPS, DIM)), ALU.add
                                            ).then_inc(S["biased"], 1)
                for s in range(W):
                    dve.wait_ge(stored[s], 16 * i)
                    dve.wait_ge(S["mixed"], at(i, s))
                    nc.vector.tensor_tensor(final[s][:, :, :], g.h[:, ds((W * i + s) * TPS, TPS), :],
                                            g.ps[s][:, 0:TPS * DIM].rearrange("p (t d) -> p t d", t=TPS), ALU.add
                                            ).then_inc(S["added"], 1)

        @block.scalar
        def _(act):
            with act.Fori(0, STEPS) as i:
                for s in range(W):
                    act.wait_ge(S["mixed"], W * i)
                    nc.scalar.nop(nofuse=True)
                    nc.scalar.copy(mix[s][:, :], g.mix_t[:, ds((W * i + s) * SEQ, SEQ)]).then_inc(S["fetched"], 1)

        @block.tensor
        def _(pe):
            with pe.Fori(0, STEPS) as i:
                for s in range(W):
                    pe.wait_ge(S["biased"], at(i, s))
                    pe.wait_ge(S["fetched"], at(i, s))
                    pe.wait_ge(S["added"], W * i)
                    for gr in range(GPS):
                        r0, t = GROUP * (gr % 2), gr // 2
                        last = nc.tensor.matmul(g.ps[s][r0:r0 + GROUP, t * DIM:(t + 1) * DIM],
                                                mix[s][:, gr * GROUP:(gr + 1) * GROUP], rows[s][:, gr, :],
                                                start=True, stop=True)
                    last.then_inc(S["mixed"], 1)

        @block.sync
        def _(sp):
            with sp.Fori(0, STEPS) as i:
                for s in range(W):
                    sp.wait_ge(S["added"], at(i, s))
                    sp.dma_start(g.out[:, ds((W * i + s) * TPS, TPS), :], final[s][:, :, :]
                                 ).then_inc(stored[s], 16)
            for s in range(W):
                sp.wait_ge(stored[s], 16 * STEPS)


def tower(nc, d, out):
    g = Shared()
    g.d, g.out = d, out
    with ExitStack() as ctx:
        sb = lambda name, shape, dt=F32: ctx.enter_context(nc.sbuf_tensor(name, shape, dt))
        sem = lambda name: ctx.enter_context(nc.semaphore(name))
        g.psum = ctx.enter_context(nc.psum_tensor("banks", [P, 8, 512], F32))
        g.ps = [g.psum[:, n, :] for n in range(8)]
        g.h = sb("h", [P, TILES, DIM])
        g.ident = sb("ident", [P, P])
        g.average = sb("average", [P, P // MEAN])
        g.block_mask = sb("block_mask", [P, P])
        g.eps5, g.eps6, g.rms_eps, g.eps_norms, g.eps_dim = (
            sb(name, [P, 1]) for name in ("eps5", "eps6", "rms_eps", "eps_norms", "eps_dim"))
        g.phi_t = sb("phi_t", [HALF, 2, P])
        g.xt = [sb(f"xt{s}", [AUG, 2, SEQ]) for s in range(W)]
        g.w1 = [sb(f"w1_{e}", [AUG, 2, 2 * HID]) for e in range(E2)]
        g.w2 = [sb(f"w2_{e}", [P, HID // P, DIM]) for e in range(E2)]
        g.w1_loaded = [sem(f"w1_loaded{e}") for e in range(E2)]
        g.w2_loaded = [sem(f"w2_loaded{e}") for e in range(E2)]
        g.scratch = nc.dram_tensor("rows_scratch", (E1, E2, P, DIM), F32, kind="Internal").ap()
        g.ids_loaded, g.gathered, g.operands_loaded = sem("ids_loaded"), sem("gathered"), sem("operands_loaded")
        g.ident_made, g.masks_made, g.consts_set = sem("ident_made"), sem("masks_made"), sem("consts_set")
        g.folds_ready, g.ones_set, g.input_ones = sem("folds_ready"), sem("ones_set"), sem("input_ones")

        def operands(scope, names):
            for n in names:
                g.t[n] = scope.enter_context(nc.sbuf_tensor(n + "_sb", list(d[n].shape), F32))[
                    tuple(slice(None) for _ in d[n].shape)]

        operands(ctx, MOE_OPERANDS)
        with ExitStack() as front:
            fsb = lambda name, shape, dt=F32: front.enter_context(nc.sbuf_tensor(name, shape, dt))
            operands(front, FRONT_OPERANDS)
            g.ids = fsb("ids", [P, TILES], U32)
            g.mean_all = fsb("mean_all", [P, P])
            g.qk_fold = fsb("qk_fold", [AUG, 2, DIM + 1])
            g.vo_fold = fsb("vo_fold", [AUG, 2, DIM])
            g.mlp_fold = fsb("mlp_fold", [AUG, 2, DIM])
            fold_weights(nc, g)
            token_mixer(nc, g)
            attention(nc, g)
        clear_spent(nc, g)
        g.yn = sb("yn_all", [P, NGROUPS, DIM])
        g.slots2_t = sb("slots2_t", [AUG, 2, E1 * E2, NGROUPS * MEAN])
        g.mix_t = sb("mix_t", [P, BATCH * SEQ])
        with ExitStack() as moe:
            msb = lambda name, shape, dt=F32: moe.enter_context(nc.sbuf_tensor(name, shape, dt))
            g.comb_t = msb("comb_t", [P, BATCH * SEQ])
            g.means_t = msb("means_t", [HALF, 2, E1, NGROUPS, MEAN])
            g.se2_t = msb("se2_t", [HALF, 2, NGROUPS, P])
            first_slots(nc, g)
            second_slots(nc, g)
            second_dispatch(nc, g)
        experts(nc, g)
        combine(nc, g)


def layouts(inputs):
    f = lambda n: np.asarray(inputs[n])
    cat, c = np.concatenate, np.ascontiguousarray

    def halves(w):
        return c(cat([w[:DIM].reshape(2, HALF, -1), np.stack([w[DIM:], w[DIM:]])], 1).transpose(1, 0, 2))

    def hidden(w, b):
        return c(cat([w, b[None]], 0).T.reshape(HC, P, DIM + 1).transpose(1, 0, 2))

    def hid_rows(w):
        return c(w.reshape(HC, P, DIM).transpose(1, 0, 2))

    def seq_tiles(w):
        return c(w.reshape(TPS, P, DIM).transpose(1, 0, 2))

    d = {
        "ids": c(f("x").reshape(TILES, P).T).view(np.uint32),
        "emb": c(f("L0_tok_emb")),
        "wq_t": hidden(f("L0_tok_Wq"), f("L0_tok_bq")),
        "wk_t": hidden(f("L0_tok_Wk"), f("L0_tok_bk")),
        "wv_t": hidden(f("L0_tok_Wv"), f("L0_tok_bv")),
        "w1_t": hidden(f("L0_tok_W1"), f("L0_tok_b1")),
        "wo": hid_rows(f("L0_tok_Wo")),
        "w2": hid_rows(f("L0_tok_W2")),
        "tail_bias": c(np.stack([f("L0_tok_bo"), f("L0_tok_b2")])[None]),
        "ln_w1": seq_tiles(f("L0_tok_ln1_w")), "ln_b1": seq_tiles(f("L0_tok_ln1_b")),
        "ln_w2": seq_tiles(f("L0_tok_ln2_w")), "ln_b2": seq_tiles(f("L0_tok_ln2_b")),
        "pos": seq_tiles(pos_encoding()),
        "qkv_t": halves(cat([f("L0_attn_qkv_w").T, f("L0_attn_qkv_b")[None]], 0)),
        "proj_t": halves(cat([f("L0_attn_proj_w").T, f("L0_attn_proj_b")[None]], 0)),
        "qk_weights": c(np.broadcast_to(np.stack([f("L0_attn_q_norm_w"), f("L0_attn_k_norm_w")]), (P, 2, HDIM))),
        "gamma_in": c(np.broadcast_to(f("L0_ffn_gamma_in"), (P, DIM))),
        "slots1": c(f("L0_ffn_slots1").reshape(P, DIM)),
        "gamma2": c(np.repeat(f("L0_ffn_gamma2"), S1, 0)),
        "b2": c(np.repeat(f("L0_ffn_b2").reshape(E1 * E2, DIM), MEAN, 0)),
        "w_slot2": c(f("L0_ffn_w_slot2").reshape(E1, 2, HALF, E2 * DIM).transpose(0, 2, 1, 3)),
        "w1": c(cat([f("L0_ffn_w1").reshape(E1, E2, 2, HALF, 2 * HID),
                     np.broadcast_to(f("L0_ffn_b1")[:, :, None, None, :], (E1, E2, 2, 1, 2 * HID))], 3
                    ).transpose(0, 1, 3, 2, 4)),
        "w2e": c(f("L0_ffn_w2").reshape(E1, E2, HID // P, P, DIM).transpose(0, 1, 3, 2, 4)),
    }
    return d


def kernel(**inputs):
    from concourse import bacc
    from concourse.bass_utils import run_bass_kernel_spmd

    nc = bacc.Bacc("TRN2", target_bir_lowering=False, num_devices=1)
    arrays = layouts(inputs)
    d = {n: nc.dram_tensor("in_" + n, a.shape, mybir.dt.from_np(a.dtype), kind="ExternalInput").ap()
         for n, a in arrays.items()}
    out = nc.dram_tensor("out", (P, TILES, DIM), F32, kind="ExternalOutput").ap()
    tower(nc, d, out)
    r = run_bass_kernel_spmd(nc, [{"in_" + n: a for n, a in arrays.items()}], core_ids=[0])
    got = r.results[0]["out"]
    return np.ascontiguousarray(got.transpose(1, 0, 2)).reshape(BATCH, SEQ, DIM)
```

```python
from contextlib import ExitStack

import numpy as np

import concourse.bass as bass
from concourse import mybir

ALU = mybir.AluOpType
ACT = mybir.ActivationFunctionType
AX = mybir.AxisListType
F32 = mybir.dt.float32
BF16 = mybir.dt.bfloat16
U32 = mybir.dt.uint32

P = 128
BATCH, SEQ, DIM = 8, 256, 192
HALF = DIM // 2
AUG = HALF + 1
TILES = BATCH * SEQ // P
TPS = SEQ // P
TOK_HID = 768
HC = TOK_HID // P
HEADS, HDIM = 12, 16
GROUP = 64
GPS = SEQ // GROUP
NGROUPS = BATCH * GPS
E1, S1, E2 = 8, 16, 4
MEAN = 4
HID = 512
SLOTS = E1 * S1
W = 2
WIDE = 4
STEPS = BATCH // W
ROOT = float(DIM) ** 0.5
MASKED = -1.0e30
FRONT_OPERANDS = ("qkv_t", "proj_t", "ln_w1", "ln_b1", "ln_w2", "ln_b2", "pos", "qk_weights")
MOE_OPERANDS = ("gamma_in", "gamma2", "b2")
N_OPERANDS = len(FRONT_OPERANDS) + len(MOE_OPERANDS)
ds = bass.ds
EXP_LN = "natural_log_exp_and_others"


def pos_encoding():
    pos = np.arange(SEQ, dtype=np.float32)[:, None]
    i = np.arange(DIM, dtype=np.float32)[None, :]
    ang = pos / np.power(np.float32(10000.0), i / np.float32(DIM))
    return np.where((np.arange(DIM) % 2 == 0)[None, :], np.sin(ang), np.cos(ang)).astype(np.float32)


class Shared:

    def __init__(self):
        self.t = {}
        self.spent = []

    def stage_semaphore(self, stage, semaphore):
        s = stage.enter_context(semaphore)
        self.spent.append(s)
        return s


def clear_spent(nc, g):
    with nc.Block() as block:
        @block.sync
        def _(sp):
            for s in g.spent:
                sp.sem_clear(s)
    g.spent = []


def fold_weights(nc, g):
    with ExitStack() as ctx:
        sb = lambda name, shape, dt=F32: ctx.enter_context(nc.sbuf_tensor(name, shape, dt))
        sem = lambda name: g.stage_semaphore(ctx, nc.semaphore(name))
        wq_t = sb("wq_t", [P, HC, DIM + 1])
        wk_t = sb("wk_t", [P, HC, DIM + 1])
        wv_t = sb("wv_t", [P, HC, DIM + 1])
        w1_t = sb("w1_t", [P, HC, DIM + 1])
        wo = sb("wo", [P, HC, DIM])
        w2 = sb("w2", [P, HC, DIM])
        tail_bias = sb("tail_bias", [1, 2, DIM])
        last_row = sb("last_row", [1, AUG])
        slots_raw = sb("slots_raw", [P, DIM])
        slots_sq = sb("slots_sq", [P, DIM])
        slots_ss = sb("slots_ss", [P, 1])
        slots_ln = sb("slots_ln", [P, 1])
        slots_rn = sb("slots_rn", [P, 1])
        loaded_qk = sem("loaded_qk")
        loaded_v = sem("loaded_v")
        loaded_1 = sem("loaded_1")
        loaded_bias = sem("loaded_bias")
        loaded_slots = sem("loaded_slots")
        zeroed = sem("zeroed")
        row_set = sem("row_set")
        folded = sem("folded")
        slots_squared = sem("slots_squared")
        slots_logged = sem("slots_logged")
        slots_rooted = sem("slots_rooted")
        slots_normed = sem("slots_normed")
        slots_turned = sem("slots_turned")
        ident_zeroed = sem("ident_zeroed")
        masks_zeroed = sem("masks_zeroed")
        block = ctx.enter_context(nc.Block())

        @block.sync
        def _(sp):
            sp.dma_start(wq_t[:, :, :], g.d["wq_t"]).then_inc(loaded_qk, 16)
            sp.dma_start(wv_t[:, :, :], g.d["wv_t"]).then_inc(loaded_v, 16)
            sp.dma_start(w1_t[:, :, :], g.d["w1_t"]).then_inc(loaded_1, 16)
            sp.dma_start(tail_bias[:, :, :], g.d["tail_bias"]).then_inc(loaded_bias, 16)
            for name in FRONT_OPERANDS + MOE_OPERANDS:
                sp.dma_start(g.t[name], g.d[name]).then_inc(g.operands_loaded, 16)
            sp.wait_ge(g.operands_loaded, 16 * N_OPERANDS)

        @block.gpsimd
        def _(pool):
            pool.dma_start(g.ids[:, :], g.d["ids"]).then_inc(g.ids_loaded, 16)
            pool.wait_ge(g.ids_loaded, 16)
            for t in range(TILES):
                pool.indirect_dma_start(g.h[:, t, :], None, g.d["emb"],
                                        bass.IndirectOffsetOnAxis(ap=g.ids[:, t:t + 1], axis=0)
                                        ).then_inc(g.gathered, 16)
            nc.gpsimd.memset(g.ident[:, :], 0.0).then_inc(ident_zeroed, 1)
            nc.gpsimd.memset(g.average[:, :], 1.0 / MEAN).then_inc(masks_zeroed, 1)
            nc.gpsimd.memset(g.block_mask[:, :], 0.0).then_inc(masks_zeroed, 1)
            pool.wait_ge(ident_zeroed, 1)
            nc.gpsimd.affine_select(out=g.ident[:, :], in_=g.ident[:, :], compare_op=ALU.not_equal, fill=1.0,
                                    base=0, pattern=[[-1, P]], channel_multiplier=1).then_inc(g.ident_made, 1)
            pool.wait_ge(masks_zeroed, 2)
            nc.gpsimd.affine_select(out=g.average[:, :], in_=g.average[:, :], compare_op=ALU.is_ge, fill=0.0,
                                    base=0, pattern=[[-MEAN, P // MEAN]], channel_multiplier=1
                                    ).then_inc(masks_zeroed, 1)
            nc.gpsimd.affine_select(out=g.block_mask[:, :], in_=g.block_mask[:, :], compare_op=ALU.is_ge,
                                    fill=MASKED, base=0, pattern=[[-S1, E1], [0, S1]], channel_multiplier=1
                                    ).then_inc(masks_zeroed, 1)
            pool.wait_ge(masks_zeroed, 4)
            nc.gpsimd.affine_select(out=g.average[:, :], in_=g.average[:, :], compare_op=ALU.is_ge, fill=0.0,
                                    base=MEAN - 1, pattern=[[MEAN, P // MEAN]], channel_multiplier=-1
                                    ).then_inc(g.masks_made, 1)
            nc.gpsimd.affine_select(out=g.block_mask[:, :], in_=g.block_mask[:, :], compare_op=ALU.is_ge,
                                    fill=MASKED, base=S1 - 1, pattern=[[S1, E1], [0, S1]],
                                    channel_multiplier=-1).then_inc(g.masks_made, 1)

        @block.scalar
        def _(act):
            act.dma_start(wk_t[:, :, :], g.d["wk_t"]).then_inc(loaded_qk, 16)
            act.dma_start(wo[:, :, :], g.d["wo"]).then_inc(loaded_v, 16)
            act.dma_start(w2[:, :, :], g.d["w2"]).then_inc(loaded_1, 16)
            act.dma_start(slots_raw[:, :], g.d["slots1"]).then_inc(loaded_slots, 16)
            nc.scalar.preload_act_table_set(EXP_LN)
            act.wait_ge(loaded_slots, 16)
            nc.scalar.activation(slots_sq[:, :], slots_raw[:, :], ACT.Square,
                                 accum_out=slots_ss[:, :]).then_inc(slots_squared, 1)
            act.wait_ge(slots_squared, 1)
            act.wait_ge(g.consts_set, 1)
            nc.scalar.activation(slots_ln[:, :], slots_ss[:, :], ACT.Ln, bias=g.eps6[:, :]
                                 ).then_inc(slots_logged, 1)
            act.wait_ge(slots_logged, 1)
            nc.scalar.activation(slots_rn[:, :], slots_ln[:, :], ACT.Exp, scale=-0.5).then_inc(slots_rooted, 1)

        @block.tensor
        def _(pe):
            pe.wait_ge(loaded_qk, 32)
            for c in range(2):
                for j in range(HC):
                    last = nc.tensor.matmul(g.ps[c][0:AUG, 0:DIM + 1], wk_t[:, j, c * HALF:c * HALF + AUG],
                                            wq_t[:, j, :], start=(j == 0), stop=(j == HC - 1))
                last.then_inc(folded, 1)
            pe.wait_ge(zeroed, 1)
            pe.wait_ge(row_set, 1)
            pe.wait_ge(loaded_bias, 16)
            for n, (lhs, rhs, loaded) in enumerate(((wv_t, wo, loaded_v), (w1_t, w2, loaded_1))):
                pe.wait_ge(loaded, 32)
                for c in range(2):
                    bank = g.ps[2 + 2 * n + c]
                    for j in range(HC):
                        last = nc.tensor.matmul(bank[0:AUG, 0:DIM], lhs[:, j, c * HALF:c * HALF + AUG],
                                                rhs[:, j, :], start=(j == 0), stop=(c == 0 and j == HC - 1))
                    if c == 1:
                        last = nc.tensor.matmul(bank[0:AUG, 0:DIM], last_row[:, :], tail_bias[:, n, :],
                                                start=False, stop=True)
                    last.then_inc(folded, 1)
            pe.wait_ge(slots_normed, 1)
            pe.wait_ge(g.ident_made, 1)
            for c in range(2):
                last = nc.tensor.transpose(g.ps[6][0:HALF, c * P:(c + 1) * P],
                                           slots_raw[:, c * HALF:(c + 1) * HALF], g.ident[:, :])
            last.then_inc(slots_turned, 1)

        @block.vector
        def _(dve):
            nc.vector.memset(g.eps6[:, :], 1e-6)
            nc.vector.memset(g.eps5[:, :], 1e-5)
            nc.vector.memset(g.eps_norms[:, :], 1e-11 / DIM)
            nc.vector.memset(g.eps_dim[:, :], 1e-6 / DIM)
            nc.vector.memset(g.rms_eps[:, :], 1e-6).then_inc(g.consts_set, 1)
            nc.vector.memset(last_row[:, :], 0.0).then_inc(zeroed, 1)
            nc.vector.memset(g.mean_all[:, :], 1.0 / P).then_inc(g.consts_set, 1)
            dve.wait_ge(zeroed, 1)
            nc.vector.memset(last_row[:, HALF:AUG], 1.0).then_inc(row_set, 1)
            for s in range(WIDE):
                nc.vector.memset(g.xt[s][HALF:AUG, :, :], 1.0).then_inc(g.ones_set, 1)
            for n, fold in enumerate((g.qk_fold, g.vo_fold, g.mlp_fold)):
                for c in range(2):
                    dve.wait_ge(folded, 2 * n + c + 1)
                    nc.vector.tensor_copy(fold[:, c, :], g.ps[2 * n + c][0:AUG, 0:fold.shape[2]]
                                          ).then_inc(g.folds_ready, 1)
            dve.wait_ge(slots_rooted, 1)
            nc.vector.tensor_scalar(slots_raw[:, :], slots_raw[:, :], slots_rn[:, :], ROOT, ALU.mult, ALU.mult
                                    ).then_inc(slots_normed, 1)
            dve.wait_ge(slots_turned, 1)
            nc.vector.tensor_copy(g.phi_t[:, :, :], g.ps[6][0:HALF, 0:2 * P].rearrange("p (c n) -> p c n", c=2)
                                  ).then_inc(g.folds_ready, 1)


def token_mixer(nc, g):
    with ExitStack() as ctx:
        def sb(name, shape, dt=F32):
            return [ctx.enter_context(nc.sbuf_tensor(f"{name}{s}", shape, dt)) for s in range(WIDE)]

        sem = lambda name: g.stage_semaphore(ctx, nc.semaphore(name))
        y = sb("y", [P, TPS, DIM])
        key_t = sb("key_t", [AUG, 2, SEQ])
        value = sb("value", [P, TPS, DIM])
        prob = sb("prob", [P, TPS, SEQ])
        prob_t = sb("prob_t", [P, TPS, SEQ])
        neg_max = sb("neg_max", [P, TPS])
        row_sum = sb("row_sum", [P, TPS])
        inv_sum = sb("inv_sum", [P, TPS])
        f_out = sb("f_out", [P, TPS, DIM])
        bn = sb("bn", [P, TPS, 6])
        stat = sb("stat", [P, 2])
        neg_var = sb("neg_var", [P, 1])
        log_var = sb("log_var", [P, 1])
        rstd = sb("rstd", [P, 1])
        shift = sb("shift", [P, 1])
        tok = {n: sem("tok_" + n) for n in (
            "placed", "turned", "turned_kept", "keys", "keys_kept", "values", "values_kept", "scores",
            "maxed", "exped", "inverted", "probs_turned", "probs_kept", "mixed", "added", "stats1",
            "stats2", "stats3", "stats_summed", "var_ready", "logged", "rooted", "shifted", "scaled",
            "weighted", "normed", "fed", "gelued", "fed_added")}

        def at(i, s, per=1, n=1):
            return (WIDE * i + s) * per + n

        def nth(i, s, which):
            return WIDE * (2 * i + which) + s + 1

        block = ctx.enter_context(nc.Block())

        def norm_stats_pe(pe, i, s, which):
            pe.wait_ge(tok["stats3"], nth(i, s, which))
            nc.tensor.matmul(g.ps[2 * s][:, 0:2], g.mean_all[:, :], stat[s][:, :], start=True, stop=True
                             ).then_inc(tok["stats_summed"], 1)

        @block.tensor
        def _(pe):
            pe.wait_ge(g.consts_set, 2)
            with pe.Fori(0, BATCH // WIDE) as i:
                for s in range(WIDE):
                    pe.wait_ge(tok["placed"], at(i, s))
                    for c in range(2):
                        for t in range(TPS):
                            last = nc.tensor.transpose(
                                g.ps[2 * s][0:HALF, c * SEQ + t * P:c * SEQ + (t + 1) * P],
                                y[s][:, t, c * HALF:(c + 1) * HALF], g.ident[:, :])
                    last.then_inc(tok["turned"], 1)
                for s in range(WIDE):
                    pe.wait_ge(tok["turned_kept"], nth(i, s, 0))
                    for a in range(2):
                        for c in range(2):
                            k = HALF + c
                            last = nc.tensor.matmul(
                                g.ps[2 * s + 1][0:AUG, a * SEQ:(a + 1) * SEQ],
                                g.qk_fold[0:k, c, a * HALF:a * HALF + AUG], g.xt[s][0:k, c, :],
                                start=(c == 0), stop=(c == 1))
                    last.then_inc(tok["keys"], 1)
                for s in range(WIDE):
                    for t in range(TPS):
                        for c in range(2):
                            k = HALF + c
                            last = nc.tensor.matmul(
                                g.ps[2 * s][:, t * DIM:(t + 1) * DIM], g.xt[s][0:k, c, t * P:(t + 1) * P],
                                g.vo_fold[0:k, c, :], start=(c == 0), stop=(c == 1))
                    last.then_inc(tok["values"], 1)
                for s in range(WIDE):
                    pe.wait_ge(tok["keys_kept"], at(i, s))
                    for t in range(TPS):
                        for c in range(2):
                            k = HALF + c
                            last = nc.tensor.matmul(
                                g.ps[2 * s + 1][:, t * SEQ:(t + 1) * SEQ], g.xt[s][0:k, c, t * P:(t + 1) * P],
                                key_t[s][0:k, c, :], start=(c == 0), stop=(c == 1))
                    last.then_inc(tok["scores"], 1)
                for s in range(WIDE):
                    pe.wait_ge(tok["exped"], at(i, s, 2, 2))
                    pe.wait_ge(tok["values_kept"], at(i, s))
                    for m in range(TPS):
                        for t in range(TPS):
                            last = nc.tensor.transpose(
                                g.ps[2 * s][:, m * SEQ + t * P:m * SEQ + (t + 1) * P],
                                prob[s][:, t, m * P:(m + 1) * P], g.ident[:, :])
                    last.then_inc(tok["probs_turned"], 1)
                for s in range(WIDE):
                    pe.wait_ge(tok["probs_kept"], at(i, s))
                    for t in range(TPS):
                        for m in range(TPS):
                            last = nc.tensor.matmul(
                                g.ps[2 * s + 1][:, t * DIM:(t + 1) * DIM], prob_t[s][:, m, t * P:(t + 1) * P],
                                value[s][:, m, :], start=(m == 0), stop=(m == TPS - 1))
                    last.then_inc(tok["mixed"], 1)
                for s in range(WIDE):
                    norm_stats_pe(pe, i, s, 0)
                for s in range(WIDE):
                    pe.wait_ge(tok["normed"], nth(i, s, 0))
                    for c in range(2):
                        for t in range(TPS):
                            last = nc.tensor.transpose(
                                g.ps[2 * s + 1][0:HALF, c * SEQ + t * P:c * SEQ + (t + 1) * P],
                                y[s][:, t, c * HALF:(c + 1) * HALF], g.ident[:, :])
                    last.then_inc(tok["turned"], 1)
                for s in range(WIDE):
                    pe.wait_ge(tok["turned_kept"], nth(i, s, 1))
                    for t in range(TPS):
                        for c in range(2):
                            k = HALF + c
                            last = nc.tensor.matmul(
                                g.ps[2 * s][:, t * DIM:(t + 1) * DIM], g.xt[s][0:k, c, t * P:(t + 1) * P],
                                g.mlp_fold[0:k, c, :], start=(c == 0), stop=(c == 1))
                    last.then_inc(tok["fed"], 1)
                for s in range(WIDE):
                    norm_stats_pe(pe, i, s, 1)

        @block.scalar
        def _(act):
            act.wait_ge(g.consts_set, 2)

            def turned_copy(i, s, which, bank):
                act.wait_ge(tok["turned"], nth(i, s, which))
                nc.scalar.copy(g.xt[s][0:HALF, :, :], g.ps[bank][0:HALF, :].rearrange("p (c n) -> p c n", c=2)
                               ).then_inc(tok["turned_kept"], 1)

            def root(i, s, which):
                n = nth(i, s, which)
                act.wait_ge(tok["var_ready"], n)
                nc.scalar.activation(log_var[s][:, :], neg_var[s][:, :], ACT.Ln, bias=g.eps5[:, :], scale=-1.0
                                     ).then_inc(tok["logged"], 1)
                act.wait_ge(tok["logged"], n)
                nc.scalar.activation(rstd[s][:, :], log_var[s][:, :], ACT.Exp, scale=-0.5
                                     ).then_inc(tok["rooted"], 1)

            with act.Fori(0, BATCH // WIDE) as i:
                nc.scalar.preload_act_table_set(EXP_LN)
                for s in range(WIDE):
                    turned_copy(i, s, 0, 2 * s)
                for s in range(WIDE):
                    act.wait_ge(tok["values"], at(i, s))
                    nc.scalar.copy(value[s][:, :, :],
                                   g.ps[2 * s][:, 0:TPS * DIM].rearrange("p (t n) -> p t n", t=TPS)
                                   ).then_inc(tok["values_kept"], 1)
                for s in range(WIDE):
                    act.wait_ge(tok["maxed"], at(i, s))
                    for t in range(TPS):
                        nc.scalar.activation(prob[s][:, t, :], g.ps[2 * s + 1][:, t * SEQ:(t + 1) * SEQ], ACT.Exp,
                                             bias=neg_max[s][:, t:t + 1], accum_out=row_sum[s][:, t:t + 1]
                                             ).then_inc(tok["exped"], 1)
                for s in range(WIDE):
                    root(i, s, 0)
                for s in range(WIDE):
                    turned_copy(i, s, 1, 2 * s + 1)
                for s in range(WIDE):
                    act.wait_ge(tok["fed"], at(i, s))
                    nc.scalar.activation(f_out[s][:, :, :],
                                         g.ps[2 * s][:, 0:TPS * DIM].rearrange("p (t n) -> p t n", t=TPS),
                                         ACT.Gelu).then_inc(tok["gelued"], 1)
                nc.scalar.preload_act_table_set(EXP_LN)
                for s in range(WIDE):
                    root(i, s, 1)

        @block.vector
        def _(dve):
            dve.wait_ge(g.gathered, 16 * TILES)
            dve.wait_ge(g.operands_loaded, 16 * N_OPERANDS)

            def stats(i, s, which, added):
                n = nth(i, s, which)
                dve.wait_ge(tok["added"], added)
                for t in range(TPS):
                    nc.vector.bn_stats(bn[s][:, t, :], y[s][:, t, :]).then_inc(tok["stats1"], 1)
                dve.wait_ge(tok["stats1"], 2 * n)
                nc.vector.nop(nofuse=True)
                nc.vector.bn_aggr(stat[s][:, :], bn[s][:, :, :]).then_inc(tok["stats2"], 1)
                dve.wait_ge(tok["stats2"], n)
                nc.vector.scalar_tensor_tensor(out=stat[s][:, 1:2], in0=stat[s][:, 0:1], scalar=stat[s][:, 0:1],
                                               in1=stat[s][:, 1:2], op0=ALU.mult, op1=ALU.add
                                               ).then_inc(tok["stats3"], 1)

            def variance(i, s, which):
                n = nth(i, s, which)
                dve.wait_ge(tok["stats_summed"], n)
                nc.vector.tensor_copy(stat[s][:, :], g.ps[2 * s][:, 0:2]).then_inc(tok["shifted"], 1)
                dve.wait_ge(tok["shifted"], 2 * n - 1)
                nc.vector.scalar_tensor_tensor(out=neg_var[s][:, :], in0=stat[s][:, 0:1], scalar=stat[s][:, 0:1],
                                               in1=stat[s][:, 1:2], op0=ALU.mult, op1=ALU.subtract
                                               ).then_inc(tok["var_ready"], 1)
                dve.wait_ge(tok["rooted"], n)
                nc.vector.scalar_tensor_tensor(out=shift[s][:, :], in0=stat[s][:, 0:1], scalar=-1.0,
                                               in1=rstd[s][:, :], op0=ALU.mult, op1=ALU.mult
                                               ).then_inc(tok["shifted"], 1)
                dve.wait_ge(tok["shifted"], 2 * n)
                nc.vector.tensor_scalar(y[s][:, :, :], y[s][:, :, :], rstd[s][:, :], shift[s][:, :],
                                        ALU.mult, ALU.add).then_inc(tok["scaled"], 1)

            def weigh(i, s, which, weight, bias, out):
                n = nth(i, s, which)
                dve.wait_ge(tok["scaled"], n)
                nc.vector.tensor_tensor(y[s][:, :, :], y[s][:, :, :], weight, ALU.mult
                                        ).then_inc(tok["weighted"], 1)
                dve.wait_ge(tok["weighted"], n)
                nc.vector.tensor_tensor(out, y[s][:, :, :], bias, ALU.add).then_inc(tok["normed"], 1)

            with dve.Fori(0, BATCH // WIDE) as i:
                dve.wait_ge(tok["normed"], 2 * WIDE * i)
                for s in range(WIDE):
                    nc.vector.tensor_tensor(y[s][:, :, :], g.h[:, ds(TPS * (WIDE * i + s), TPS), :], g.t["pos"],
                                            ALU.add).then_inc(tok["placed"], 1)
                for s in range(WIDE):
                    dve.wait_ge(tok["keys"], at(i, s))
                    nc.vector.tensor_copy(key_t[s][:, :, :],
                                          g.ps[2 * s + 1][0:AUG, :].rearrange("p (c n) -> p c n", c=2)
                                          ).then_inc(tok["keys_kept"], 1)
                for s in range(WIDE):
                    dve.wait_ge(tok["scores"], at(i, s))
                    nc.vector.tensor_reduce(neg_max[s][:, :],
                                            g.ps[2 * s + 1][:, :].rearrange("p (t n) -> p t n", t=TPS),
                                            AX.X, ALU.max, negate=True).then_inc(tok["maxed"], 1)
                for s in range(WIDE):
                    dve.wait_ge(tok["probs_turned"], at(i, s))
                    nc.vector.tensor_copy(prob_t[s][:, :, :],
                                          g.ps[2 * s][:, :].rearrange("p (m n) -> p m n", m=TPS)
                                          ).then_inc(tok["probs_kept"], 1)
                    nc.vector.reciprocal(inv_sum[s][:, :], row_sum[s][:, :]).then_inc(tok["inverted"], 1)
                for s in range(WIDE):
                    dve.wait_ge(tok["mixed"], at(i, s))
                    dve.wait_ge(tok["inverted"], at(i, s))
                    for t in range(TPS):
                        nc.vector.scalar_tensor_tensor(
                            out=y[s][:, t, :], in0=g.ps[2 * s + 1][:, t * DIM:(t + 1) * DIM],
                            scalar=inv_sum[s][:, t:t + 1], in1=y[s][:, t, :], op0=ALU.mult, op1=ALU.add
                            ).then_inc(tok["added"], 1)
                for s in range(WIDE):
                    stats(i, s, 0, at(i, s, 2, 2))
                for s in range(WIDE):
                    variance(i, s, 0)
                for s in range(WIDE):
                    weigh(i, s, 0, g.t["ln_w1"], g.t["ln_b1"], y[s][:, :, :])
                for s in range(WIDE):
                    dve.wait_ge(tok["gelued"], at(i, s))
                    nc.vector.tensor_tensor(y[s][:, :, :], y[s][:, :, :], f_out[s][:, :, :], ALU.add
                                            ).then_inc(tok["fed_added"], 1)
                for s in range(WIDE):
                    dve.wait_ge(tok["fed_added"], at(i, s))
                    stats(i, s, 1, at(i, s, 2, 2))
                for s in range(WIDE):
                    variance(i, s, 1)
                for s in range(WIDE):
                    weigh(i, s, 1, g.t["ln_w2"], g.t["ln_b2"], g.h[:, ds(TPS * (WIDE * i + s), TPS), :])


def attention(nc, g):
    QUADS, QH = 3, 4
    PARTS = 6
    KS = PARTS * HDIM
    KM = KS + 2 * QH
    QK = 2 * TPS * HEADS
    SUM = HDIM
    with ExitStack() as ctx:
        sb = lambda name, shape, dt=F32: ctx.enter_context(nc.sbuf_tensor(name, shape, dt))
        sem = lambda name: g.stage_semaphore(ctx, nc.semaphore("att_" + name))
        q_t = [sb(f"q_t{s}", [KM, HEADS, SEQ], BF16) for s in range(2)]
        k_t = [sb(f"k_t{s}", [KM, HEADS, SEQ], BF16) for s in range(2)]
        val = [sb(f"val{s}", [P, TPS, HEADS, 32]) for s in range(2)]
        bn = sb("att_bn", [P, TPS, 6])
        mv = sb("att_mv", [P, TPS, 2])
        log_v = sb("att_log", [P, TPS])
        rstd = sb("att_rstd", [P, TPS])
        x = sb("att_x", [P, TPS, DIM])
        sq = sb("att_sq", [P, TPS, 2 * DIM])
        ss = sb("att_ss", [P, QK])
        log_s = sb("att_log_s", [P, QK])
        rms = sb("att_rms", [P, QK])
        weight = sb("att_weight", [P, HDIM])
        qk = sb("att_qk", [P, QK, HDIM])
        rem = sb("att_rem", [P, QK, HDIM])
        stack = sb("att_stack", [P, QK, PARTS, HDIM], BF16)
        neg_max = sb("att_max", [P, QH, TPS])
        max_rem = sb("att_max_rem", [P, TPS, QH])
        max_bf = sb("att_max_bf", [P, TPS, 2, QH], BF16)
        ident_b = sb("att_ident", [P, P], BF16)
        prob = [sb(f"att_prob{u}", [P, 2, TPS, SEQ]) for u in range(2)]
        out_t = sb("att_out_t", [P, QUADS, SEQ])
        inv = sb("att_inv", [P, TPS, HEADS])
        mixed = sb("att_mixed", [P, TPS, HEADS, HDIM])
        x_t, mixed_t = g.xt[0:2], g.xt[2]
        preset = sem("preset")
        val_cleared = sem("val_cleared")
        picks_cleared = sem("picks_cleared")
        picks_set = sem("picks_set")
        S = {n: sem(n) for n in (
            "stats", "mean_var", "logged", "rooted", "normed", "x_turned", "x_kept", "qk_made", "v_made",
            "v_kept", "squared", "summed", "rms_logged", "rms_rooted", "scaled", "weighted", "part1",
            "rem1", "part2", "part3", "copied", "filled", "fill_kept_v", "fill_kept_s",
            "max_scored", "maxed", "max_hi", "max_rem", "max_lo", "max_turned", "max_kept",
            "scored", "exped", "mixed", "out_kept", "out_turned", "inverted", "divided", "mixed_turned",
            "mixed_kept", "projected", "added", "weight_made")}
        block = ctx.enter_context(nc.Block())
        FILLS = {(1, 2): 0, (2, 1): 1, (2, 2): 2}
        O_BANKS = (4, 5)
        flat = lambda a, b, rows=P: g.psum[0:rows, a:b, :].rearrange("p b n -> p (b n)")

        def schedule(eng, prologue, body, finish):
            prologue()
            body(0, 0, first=True)
            with eng.Fori(0, (BATCH - 4) // 2) as i:
                body(2 * i + 1, 1)
                body(2 * i + 2, 0)
            body(BATCH - 3, 1, stat=False)
            body(BATCH - 2, 0, stat=False, make=False)
            body(BATCH - 1, 1, stat=False, make=False, fill=False)
            finish(BATCH - 1, 1)


        @block.tensor
        def _(pe):
            pe.wait_ge(preset, 5)

            def turn_x(n):
                if not isinstance(n, int) or n:
                    pe.wait_ge(S["scaled"], 2 * n)
                    pe.wait_ge(S["fill_kept_v"], 3 * (n - 1))
                    pe.wait_ge(S["fill_kept_s"], 3 * (n - 1))
                pe.wait_ge(S["normed"], 2 * n + 2)
                for c in range(2):
                    for t in range(TPS):
                        last = nc.tensor.transpose(
                            g.ps[6][0:HALF, c * SEQ + t * P:c * SEQ + (t + 1) * P],
                            x[:, t, c * HALF:(c + 1) * HALF], g.ident[:, :])
                last.then_inc(S["x_turned"], 1)

            def make_qk(n, s):
                pe.wait_ge(S["x_kept"], n + 1)
                for t in range(TPS):
                    for c in range(2):
                        k = HALF + c
                        last = nc.tensor.matmul(g.ps[7 - t][:, 0:2 * DIM], x_t[s][0:k, c, t * P:(t + 1) * P],
                                                g.t["qkv_t"][0:k, c, 0:2 * DIM], start=(c == 0), stop=(c == 1))
                    last.then_inc(S["qk_made"], 1)

            def make_v(n, s, scaled):
                pe.wait_ge(S["scaled"], 2 * scaled)
                for t in range(TPS):
                    for c in range(2):
                        k = HALF + c
                        last = nc.tensor.matmul(g.ps[7][:, t * DIM:(t + 1) * DIM],
                                                x_t[s][0:k, c, t * P:(t + 1) * P],
                                                g.t["qkv_t"][0:k, c, 2 * DIM:3 * DIM],
                                                start=(c == 0), stop=(c == 1))
                last.then_inc(S["v_made"], 1)

            def fill_quad(n, quad):
                if quad == 0:
                    pe.wait_ge(S["copied"], 6 * n + 6)
                    pe.wait_ge(S["part3"], 2 * n + 2)
                    pe.wait_ge(S["v_kept"], n + 1)
                for which, kept in ((0, "fill_kept_v"), (1, "fill_kept_s")):
                    if quad:
                        pe.wait_ge(S[kept], 3 * n + quad)
                    bank = g.ps[6 + which].bitcast(BF16)
                    for h in range(QH):
                        for t in range(TPS):
                            row = (t * 2 + which) * HEADS + quad * QH + h
                            last = nc.tensor.transpose(
                                bank[0:KS, h * SEQ + t * P:h * SEQ + (t + 1) * P],
                                stack[:, row, :, :].rearrange("p a b -> p (a b)"), ident_b[:, :])
                    last.then_inc(S["filled"], 1)

            def prologue():
                turn_x(0)
                make_qk(0, 0)
                turn_x(1)
                make_qk(1, 1)
                make_v(0, 0, 2)
                for quad in range(QUADS):
                    fill_quad(0, quad)

            def front(n, s, slot, stat, make, fills):
                if slot == (0, 1) and make:
                    turn_x(n + 2)
                if slot == (0, 2) and make:
                    make_qk(n + 2, s)
                if slot == (1, 2) and fills:
                    make_v(n + 1, 1 - s, n + 3 if make else BATCH)
                if slot in FILLS and fills:
                    fill_quad(n + 1, FILLS[slot])

            def max_scores(n, s, q, u):
                count = QUADS * n + q
                if u == 0:
                    pe.wait_ge(S["fill_kept_v"], 3 * n + q + 1)
                    pe.wait_ge(S["fill_kept_s"], 3 * n + q + 1)
                    pe.wait_ge(S["max_kept"], count)
                else:
                    pe.wait_ge(S["maxed"], 2 * count + 1)
                for hh in range(2):
                    h = QH * q + 2 * u + hh
                    for t in range(TPS):
                        last = nc.tensor.matmul(g.ps[hh][:, t * SEQ:(t + 1) * SEQ],
                                                q_t[s][0:KS, h, t * P:(t + 1) * P], k_t[s][0:KS, h, :],
                                                start=True, stop=True)
                last.then_inc(S["max_scored"], 1)

            def turn_max(n, q):
                count = QUADS * n + q
                pe.wait_ge(S["max_lo"], count + 1)
                for t in range(TPS):
                    last = nc.tensor.transpose(g.ps[0].bitcast(BF16)[KS:KM, t * P:(t + 1) * P],
                                               max_bf[:, t, :, :].rearrange("p a b -> p (a b)"), ident_b[:, :])
                last.then_inc(S["max_turned"], 1)

            def scores(n, s, q, u):
                count = 2 * (QUADS * n + q) + u
                if u == 0:
                    pe.wait_ge(S["max_kept"], QUADS * n + q + 1)
                pe.wait_ge(S["exped"], count)
                for hh in range(2):
                    h = QH * q + 2 * u + hh
                    for m in range(TPS):
                        last = nc.tensor.matmul(g.ps[2 + hh][:, m * SEQ:(m + 1) * SEQ],
                                                k_t[s][:, h, m * P:(m + 1) * P], q_t[s][:, h, :],
                                                start=True, stop=True)
                last.then_inc(S["scored"], 1)

            def mix(n, s, q):
                pe.wait_ge(S["exped"], 2 * (QUADS * n + q) + 2)
                if q == 0:
                    pe.wait_ge(S["mixed_kept"], n)
                    pe.wait_ge(S["added"], n)
                bank = g.ps[O_BANKS[q // 2]]
                for m in range(TPS):
                    for j in range(QH):
                        last = nc.tensor.matmul(
                            bank[32 * j:32 * j + 32, (q % 2) * SEQ:(q % 2 + 1) * SEQ],
                            val[s][:, m, QH * q + j, :], prob[j // 2][:, j % 2, m, :],
                            start=(m == 0), stop=(m == TPS - 1))
                last.then_inc(S["mixed"], 1)

            def turn_out(n):
                pe.wait_ge(S["out_kept"], n + 1)
                for t in range(TPS):
                    for q in range(QUADS):
                        last = nc.tensor.transpose(g.ps[O_BANKS[t]][:, q * P:(q + 1) * P],
                                                   out_t[:, q, t * P:(t + 1) * P], g.ident[:, :])
                last.then_inc(S["out_turned"], 1)

            def turn_mixed(n):
                pe.wait_ge(S["divided"], n + 1)
                flat_mixed = mixed[:, :, :, :].rearrange("p t h d -> p t (h d)")
                for c in range(2):
                    for t in range(TPS):
                        last = nc.tensor.transpose(
                            g.ps[4][0:HALF, c * SEQ + t * P:c * SEQ + (t + 1) * P],
                            flat_mixed[:, t, c * HALF:(c + 1) * HALF], g.ident[:, :])
                last.then_inc(S["mixed_turned"], 1)

            def project(n):
                pe.wait_ge(S["mixed_kept"], n + 1)
                for t in range(TPS):
                    for c in range(2):
                        k = HALF + c
                        last = nc.tensor.matmul(g.ps[5][:, t * DIM:(t + 1) * DIM],
                                                mixed_t[0:k, c, t * P:(t + 1) * P],
                                                g.t["proj_t"][0:k, c, :], start=(c == 0), stop=(c == 1))
                last.then_inc(S["projected"], 1)

            def body(n, s, first=False, stat=True, make=True, fill=True):
                for q in range(QUADS):
                    pn, ps_, pq = (n, s, q - 1) if q else (n - 1, 1 - s, QUADS - 1)
                    prev = q or not first
                    max_scores(n, s, q, 0)
                    if prev:
                        scores(pn, ps_, pq, 0)
                    if q == 1 and not first:
                        turn_out(n - 1)
                    front(n, s, (q, 0), stat, make, fill)
                    max_scores(n, s, q, 1)
                    if prev:
                        scores(pn, ps_, pq, 1)
                    if q == 1 and not first:
                        turn_mixed(n - 1)
                    front(n, s, (q, 1), stat, make, fill)
                    if q == 1 and not first:
                        project(n - 1)
                    if prev:
                        mix(pn, ps_, pq)
                    turn_max(n, q)
                    front(n, s, (q, 2), stat, make, fill)

            def finish(n, s):
                for u in range(2):
                    scores(n, s, QUADS - 1, u)
                mix(n, s, QUADS - 1)
                turn_out(n)
                turn_mixed(n)
                project(n)

            schedule(pe, prologue, body, finish)


        @block.scalar
        def _(act):
            nc.scalar.preload_act_table_set(EXP_LN)
            act.wait_ge(g.consts_set, 2)

            def root_var(n):
                act.wait_ge(S["mean_var"], 2 * n + 2)
                nc.scalar.activation(log_v[:, :], mv[:, :, 1], ACT.Ln, bias=g.eps5[:, :]).then_inc(S["logged"], 1)
                act.wait_ge(S["logged"], n + 1)
                nc.scalar.activation(rstd[:, :], log_v[:, :], ACT.Exp, scale=-0.5).then_inc(S["rooted"], 1)

            def keep_x(n, s):
                act.wait_ge(S["x_turned"], n + 1)
                nc.scalar.copy(x_t[s][0:HALF, :, :], g.ps[6][0:HALF, :].rearrange("p (c n) -> p c n", c=2)
                               ).then_inc(S["x_kept"], 1)

            def square(n):
                for t in range(TPS):
                    act.wait_ge(S["qk_made"], 2 * n + t + 1)
                    nc.scalar.activation(sq[:, t, :], g.ps[7 - t][:, 0:2 * DIM], ACT.Square
                                         ).then_inc(S["squared"], 1)

            def root_rms(n):
                act.wait_ge(S["summed"], n + 1)
                nc.scalar.activation(log_s[:, :], ss[:, :], ACT.Ln, scale=1.0 / HDIM, bias=g.rms_eps[:, :]
                                     ).then_inc(S["rms_logged"], 1)
                act.wait_ge(S["rms_logged"], n + 1)
                nc.scalar.activation(rms[:, :], log_s[:, :], ACT.Exp, scale=-0.5).then_inc(S["rms_rooted"], 1)

            def keep_v(n, s):
                act.wait_ge(S["v_made"], n + 1)
                nc.scalar.copy(val[s][:, :, :, 0:HDIM].rearrange("p t h d -> p (t h) d"),
                               g.ps[7][:, 0:TPS * DIM].rearrange("p (g d) -> p g d", d=HDIM)
                               ).then_inc(S["v_kept"], 1)

            def keep_fill(n, s, quad):
                act.wait_ge(S["filled"], 6 * n + 2 * quad + 2)
                nc.scalar.copy(k_t[s][0:KS, quad * QH:(quad + 1) * QH, :],
                               g.ps[7].bitcast(BF16)[0:KS, :].rearrange("p (h n) -> p h n", h=QH)
                               ).then_inc(S["fill_kept_s"], 1)

            def prologue():
                for n in range(2):
                    root_var(n)
                    keep_x(n, n)
                    square(n)
                    root_rms(n)
                root_var(2)
                keep_v(0, 0)
                for quad in range(QUADS):
                    keep_fill(0, 0, quad)

            def front(n, s, slot, stat, make, fills):
                if slot == (0, 1) and make:
                    keep_x(n + 2, s)
                if slot == (0, 2) and make:
                    square(n + 2)
                if slot == (1, 0) and make:
                    root_rms(n + 2)
                if slot == (1, 2) and fills:
                    keep_v(n + 1, 1 - s)
                if slot in FILLS and fills:
                    keep_fill(n + 1, 1 - s, FILLS[slot])
                if slot == (2, 2) and stat:
                    root_var(n + 3)

            def expo(n, q, u):
                count = 2 * (QUADS * n + q) + u
                act.wait_ge(S["scored"], count + 1)
                act.wait_ge(S["mixed"], QUADS * n + q)
                nc.scalar.activation(prob[u][:, :, :, :].rearrange("p a b n -> p (a b n)"), flat(2, 4), ACT.Exp
                                     ).then_inc(S["exped"], 1)

            def keep_out(n):
                act.wait_ge(S["mixed"], QUADS * n + QUADS)
                nc.scalar.copy(out_t[:, :, :].rearrange("p q n -> p (q n)"), flat(4, 6)[:, 0:QUADS * SEQ]
                               ).then_inc(S["out_kept"], 1)

            def keep_mixed(n):
                act.wait_ge(S["mixed_turned"], n + 1)
                nc.scalar.copy(mixed_t[0:HALF, :, :], g.ps[4][0:HALF, :].rearrange("p (c n) -> p c n", c=2)
                               ).then_inc(S["mixed_kept"], 1)

            def body(n, s, first=False, stat=True, make=True, fill=True):
                for q in range(QUADS):
                    pn, pq = (n, q - 1) if q else (n - 1, QUADS - 1)
                    prev = q or not first
                    if q == 1 and not first:
                        keep_out(n - 1)
                    if prev:
                        expo(pn, pq, 0)
                    front(n, s, (q, 0), stat, make, fill)
                    if prev:
                        expo(pn, pq, 1)
                    if q == 1 and not first:
                        keep_mixed(n - 1)
                    front(n, s, (q, 1), stat, make, fill)
                    front(n, s, (q, 2), stat, make, fill)

            def finish(n, s):
                for u in range(2):
                    expo(n, QUADS - 1, u)
                keep_out(n)
                keep_mixed(n)

            schedule(act, prologue, body, finish)


        @block.vector
        def _(dve):
            nc.vector.tensor_copy(ident_b[:, :], g.ident[:, :]).then_inc(preset, 1)
            for s in range(2):
                nc.vector.memset(val[s][:, :, :, HDIM:], 0.0).then_inc(val_cleared, 1)
            dve.wait_ge(val_cleared, 2)
            for s in range(2):
                nc.vector.memset(val[s][:, :, :, SUM:SUM + 1], 1.0).then_inc(preset, 1)

            def norm_stats(n):
                dve.wait_ge(S["rooted"], n)
                for t in range(TPS):
                    nc.vector.nop(nofuse=True)
                    nc.vector.bn_stats(bn[:, t, :], g.h[:, ds(TPS * n + t, 1), :].rearrange("p a n -> p (a n)")
                                       ).then_inc(S["stats"], 1)
                dve.wait_ge(S["stats"], 2 * n + 2)
                nc.vector.nop(nofuse=True)
                for t in range(TPS):
                    nc.vector.bn_aggr(mv[:, t, :], bn[:, t, :]).then_inc(S["mean_var"], 1)

            def norm(n):
                dve.wait_ge(S["rooted"], n + 1)
                dve.wait_ge(S["x_turned"], n)
                for t in range(TPS):
                    nc.vector.tensor_scalar(x[:, t, :], g.h[:, ds(TPS * n + t, 1), :].rearrange("p a n -> p (a n)"),
                                            mv[:, t, 0:1], rstd[:, t:t + 1], ALU.subtract, ALU.mult
                                            ).then_inc(S["normed"], 1)

            def sum_squares(n):
                dve.wait_ge(S["squared"], 2 * n + 2)
                nc.vector.tensor_reduce(ss[:, :], sq[:, :, :].rearrange("p t (g d) -> p (t g) d", d=HDIM),
                                        AX.X, ALU.add).then_inc(S["summed"], 1)

            def scale(n):
                dve.wait_ge(S["rms_rooted"], n + 1)
                dve.wait_ge(S["part3"], 2 * n)
                for t in range(TPS):
                    r = rms[:, t * 24:(t + 1) * 24]
                    nc.vector.tensor_tensor(qk[:, t * 24:(t + 1) * 24, :],
                                            g.ps[7 - t][:, 0:2 * DIM].rearrange("p (g d) -> p g d", d=HDIM),
                                            r.unsqueeze(2).broadcast_to((P, 24, HDIM)), ALU.mult
                                            ).then_inc(S["scaled"], 1)

            def slots(which, first, count, step=1):
                rows = stack[:, :, :, :].rearrange("p (t w h) a d -> p t w h a d", t=TPS, w=2)[:, :, which]
                return rows[:, :, :, first:first + step * (count - 1) + 1:step, :]

            def split(n):
                both = lambda v, which: v[:, :, :].rearrange("p (t w h) d -> p t w h d", t=TPS, w=2)[:, :, which]
                dve.wait_ge(S["weighted"], 2 * n + 2)
                dve.wait_ge(S["filled"], 6 * n)
                for which, slot in ((0, 0), (1, 5)):
                    nc.vector.tensor_copy(slots(which, slot, 1)[:, :, :, 0], both(qk, which)).then_inc(S["part1"], 1)
                dve.wait_ge(S["part1"], 2 * n + 2)
                for which, slot in ((0, 0), (1, 5)):
                    nc.vector.tensor_tensor(both(rem, which), both(qk, which), slots(which, slot, 1)[:, :, :, 0],
                                            ALU.subtract).then_inc(S["rem1"], 1)

            def split_rest(n):
                both = lambda v, which: v[:, :, :].rearrange("p (t w h) d -> p t w h d", t=TPS, w=2)[:, :, which]
                dve.wait_ge(S["rem1"], 2 * n + 2)
                for which, slot in ((0, 1), (1, 0)):
                    nc.vector.tensor_copy(slots(which, slot, 1)[:, :, :, 0], both(rem, which)).then_inc(S["part2"], 1)
                dve.wait_ge(S["part2"], 2 * n + 2)
                for which, slot, part2 in ((0, 5, 1), (1, 2, 0)):
                    nc.vector.tensor_tensor(slots(which, slot, 1)[:, :, :, 0], both(rem, which),
                                            slots(which, part2, 1)[:, :, :, 0], ALU.subtract
                                            ).then_inc(S["part3"], 1)

            def repeat(n):
                dve.wait_ge(S["part2"], 2 * n + 2)
                dve.wait_ge(S["filled"], 6 * n)
                for which, to, of in ((0, 2, 0), (0, 4, 0), (0, 3, 1), (1, 3, 5), (1, 4, 5), (1, 1, 0)):
                    nc.vector.tensor_copy(slots(which, to, 1)[:, :, :, 0], slots(which, of, 1)[:, :, :, 0]
                                          ).then_inc(S["copied"], 1)

            def keep_fill(n, s, quad):
                dve.wait_ge(S["filled"], 6 * n + 2 * quad + 1)
                nc.vector.tensor_copy(q_t[s][0:KS, quad * QH:(quad + 1) * QH, :],
                                      g.ps[6].bitcast(BF16)[0:KS, :].rearrange("p (h n) -> p h n", h=QH)
                                      ).then_inc(S["fill_kept_v"], 1)

            def prologue():
                norm_stats(0)
                norm(0)
                sum_squares(0)
                scale(0)
                norm_stats(1)
                norm(1)
                norm_stats(2)
                split(0)
                split_rest(0)
                repeat(0)
                sum_squares(1)
                scale(1)
                for quad in range(QUADS):
                    keep_fill(0, 0, quad)

            def front(n, s, slot, stat, make, fills):
                if slot == (0, 0) and make:
                    norm(n + 2)
                if slot == (0, 1) and fills:
                    split(n + 1)
                if slot == (0, 2) and fills:
                    split_rest(n + 1)
                if slot == (1, 0):
                    if make:
                        sum_squares(n + 2)
                    if fills:
                        repeat(n + 1)
                if slot == (1, 1) and make:
                    scale(n + 2)
                if slot in FILLS and fills:
                    keep_fill(n + 1, 1 - s, FILLS[slot])
                if slot == (2, 2) and stat:
                    norm_stats(n + 3)

            def row_max(n, q, u):
                count = QUADS * n + q
                dve.wait_ge(S["max_scored"], 2 * count + u + 1)
                if u == 0:
                    dve.wait_ge(S["max_hi"], count)
                    dve.wait_ge(S["max_rem"], count)
                nc.vector.tensor_reduce(neg_max[:, 2 * u:2 * u + 2, :].rearrange("p a b -> p (a b)"),
                                        flat(0, 2).rearrange("p (g n) -> p g n", n=SEQ), AX.X, ALU.max,
                                        negate=True).then_inc(S["maxed"], 1)

            def split_max(n, q):
                count = QUADS * n + q
                by_tile = neg_max[:, :, :].rearrange("p h t -> p t h")
                dve.wait_ge(S["maxed"], 2 * count + 2)
                dve.wait_ge(S["max_turned"], count)
                nc.vector.tensor_copy(max_bf[:, :, 0, :], by_tile).then_inc(S["max_hi"], 1)
                dve.wait_ge(S["max_hi"], count + 1)
                dve.wait_ge(S["max_lo"], count)
                nc.vector.tensor_tensor(max_rem[:, :, :], by_tile, max_bf[:, :, 0, :], ALU.subtract
                                        ).then_inc(S["max_rem"], 1)
                dve.wait_ge(S["max_rem"], count + 1)
                nc.vector.tensor_copy(max_bf[:, :, 1, :], max_rem[:, :, :]).then_inc(S["max_lo"], 1)

            def keep_max(n, s, q):
                count = QUADS * n + q
                dve.wait_ge(S["max_turned"], count + 1)
                nc.vector.tensor_copy(q_t[s][KS:KM, QH * q:QH * (q + 1), :],
                                      g.ps[0].bitcast(BF16)[KS:KM, 0:SEQ].unsqueeze(1).broadcast_to((2 * QH, QH, SEQ))
                                      ).then_inc(S["max_kept"], 1)

            def divide(n):
                by_head = g.psum[:, 4:6, 0:QUADS * P].rearrange("p t (h c) -> p t h c", c=32)
                dve.wait_ge(S["out_turned"], n + 1)
                dve.wait_ge(S["divided"], n)
                nc.vector.reciprocal(inv[:, :, :], by_head[:, :, :, SUM]).then_inc(S["inverted"], 1)
                dve.wait_ge(S["inverted"], n + 1)
                dve.wait_ge(S["mixed_turned"], n)
                nc.vector.tensor_tensor(mixed[:, :, :, :], by_head[:, :, :, 0:HDIM],
                                        inv[:, :, :].unsqueeze(3).broadcast_to((P, TPS, HEADS, HDIM)), ALU.mult
                                        ).then_inc(S["divided"], 1)

            def add(n):
                dve.wait_ge(S["projected"], n + 1)
                state = g.h[:, ds(TPS * n, TPS), :]
                nc.vector.tensor_tensor(state, state,
                                        g.ps[5][:, 0:TPS * DIM].rearrange("p (t d) -> p t d", t=TPS), ALU.add
                                        ).then_inc(S["added"], 1)

            def body(n, s, first=False, stat=True, make=True, fill=True):
                for q in range(QUADS):
                    row_max(n, q, 0)
                    if q == 1 and not first:
                        divide(n - 1)
                    front(n, s, (q, 0), stat, make, fill)
                    row_max(n, q, 1)
                    split_max(n, q)
                    front(n, s, (q, 1), stat, make, fill)
                    if q == 1 and not first:
                        add(n - 1)
                    keep_max(n, s, q)
                    front(n, s, (q, 2), stat, make, fill)

            def finish(n, s):
                divide(n)
                add(n)

            schedule(dve, prologue, body, finish)


        @block.gpsimd
        def _(pool):
            nc.gpsimd.tensor_tensor(weight[:, :], g.t["qk_weights"][:, 0, :], g.t["qk_weights"][:, 1, :], ALU.mult
                                    ).then_inc(S["weight_made"], 1)
            pool.wait_ge(S["weight_made"], 1)
            nc.gpsimd.tensor_scalar(weight[:, :], weight[:, :], float(HDIM) ** -0.5, None, ALU.mult
                                    ).then_inc(S["weight_made"], 1)
            pool.wait_ge(S["weight_made"], 2)
            for s in range(2):
                nc.gpsimd.memset(k_t[s][KS:KM, :, :], 0.0).then_inc(picks_cleared, 1)
            pool.wait_ge(picks_cleared, 2)
            for r in range(2):
                for s in range(2):
                    rows = k_t[s][KS:KM, :, :].rearrange("p (q h) n -> p q h n", h=QH)
                    nc.gpsimd.affine_select(out=rows, in_=rows, compare_op=ALU.not_equal, fill=1.0,
                                            base=-QH * r, pattern=[[0, QUADS], [-1, QH], [0, SEQ]],
                                            channel_multiplier=1).then_inc(preset if r else picks_set, 1)
                if r == 0:
                    pool.wait_ge(picks_set, 2)

            def weigh(n):
                for t in range(TPS):
                    pool.wait_ge(S["scaled"], 2 * n + t + 1)
                    q_part = qk[:, 2 * t * HEADS:(2 * t + 1) * HEADS, :]
                    nc.gpsimd.tensor_tensor(q_part, q_part,
                                            weight[:, :].unsqueeze(1).broadcast_to((P, HEADS, HDIM)), ALU.mult
                                            ).then_inc(S["weighted"], 1)

            def prologue():
                weigh(0)
                weigh(1)

            def body(n, s, first=False, stat=True, make=True, fill=True):
                if make:
                    weigh(n + 2)

            schedule(pool, prologue, body, lambda n, s: None)


def first_slots(nc, g):
    with ExitStack() as ctx:
        def sb(name, shape, dt=F32):
            return [ctx.enter_context(nc.sbuf_tensor(f"fs_{name}{s}", shape, dt)) for s in range(WIDE)]

        sem = lambda name: g.stage_semaphore(ctx, nc.semaphore("fs_" + name))
        bn = sb("bn", [P, TPS, 6])
        mv = sb("mv", [P, TPS, 2])
        log_v = sb("log_v", [P, TPS])
        factor = sb("factor", [P, TPS])
        x = sb("x", [P, TPS, DIM])
        x_t = sb("x_t", [HALF, 2, SEQ])
        neg_slot = sb("neg_slot", [P, GPS])
        neg_tok = sb("neg_tok", [P, TPS])
        disp_t = sb("disp_t", [P, SEQ])
        disp_sum = sb("disp_sum", [P, GPS])
        comb = sb("comb", [P, TPS, P])
        comb_sum = sb("comb_sum", [P, TPS])
        comb_inv = sb("comb_inv", [P, TPS])
        disp = sb("disp", [P, GPS, P])
        square = sb("square", [P, DIM])
        slot_ss = sb("slot_ss", [P, GPS])
        eps_part = sb("eps_part", [P, GPS])
        slot_var = sb("slot_var", [P, GPS])
        slot_log = sb("slot_log", [P, GPS])
        slot_fac = sb("slot_fac", [P, GPS])
        yn = sb("yn", [P, GPS, DIM])
        S = {n: sem(n) for n in (
            "stats", "mean_var", "logged", "rooted", "centred", "weighted", "turned", "kept", "logits",
            "slot_maxed", "tok_maxed", "disp_exped", "comb_exped", "inverted", "combined", "disp_turned",
            "comb_turned", "disp_kept", "comb_kept", "slots_made", "squared", "eps_made", "var_made",
            "slot_logged", "slot_rooted", "slots_normed", "stored", "means_made", "means_kept", "zeroed")}
        at = lambda i, s, per=1: (WIDE * i + s + 1) * per
        block = ctx.enter_context(nc.Block())

        @block.tensor
        def _(pe):
            pe.wait_ge(S["zeroed"], 2 * WIDE)
            with pe.Fori(0, BATCH // WIDE) as i:
                for s in range(WIDE):
                    pe.wait_ge(S["weighted"], at(i, s))
                    for c in range(2):
                        for t in range(TPS):
                            last = nc.tensor.transpose(
                                g.ps[2 * s][0:HALF, c * SEQ + t * P:c * SEQ + (t + 1) * P],
                                x[s][:, t, c * HALF:(c + 1) * HALF], g.ident[:, :])
                    last.then_inc(S["turned"], 1)
                for s in range(WIDE):
                    pe.wait_ge(S["kept"], at(i, s))
                    bank = g.ps[2 * s + 1]
                    for c in range(2):
                        nc.tensor.matmul(bank[:, 0:SEQ], g.phi_t[:, c, :], x_t[s][0:HALF, c, :],
                                         start=(c == 0), stop=(c == 1))
                    for t in range(TPS):
                        for c in range(2):
                            last = nc.tensor.matmul(bank[:, SEQ + t * P:SEQ + (t + 1) * P],
                                                    x_t[s][0:HALF, c, t * P:(t + 1) * P], g.phi_t[:, c, :],
                                                    start=(c == 0), stop=(c == 1))
                    last.then_inc(S["logits"], 1)
                for s in range(WIDE):
                    pe.wait_ge(S["disp_exped"], at(i, s, GPS))
                    for t in range(TPS):
                        last = nc.tensor.transpose(g.ps[2 * s][:, t * P:(t + 1) * P],
                                                   disp_t[s][:, t * P:(t + 1) * P], g.ident[:, :])
                    last.then_inc(S["disp_turned"], 1)
                for s in range(WIDE):
                    pe.wait_ge(S["combined"], at(i, s))
                    for t in range(TPS):
                        last = nc.tensor.transpose(g.ps[2 * s + 1][:, t * P:(t + 1) * P], comb[s][:, t, :],
                                                   g.ident[:, :])
                    last.then_inc(S["comb_turned"], 1)
                for s in range(WIDE):
                    pe.wait_ge(S["disp_kept"], at(i, s, 2))
                    pe.wait_ge(S["comb_kept"], at(i, s))
                    for gr in range(GPS):
                        t = gr // 2
                        last = nc.tensor.matmul(g.ps[2 * s + gr % 2][:, t * DIM:(t + 1) * DIM],
                                                disp[s][:, gr, :], x[s][:, t, :], start=True, stop=True)
                    last.then_inc(S["slots_made"], 1)
                for s in range(WIDE):
                    pe.wait_ge(S["slots_normed"], at(i, s, GPS))
                    for c in range(2):
                        for gr in range(GPS):
                            m0 = (c * GPS + gr) * (P // MEAN)
                            last = nc.tensor.matmul(g.ps[2 * s + 1][0:HALF, m0:m0 + P // MEAN],
                                                    yn[s][:, gr, c * HALF:(c + 1) * HALF], g.average[:, :],
                                                    start=True, stop=True)
                    last.then_inc(S["means_made"], 1)

        @block.scalar
        def _(act):
            nc.scalar.preload_act_table_set(EXP_LN)
            act.wait_ge(g.consts_set, 2)
            with act.Fori(0, BATCH // WIDE) as i:
                for s in range(WIDE):
                    act.wait_ge(S["mean_var"], at(i, s, TPS))
                    nc.scalar.activation(log_v[s][:, :], mv[s][:, :, 1], ACT.Ln, scale=1.0 + 1e-6 / DIM,
                                         bias=g.eps_norms[:, :]).then_inc(S["logged"], 1)
                    act.wait_ge(S["logged"], at(i, s))
                    nc.scalar.activation(factor[s][:, :], log_v[s][:, :], ACT.Exp, scale=-0.5
                                         ).then_inc(S["rooted"], 1)
                for s in range(WIDE):
                    act.wait_ge(S["turned"], at(i, s))
                    nc.scalar.copy(x_t[s][0:HALF, :, :], g.ps[2 * s][0:HALF, :].rearrange("p (c n) -> p c n", c=2)
                                   ).then_inc(S["kept"], 1)
                for s in range(WIDE):
                    act.wait_ge(S["slot_maxed"], at(i, s))
                    act.wait_ge(S["tok_maxed"], at(i, s))
                    for gr in range(GPS):
                        cols = slice(gr * GROUP, (gr + 1) * GROUP)
                        nc.scalar.activation(disp_t[s][:, cols], g.ps[2 * s + 1][:, cols], ACT.Exp,
                                             bias=neg_slot[s][:, gr:gr + 1], accum_out=disp_sum[s][:, gr:gr + 1]
                                             ).then_inc(S["disp_exped"], 1)
                    for t in range(TPS):
                        nc.scalar.activation(comb[s][:, t, :], g.ps[2 * s + 1][:, SEQ + t * P:SEQ + (t + 1) * P],
                                             ACT.Exp, bias=neg_tok[s][:, t:t + 1],
                                             accum_out=comb_sum[s][:, t:t + 1]).then_inc(S["comb_exped"], 1)
                for s in range(WIDE):
                    act.wait_ge(S["disp_turned"], at(i, s))
                    for half in range(2):
                        rows = slice(GROUP * half, GROUP * (half + 1))
                        nc.scalar.copy(disp[s][rows, half::2, :],
                                       g.ps[2 * s][rows, 0:SEQ].rearrange("p (t n) -> p t n", t=TPS)
                                       ).then_inc(S["disp_kept"], 1)
                for s in range(WIDE):
                    act.wait_ge(S["slots_made"], at(i, s))
                    for gr in range(GPS):
                        t = gr // 2
                        act.wait_ge(S["squared"], at(i, s, GPS) - GPS + gr)
                        nc.scalar.activation(square[s][:, :],
                                             g.ps[2 * s + gr % 2][:, t * DIM:(t + 1) * DIM], ACT.Square,
                                             accum_out=slot_ss[s][:, gr:gr + 1]).then_inc(S["squared"], 1)
                for s in range(WIDE):
                    act.wait_ge(S["var_made"], at(i, s))
                    nc.scalar.activation(slot_log[s][:, :], slot_var[s][:, :], ACT.Ln, scale=1.0 / DIM
                                         ).then_inc(S["slot_logged"], 1)
                    act.wait_ge(S["slot_logged"], at(i, s))
                    nc.scalar.activation(slot_fac[s][:, :], slot_log[s][:, :], ACT.Exp, scale=-0.5
                                         ).then_inc(S["slot_rooted"], 1)

        @block.vector
        def _(dve):
            with dve.Fori(0, BATCH // WIDE) as i:
                for s in range(WIDE):
                    dve.wait_ge(S["rooted"], WIDE * i)
                    for t in range(TPS):
                        nc.vector.nop(nofuse=True)
                        row = g.h[:, ds(TPS * (WIDE * i + s) + t, 1), :].rearrange("p a n -> p (a n)")
                        nc.vector.bn_stats(bn[s][:, t, :], row).then_inc(S["stats"], 1)
                    dve.wait_ge(S["stats"], at(i, s, TPS))
                    nc.vector.nop(nofuse=True)
                    for t in range(TPS):
                        nc.vector.bn_aggr(mv[s][:, t, :], bn[s][:, t, :]).then_inc(S["mean_var"], 1)
                for s in range(WIDE):
                    dve.wait_ge(S["rooted"], at(i, s))
                    dve.wait_ge(S["slots_made"], WIDE * i)
                    for t in range(TPS):
                        row = g.h[:, ds(TPS * (WIDE * i + s) + t, 1), :].rearrange("p a n -> p (a n)")
                        nc.vector.tensor_scalar(x[s][:, t, :], row, mv[s][:, t, 0:1], factor[s][:, t:t + 1],
                                                ALU.subtract, ALU.mult).then_inc(S["centred"], 1)
                for s in range(WIDE):
                    dve.wait_ge(S["centred"], at(i, s, TPS))
                    nc.vector.tensor_tensor(x[s][:, :, :], x[s][:, :, :],
                                            g.t["gamma_in"].unsqueeze(1).broadcast_to((P, TPS, DIM)), ALU.mult
                                            ).then_inc(S["weighted"], 1)
                for s in range(WIDE):
                    dve.wait_ge(S["logits"], at(i, s))
                    nc.vector.tensor_reduce(neg_slot[s][:, :],
                                            g.ps[2 * s + 1][:, 0:SEQ].rearrange("p (g n) -> p g n", g=GPS),
                                            AX.X, ALU.max, negate=True).then_inc(S["slot_maxed"], 1)
                    nc.vector.tensor_reduce(neg_tok[s][:, :],
                                            g.ps[2 * s + 1][:, SEQ:].rearrange("p (t n) -> p t n", t=TPS),
                                            AX.X, ALU.max, negate=True).then_inc(S["tok_maxed"], 1)
                for s in range(WIDE):
                    dve.wait_ge(S["comb_exped"], at(i, s, TPS))
                    nc.vector.reciprocal(comb_inv[s][:, :], comb_sum[s][:, :]).then_inc(S["inverted"], 1)
                    dve.wait_ge(S["inverted"], at(i, s))
                    nc.vector.tensor_tensor(comb[s][:, :, :], comb[s][:, :, :],
                                            comb_inv[s][:, :].unsqueeze(2).broadcast_to((P, TPS, P)), ALU.mult
                                            ).then_inc(S["combined"], 1)
                for s in range(WIDE):
                    dve.wait_ge(S["comb_turned"], at(i, s))
                    nc.vector.nop(nofuse=True)
                    nc.vector.tensor_copy(g.comb_t[:, ds((WIDE * i + s) * SEQ, SEQ)], g.ps[2 * s + 1][:, 0:SEQ]
                                          ).then_inc(S["comb_kept"], 1)
                for s in range(WIDE):
                    nc.vector.scalar_tensor_tensor(out=eps_part[s][:, :], in0=disp_sum[s][:, :], scalar=1e-6,
                                                   in1=disp_sum[s][:, :], op0=ALU.mult, op1=ALU.mult
                                                   ).then_inc(S["eps_made"], 1)
                    dve.wait_ge(S["eps_made"], at(i, s))
                    dve.wait_ge(S["squared"], at(i, s, GPS))
                    nc.vector.tensor_tensor(slot_var[s][:, :], slot_ss[s][:, :], eps_part[s][:, :], ALU.add
                                            ).then_inc(S["var_made"], 1)
                for s in range(WIDE):
                    dve.wait_ge(S["slot_rooted"], at(i, s))
                    dve.wait_ge(S["stored"], WIDE * i)
                    for gr in range(GPS):
                        t = gr // 2
                        nc.vector.scalar_tensor_tensor(
                            out=yn[s][:, gr, :], in0=g.ps[2 * s + gr % 2][:, t * DIM:(t + 1) * DIM],
                            scalar=slot_fac[s][:, gr:gr + 1], in1=g.t["gamma2"], op0=ALU.mult, op1=ALU.mult
                            ).then_inc(S["slots_normed"], 1)
                for s in range(WIDE):
                    dve.wait_ge(S["means_made"], at(i, s))
                    nc.vector.nop(nofuse=True)
                    for c in range(2):
                        nc.vector.tensor_copy(
                            g.means_t[:, c, :, ds((WIDE * i + s) * GPS, GPS), :],
                            g.ps[2 * s + 1][0:HALF, c * P:(c + 1) * P].rearrange("p (g k m) -> p k g m", g=GPS, k=E1)
                            ).then_inc(S["means_kept"], 1)

        @block.gpsimd
        def _(pool):
            for s in range(WIDE):
                nc.gpsimd.memset(disp[s][0:GROUP, 1::2, :], 0.0).then_inc(S["zeroed"], 1)
                nc.gpsimd.memset(disp[s][GROUP:P, 0::2, :], 0.0).then_inc(S["zeroed"], 1)
            with pool.Fori(0, BATCH // WIDE) as i:
                for s in range(WIDE):
                    pool.wait_ge(S["slots_normed"], at(i, s, GPS))
                    nc.gpsimd.nop(nofuse=True)
                    nc.gpsimd.tensor_copy(g.yn[:, ds((WIDE * i + s) * GPS, GPS), :], yn[s][:, :, :]
                                          ).then_inc(S["stored"], 1)


def second_slots(nc, g):
    with ExitStack() as ctx:
        def sb(name, shape, dt=F32):
            return [ctx.enter_context(nc.sbuf_tensor(f"ss_{name}{s}", shape, dt)) for s in range(W)]

        sem = lambda name: g.stage_semaphore(ctx, nc.semaphore("ss_" + name))
        weight = sb("weight", [HALF, 2, E2 * DIM])
        mean_k = sb("mean_k", [HALF, 2, P])
        square = sb("square", [P, DIM])
        ss = sb("ss", [P, E2])
        log_s = sb("log_s", [P, E2])
        factor = sb("factor", [P, E2])
        se = sb("se", [P, E2, DIM])
        loaded = [sem(f"loaded{s}") for s in range(W)]
        S = {n: [sem(f"{n}{s}") for s in range(W)] for n in (
            "means", "made", "squared", "logged", "rooted", "normed", "turned", "kept_v", "kept_s")}
        block = ctx.enter_context(nc.Block())

        def pipeline(eng, early, late):
            early(0, 0)
            with eng.Fori(0, E1 // W - 1) as i:
                early(i, 1)
                late(i, 0)
                early(i + 1, 0)
                late(i, 1)
            early(E1 // W - 1, 1)
            late(E1 // W - 1, 0)
            late(E1 // W - 1, 1)

        @block.sync
        def _(sp):
            with sp.Fori(0, E1 // W) as i:
                for s in range(W):
                    sp.wait_ge(S["made"][s], i)
                    sp.dma_start(weight[s][:, :, :],
                                 g.d["w_slot2"][ds(W * i + s, 1)].rearrange("a p c n -> (a p) c n")
                                 ).then_inc(loaded[s], 16)

        @block.gpsimd
        def _(pool):
            with pool.Fori(0, E1 // W) as i:
                for s in range(W):
                    pool.wait_ge(S["made"][s], i)
                    nc.gpsimd.nop(nofuse=True)
                    nc.gpsimd.tensor_copy(mean_k[s][:, :, :].unsqueeze(2),
                                          g.means_t[:, :, ds(W * i + s, 1), :, :].rearrange(
                                              "p c k g m -> p c k (g m)")).then_inc(S["means"][s], 1)

        @block.tensor
        def _(pe):
            def make(i, s):
                pe.wait_ge(loaded[s], 16 * (i + 1))
                pe.wait_ge(S["means"][s], i + 1)
                pe.wait_ge(S["normed"][s], i)
                for b in range(2):
                    for c in range(2):
                        last = nc.tensor.matmul(g.ps[4 * s + b][:, 0:2 * DIM], mean_k[s][:, c, :],
                                                weight[s][:, c, b * 2 * DIM:(b + 1) * 2 * DIM],
                                                start=(c == 0), stop=(c == 1))
                last.then_inc(S["made"][s], 1)

            def turn(i, s):
                pe.wait_ge(S["normed"][s], i + 1)
                pe.wait_ge(S["kept_v"][s], i)
                pe.wait_ge(S["kept_s"][s], i)
                for c in range(2):
                    for e in range(E2):
                        last = nc.tensor.transpose(g.ps[4 * s + 2 + c][0:HALF, e * P:(e + 1) * P],
                                                   se[s][:, e, c * HALF:(c + 1) * HALF], g.ident[:, :])
                last.then_inc(S["turned"][s], 1)

            pipeline(pe, make, turn)

        def dest(i, s, c):
            return g.se2_t[:, c, :, ds((W * i + s) * E2 * MEAN, E2 * MEAN)].rearrange(
                "p g (e m) -> p e g m", e=E2)

        def source(s, c):
            return g.ps[4 * s + 2 + c][0:HALF, :].rearrange("p (e g m) -> p e g m", e=E2, m=MEAN)

        @block.scalar
        def _(act):
            nc.scalar.preload_act_table_set(EXP_LN)

            def root(i, s):
                act.wait_ge(S["made"][s], i + 1)
                for e in range(E2):
                    act.wait_ge(S["squared"][s], E2 * i + e)
                    nc.scalar.activation(square[s][:, :],
                                         g.ps[4 * s + e // 2][:, (e % 2) * DIM:(e % 2 + 1) * DIM], ACT.Square,
                                         accum_out=ss[s][:, e:e + 1]).then_inc(S["squared"][s], 1)
                act.wait_ge(S["squared"][s], E2 * (i + 1))
                nc.scalar.activation(log_s[s][:, :], ss[s][:, :], ACT.Ln, scale=1.0 / DIM,
                                     bias=g.eps_dim[:, :]).then_inc(S["logged"][s], 1)
                act.wait_ge(S["logged"][s], i + 1)
                nc.scalar.activation(factor[s][:, :], log_s[s][:, :], ACT.Exp, scale=-0.5
                                     ).then_inc(S["rooted"][s], 1)

            def keep(i, s):
                act.wait_ge(S["turned"][s], i + 1)
                nc.scalar.nop(nofuse=True)
                nc.scalar.copy(dest(i, s, 1), source(s, 1)).then_inc(S["kept_s"][s], 1)

            pipeline(act, root, keep)

        @block.vector
        def _(dve):
            def norm(i, s):
                dve.wait_ge(S["rooted"][s], i + 1)
                nc.vector.tensor_tensor(
                    se[s][:, :, :].rearrange("p (b e) d -> p b e d", b=2),
                    g.psum[:, 4 * s:4 * s + 2, 0:2 * DIM].rearrange("p b (e d) -> p b e d", e=2),
                    factor[s][:, :].rearrange("p (b e) -> p b e", b=2).unsqueeze(3).broadcast_to(
                        (P, 2, 2, DIM)), ALU.mult).then_inc(S["normed"][s], 1)

            def keep(i, s):
                dve.wait_ge(S["turned"][s], i + 1)
                nc.vector.nop(nofuse=True)
                nc.vector.tensor_copy(dest(i, s, 0), source(s, 0)).then_inc(S["kept_v"][s], 1)

            pipeline(dve, norm, keep)


def second_dispatch(nc, g):
    with ExitStack() as ctx:
        def sb(name, shape, dt=F32):
            return [ctx.enter_context(nc.sbuf_tensor(f"sd_{name}{s}", shape, dt)) for s in range(W)]

        sem = lambda name: g.stage_semaphore(ctx, nc.semaphore("sd_" + name))
        yn = sb("yn", [P, GPS, DIM])
        yn_t = sb("yn_t", [HALF, 2, GPS * P])
        logits = sb("logits", [P, GPS, P])
        neg_row = sb("neg_row", [P, GPS])
        neg_col = sb("neg_col", [P, GPS])
        sum_row = sb("sum_row", [P, GPS])
        sum_col = sb("sum_col", [P, GPS])
        inv_row = sb("inv_row", [P, GPS])
        inv_col = sb("inv_col", [P, GPS])
        comb = sb("comb", [P, GPS, P])
        disp_t = sb("disp_t", [P, GPS, P])
        disp = sb("disp", [P, GPS, P])
        S = {n: sem(n) for n in (
            "fetched", "yn_turned", "yn_kept_s", "yn_kept_v", "logits_made", "masked", "row_maxed",
            "row_exped", "row_inverted", "combined", "logits_turned", "col_maxed", "col_exped",
            "col_inverted", "dispatched", "disp_turned", "disp_kept", "weights_made", "weights_kept",
            "inputs_made", "inputs_kept_s", "inputs_kept_v")}
        at = lambda i, s, per=1: (W * i + s + 1) * per
        block = ctx.enter_context(nc.Block())
        cols4 = lambda bank: bank.rearrange("p (g n) -> p g n", g=GPS)

        @block.tensor
        def _(pe):
            with pe.Fori(0, STEPS) as i:
                for s in range(W):
                    pe.wait_ge(S["fetched"], W * (i + 1))
                    pe.wait_ge(S["disp_kept"], W * i)
                    pe.wait_ge(S["weights_kept"], W * i)
                    for c in range(2):
                        for gr in range(GPS):
                            last = nc.tensor.transpose(g.ps[4 * s + c][0:HALF, gr * P:(gr + 1) * P],
                                                       yn[s][:, gr, c * HALF:(c + 1) * HALF], g.ident[:, :])
                    last.then_inc(S["yn_turned"], 1)
                for s in range(W):
                    pe.wait_ge(S["yn_kept_s"], at(i, s))
                    pe.wait_ge(S["yn_kept_v"], at(i, s))
                    pe.wait_ge(S["inputs_kept_v"], W * i)
                    pe.wait_ge(S["inputs_kept_s"], W * i)
                    for gr in range(GPS):
                        for c in range(2):
                            last = nc.tensor.matmul(
                                g.ps[4 * s + 2][:, gr * P:(gr + 1) * P], yn_t[s][:, c, gr * P:(gr + 1) * P],
                                g.se2_t[:, c, ds((W * i + s) * GPS + gr, 1), :].rearrange("p a n -> p (a n)"),
                                start=(c == 0), stop=(c == 1))
                    last.then_inc(S["logits_made"], 1)
                for s in range(W):
                    pe.wait_ge(S["masked"], at(i, s))
                    for gr in range(GPS):
                        last = nc.tensor.transpose(g.ps[4 * s + 3][:, gr * P:(gr + 1) * P], logits[s][:, gr, :],
                                                   g.ident[:, :])
                    last.then_inc(S["logits_turned"], 1)
                for s in range(W):
                    pe.wait_ge(S["combined"], at(i, s))
                    for gr in range(GPS):
                        last = nc.tensor.matmul(
                            g.ps[4 * s + 1][:, gr * GROUP:(gr + 1) * GROUP], comb[s][:, gr, :],
                            g.comb_t[:, ds((W * i + s) * SEQ + gr * GROUP, GROUP)], start=True, stop=True)
                    last.then_inc(S["weights_made"], 1)
                for s in range(W):
                    pe.wait_ge(S["dispatched"], at(i, s))
                    for gr in range(GPS):
                        last = nc.tensor.transpose(g.ps[4 * s][:, gr * P:(gr + 1) * P], disp_t[s][:, gr, :],
                                                   g.ident[:, :])
                    last.then_inc(S["disp_turned"], 1)
                for s in range(W):
                    pe.wait_ge(S["disp_kept"], at(i, s))
                    for c in range(2):
                        for gr in range(GPS):
                            last = nc.tensor.matmul(g.ps[4 * s + 2 + c][0:HALF, gr * P:(gr + 1) * P],
                                                    yn[s][:, gr, c * HALF:(c + 1) * HALF], disp[s][:, gr, :],
                                                    start=True, stop=True)
                    last.then_inc(S["inputs_made"], 1)

        def inputs(i, s, c):
            out = g.slots2_t[0:HALF, c, :, ds((W * i + s) * GPS * MEAN, GPS * MEAN)].rearrange(
                "p k (g m) -> p k g m", m=MEAN)
            return out, g.ps[4 * s + 2 + c][0:HALF, :].rearrange("p (g k m) -> p k g m", g=GPS, m=MEAN)

        @block.scalar
        def _(act):
            nc.scalar.preload_act_table_set(EXP_LN)
            with act.Fori(0, STEPS) as i:
                act.wait_ge(S["inputs_made"], W * i)
                nc.scalar.nop(nofuse=True)
                nc.scalar.copy(yn[0][:, :, :], g.yn[:, ds(W * i * GPS, GPS), :]).then_inc(S["fetched"], 1)
                for s in range(W):
                    act.wait_ge(S["yn_turned"], at(i, s))
                    nc.scalar.copy(yn_t[s][:, 0, :], g.ps[4 * s][0:HALF, :]).then_inc(S["yn_kept_s"], 1)
                for s in range(W):
                    act.wait_ge(S["row_maxed"], at(i, s))
                    for gr in range(GPS):
                        nc.scalar.activation(comb[s][:, gr, :], logits[s][:, gr, :], ACT.Exp,
                                             bias=neg_row[s][:, gr:gr + 1], accum_out=sum_row[s][:, gr:gr + 1]
                                             ).then_inc(S["row_exped"], 1)
                for s in range(W):
                    act.wait_ge(S["col_maxed"], at(i, s))
                    for gr in range(GPS):
                        nc.scalar.activation(disp_t[s][:, gr, :], g.ps[4 * s + 3][:, gr * P:(gr + 1) * P], ACT.Exp,
                                             bias=neg_col[s][:, gr:gr + 1], accum_out=sum_col[s][:, gr:gr + 1]
                                             ).then_inc(S["col_exped"], 1)
                for s in range(W):
                    act.wait_ge(S["disp_turned"], at(i, s))
                    nc.scalar.copy(disp[s][:, :, :], cols4(g.ps[4 * s])).then_inc(S["disp_kept"], 1)
                for s in range(W):
                    act.wait_ge(S["inputs_made"], at(i, s))
                    nc.scalar.nop(nofuse=True)
                    out, of = inputs(i, s, 1)
                    nc.scalar.copy(out, of).then_inc(S["inputs_kept_s"], 1)

        @block.vector
        def _(dve):
            nc.vector.memset(g.slots2_t[HALF:AUG, 1, :, :], 1.0).then_inc(g.input_ones, 1)
            with dve.Fori(0, STEPS) as i:
                dve.wait_ge(S["inputs_made"], W * i)
                nc.vector.nop(nofuse=True)
                nc.vector.tensor_copy(yn[1][:, :, :], g.yn[:, ds((W * i + 1) * GPS, GPS), :]
                                      ).then_inc(S["fetched"], 1)
                for s in range(W):
                    dve.wait_ge(S["yn_turned"], at(i, s))
                    nc.vector.tensor_copy(yn_t[s][:, 1, :], g.ps[4 * s + 1][0:HALF, :]
                                          ).then_inc(S["yn_kept_v"], 1)
                for s in range(W):
                    dve.wait_ge(S["logits_made"], at(i, s))
                    nc.vector.tensor_tensor(logits[s][:, :, :], cols4(g.ps[4 * s + 2]),
                                            g.block_mask[:, :].unsqueeze(1).broadcast_to((P, GPS, P)), ALU.add
                                            ).then_inc(S["masked"], 1)
                    dve.wait_ge(S["masked"], at(i, s))
                    nc.vector.tensor_reduce(neg_row[s][:, :], logits[s][:, :, :], AX.X, ALU.max, negate=True
                                            ).then_inc(S["row_maxed"], 1)
                for s in range(W):
                    dve.wait_ge(S["logits_turned"], at(i, s))
                    nc.vector.tensor_reduce(neg_col[s][:, :], cols4(g.ps[4 * s + 3]), AX.X, ALU.max, negate=True
                                            ).then_inc(S["col_maxed"], 1)
                for s in range(W):
                    dve.wait_ge(S["row_exped"], at(i, s, GPS))
                    nc.vector.reciprocal(inv_row[s][:, :], sum_row[s][:, :]).then_inc(S["row_inverted"], 1)
                    dve.wait_ge(S["row_inverted"], at(i, s))
                    nc.vector.tensor_tensor(comb[s][:, :, :], comb[s][:, :, :],
                                            inv_row[s][:, :].unsqueeze(2).broadcast_to((P, GPS, P)), ALU.mult
                                            ).then_inc(S["combined"], 1)
                for s in range(W):
                    dve.wait_ge(S["col_exped"], at(i, s, GPS))
                    nc.vector.reciprocal(inv_col[s][:, :], sum_col[s][:, :]).then_inc(S["col_inverted"], 1)
                    dve.wait_ge(S["col_inverted"], at(i, s))
                    nc.vector.tensor_tensor(disp_t[s][:, :, :], disp_t[s][:, :, :],
                                            inv_col[s][:, :].unsqueeze(2).broadcast_to((P, GPS, P)), ALU.mult
                                            ).then_inc(S["dispatched"], 1)
                for s in range(W):
                    dve.wait_ge(S["weights_made"], at(i, s))
                    nc.vector.nop(nofuse=True)
                    nc.vector.tensor_copy(g.mix_t[:, ds((W * i + s) * SEQ, SEQ)], g.ps[4 * s + 1][:, 0:SEQ]
                                          ).then_inc(S["weights_kept"], 1)
                for s in range(W):
                    dve.wait_ge(S["inputs_made"], at(i, s))
                    nc.vector.nop(nofuse=True)
                    out, of = inputs(i, s, 0)
                    nc.vector.tensor_copy(out, of).then_inc(S["inputs_kept_v"], 1)


def load_expert(sp, g, k, e):
    sp.dma_start(g.w1[e][:, :, :], g.d["w1"][ds(k, 1), e].rearrange("a p c n -> (a p) c n")
                 ).then_inc(g.w1_loaded[e], 16)
    sp.dma_start(g.w2[e][:, :, :], g.d["w2e"][ds(k, 1), e].rearrange("a p c n -> (a p) c n")
                 ).then_inc(g.w2_loaded[e], 16)


def experts(nc, g):
    HB = HID // P
    with ExitStack() as ctx:
        def sb(name, shape, dt=F32):
            return [ctx.enter_context(nc.sbuf_tensor(f"ex_{name}{u}", shape, dt)) for u in range(2)]

        sem = lambda name: g.stage_semaphore(ctx, nc.semaphore("ex_" + name))
        gelu = sb("gelu", [P, HID])
        act_t = sb("act_t", [P, HID])
        rows = sb("rows", [P, DIM])
        S = {n: sem(n) for n in ("gates", "values", "gelued", "acted", "made", "kept")}
        written = [sem(f"written{e}") for e in range(E2)]
        gathered = sem("gathered")
        block = ctx.enter_context(nc.Block())
        gate_bank, value_bank, out_bank = (lambda e: g.ps[4 * (e % 2)], lambda e: g.ps[4 * (e % 2) + 1],
                                           lambda e: g.ps[4 * (e % 2) + 2])

        @block.sync
        def _(sp):
            for e in range(E2):
                load_expert(sp, g, 0, e)
            with sp.Fori(1, E1) as k:
                for e in range(E2):
                    sp.wait_ge(S["values"], E2 * (k - 1) + e + 1)
                    sp.wait_ge(S["made"], E2 * (k - 1) + e + 1)
                    load_expert(sp, g, k, e)

        @block.tensor
        def _(pe):
            pe.wait_ge(g.input_ones, 1)

            def hidden(k, e):
                n = E2 * k + e
                pe.wait_ge(g.w1_loaded[e], 16 * (k + 1))
                x = lambda c: g.slots2_t[0:HALF + c, c, ds(n, 1), :].rearrange("p a n -> p (a n)")
                for bank, first, done, free in ((gate_bank(e), HID, "gates", "gelued"),
                                                (value_bank(e), 0, "values", "acted")):
                    if e >= 2:
                        pe.wait_ge(S[free], n - 1)
                    else:
                        pe.wait_ge(S[free], E2 * k)
                    for j in range(HB):
                        for c in range(2):
                            last = nc.tensor.matmul(
                                bank[:, j * P:(j + 1) * P],
                                g.w1[e][0:HALF + c, c, first + j * P:first + (j + 1) * P], x(c),
                                start=(c == 0), stop=(c == 1))
                    last.then_inc(S[done], 1)

            def output(k, e):
                n = E2 * k + e
                pe.wait_ge(S["acted"], n + 1)
                pe.wait_ge(g.w2_loaded[e], 16 * (k + 1))
                if e >= 2:
                    pe.wait_ge(S["kept"], n - 1)
                else:
                    pe.wait_ge(S["kept"], E2 * k)
                for j in range(HB):
                    last = nc.tensor.matmul(out_bank(e)[:, 0:DIM], act_t[e % 2][:, j * P:(j + 1) * P],
                                            g.w2[e][:, j, :], start=(j == 0), stop=(j == HB - 1))
                last.then_inc(S["made"], 1)

            with pe.Fori(0, E1) as k:
                hidden(k, 0)
                for e in range(1, E2):
                    hidden(k, e)
                    output(k, e - 1)
                output(k, E2 - 1)

        @block.scalar
        def _(act):
            def gate(k, e):
                n = E2 * k + e
                act.wait_ge(S["gates"], n + 1)
                if e >= 2:
                    act.wait_ge(S["acted"], n - 1)
                else:
                    act.wait_ge(S["acted"], E2 * k)
                nc.scalar.activation(gelu[e % 2][:, :], gate_bank(e)[:, :], ACT.Gelu_apprx_tanh
                                     ).then_inc(S["gelued"], 1)

            def keep(k, e):
                n = E2 * k + e
                act.wait_ge(S["made"], n + 1)
                if e >= 2:
                    act.wait_ge(written[e - 2], 16 * (k + 1))
                else:
                    act.wait_ge(written[e + 2], 16 * k)
                nc.scalar.copy(rows[e % 2][:, :], out_bank(e)[:, 0:DIM]).then_inc(S["kept"], 1)
                act.wait_ge(S["kept"], n + 1)
                act.dma_start(g.scratch[ds(k, 1), e].rearrange("a p n -> (a p) n"), rows[e % 2][:, :]
                              ).then_inc(written[e], 16)

            with act.Fori(0, E1) as k:
                gate(k, 0)
                for e in range(1, E2):
                    gate(k, e)
                    keep(k, e - 1)
                keep(k, E2 - 1)

        @block.vector
        def _(dve):
            with dve.Fori(0, E1) as k:
                for e in range(E2):
                    n = E2 * k + e
                    dve.wait_ge(S["gelued"], n + 1)
                    dve.wait_ge(S["values"], n + 1)
                    if e >= 2:
                        dve.wait_ge(S["made"], n - 1)
                    else:
                        dve.wait_ge(S["made"], E2 * k)
                    nc.vector.tensor_tensor(act_t[e % 2][:, :], value_bank(e)[:, :], gelu[e % 2][:, :], ALU.mult
                                            ).then_inc(S["acted"], 1)

        @block.gpsimd
        def _(pool):
            for k in range(E1):
                for e in range(E2):
                    p0 = (k * E2 + e) * MEAN
                    pool.wait_ge(written[e], 16 * (k + 1))
                    pool.dma_start(g.yn[p0:p0 + MEAN, :, :],
                                   g.scratch[k, e].rearrange("(g m) d -> m g d", m=MEAN)).then_inc(gathered, 16)
            pool.wait_ge(gathered, 16 * E1 * E2)


def combine(nc, g):
    with ExitStack() as ctx:
        def sb(name, shape, dt=F32):
            return [ctx.enter_context(nc.sbuf_tensor(f"co_{name}{s}", shape, dt)) for s in range(W)]

        sem = lambda name: g.stage_semaphore(ctx, nc.semaphore("co_" + name))
        rows = sb("rows", [P, GPS, DIM])
        mix = sb("mix", [P, SEQ])
        final = sb("final", [P, TPS, DIM])
        S = {n: sem(n) for n in ("biased", "fetched", "mixed", "added")}
        stored = [sem(f"stored{s}") for s in range(W)]
        at = lambda i, s, per=1: (W * i + s + 1) * per
        block = ctx.enter_context(nc.Block())

        @block.vector
        def _(dve):
            with dve.Fori(0, STEPS) as i:
                for s in range(W):
                    dve.wait_ge(S["mixed"], W * i)
                    nc.vector.tensor_tensor(rows[s][:, :, :], g.yn[:, ds((W * i + s) * GPS, GPS), :],
                                            g.t["b2"].unsqueeze(1).broadcast_to((P, GPS, DIM)), ALU.add
                                            ).then_inc(S["biased"], 1)
                for s in range(W):
                    dve.wait_ge(stored[s], 16 * i)
                    dve.wait_ge(S["mixed"], at(i, s))
                    nc.vector.tensor_tensor(final[s][:, :, :], g.h[:, ds((W * i + s) * TPS, TPS), :],
                                            g.ps[s][:, 0:TPS * DIM].rearrange("p (t d) -> p t d", t=TPS), ALU.add
                                            ).then_inc(S["added"], 1)

        @block.scalar
        def _(act):
            with act.Fori(0, STEPS) as i:
                for s in range(W):
                    act.wait_ge(S["mixed"], W * i)
                    nc.scalar.nop(nofuse=True)
                    nc.scalar.copy(mix[s][:, :], g.mix_t[:, ds((W * i + s) * SEQ, SEQ)]).then_inc(S["fetched"], 1)

        @block.tensor
        def _(pe):
            with pe.Fori(0, STEPS) as i:
                for s in range(W):
                    pe.wait_ge(S["biased"], at(i, s))
                    pe.wait_ge(S["fetched"], at(i, s))
                    pe.wait_ge(S["added"], W * i)
                    for gr in range(GPS):
                        r0, t = GROUP * (gr % 2), gr // 2
                        last = nc.tensor.matmul(g.ps[s][r0:r0 + GROUP, t * DIM:(t + 1) * DIM],
                                                mix[s][:, gr * GROUP:(gr + 1) * GROUP], rows[s][:, gr, :],
                                                start=True, stop=True)
                    last.then_inc(S["mixed"], 1)

        @block.sync
        def _(sp):
            with sp.Fori(0, STEPS) as i:
                for s in range(W):
                    sp.wait_ge(S["added"], at(i, s))
                    sp.dma_start(g.out[:, ds((W * i + s) * TPS, TPS), :], final[s][:, :, :]
                                 ).then_inc(stored[s], 16)
            for s in range(W):
                sp.wait_ge(stored[s], 16 * STEPS)


def tower(nc, d, out):
    g = Shared()
    g.d, g.out = d, out
    with ExitStack() as ctx:
        sb = lambda name, shape, dt=F32: ctx.enter_context(nc.sbuf_tensor(name, shape, dt))
        sem = lambda name: ctx.enter_context(nc.semaphore(name))
        g.psum = ctx.enter_context(nc.psum_tensor("banks", [P, 8, 512], F32))
        g.ps = [g.psum[:, n, :] for n in range(8)]
        g.h = sb("h", [P, TILES, DIM])
        g.ident = sb("ident", [P, P])
        g.average = sb("average", [P, P // MEAN])
        g.block_mask = sb("block_mask", [P, P])
        g.eps5, g.eps6, g.rms_eps, g.eps_norms, g.eps_dim = (
            sb(name, [P, 1]) for name in ("eps5", "eps6", "rms_eps", "eps_norms", "eps_dim"))
        g.phi_t = sb("phi_t", [HALF, 2, P])
        g.w1 = [sb(f"w1_{e}", [AUG, 2, 2 * HID]) for e in range(E2)]
        g.w2 = [sb(f"w2_{e}", [P, HID // P, DIM]) for e in range(E2)]
        g.w1_loaded = [sem(f"w1_loaded{e}") for e in range(E2)]
        g.w2_loaded = [sem(f"w2_loaded{e}") for e in range(E2)]
        g.scratch = nc.dram_tensor("rows_scratch", (E1, E2, P, DIM), F32, kind="Internal").ap()
        g.ids_loaded, g.gathered, g.operands_loaded = sem("ids_loaded"), sem("gathered"), sem("operands_loaded")
        g.ident_made, g.masks_made, g.consts_set = sem("ident_made"), sem("masks_made"), sem("consts_set")
        g.folds_ready, g.ones_set, g.input_ones = sem("folds_ready"), sem("ones_set"), sem("input_ones")

        def operands(scope, names):
            for n in names:
                g.t[n] = scope.enter_context(nc.sbuf_tensor(n + "_sb", list(d[n].shape), F32))[
                    tuple(slice(None) for _ in d[n].shape)]

        operands(ctx, MOE_OPERANDS)
        with ExitStack() as front:
            fsb = lambda name, shape, dt=F32: front.enter_context(nc.sbuf_tensor(name, shape, dt))
            operands(front, FRONT_OPERANDS)
            g.ids = fsb("ids", [P, TILES], U32)
            g.mean_all = fsb("mean_all", [P, P])
            g.xt = [fsb(f"xt{s}", [AUG, 2, SEQ]) for s in range(WIDE)]
            g.qk_fold = fsb("qk_fold", [AUG, 2, DIM + 1])
            g.vo_fold = fsb("vo_fold", [AUG, 2, DIM])
            g.mlp_fold = fsb("mlp_fold", [AUG, 2, DIM])
            fold_weights(nc, g)
            token_mixer(nc, g)
            attention(nc, g)
        clear_spent(nc, g)
        g.yn = sb("yn_all", [P, NGROUPS, DIM])
        g.comb_t = sb("comb_t", [P, BATCH * SEQ])
        g.means_t = sb("means_t", [HALF, 2, E1, NGROUPS, MEAN])
        first_slots(nc, g)
        g.slots2_t = sb("slots2_t", [AUG, 2, E1 * E2, NGROUPS * MEAN])
        g.mix_t = sb("mix_t", [P, BATCH * SEQ])
        with ExitStack() as second:
            g.se2_t = second.enter_context(nc.sbuf_tensor("se2_t", [HALF, 2, NGROUPS, P], F32))
            second_slots(nc, g)
            second_dispatch(nc, g)
        experts(nc, g)
        combine(nc, g)


def layouts(inputs):
    f = lambda n: np.asarray(inputs[n])
    cat, c = np.concatenate, np.ascontiguousarray

    def halves(w):
        return c(cat([w[:DIM].reshape(2, HALF, -1), np.stack([w[DIM:], w[DIM:]])], 1).transpose(1, 0, 2))

    def hidden(w, b):
        return c(cat([w, b[None]], 0).T.reshape(HC, P, DIM + 1).transpose(1, 0, 2))

    def hid_rows(w):
        return c(w.reshape(HC, P, DIM).transpose(1, 0, 2))

    def seq_tiles(w):
        return c(w.reshape(TPS, P, DIM).transpose(1, 0, 2))

    d = {
        "ids": c(f("x").reshape(TILES, P).T).view(np.uint32),
        "emb": c(f("L0_tok_emb")),
        "wq_t": hidden(f("L0_tok_Wq"), f("L0_tok_bq")),
        "wk_t": hidden(f("L0_tok_Wk"), f("L0_tok_bk")),
        "wv_t": hidden(f("L0_tok_Wv"), f("L0_tok_bv")),
        "w1_t": hidden(f("L0_tok_W1"), f("L0_tok_b1")),
        "wo": hid_rows(f("L0_tok_Wo")),
        "w2": hid_rows(f("L0_tok_W2")),
        "tail_bias": c(np.stack([f("L0_tok_bo"), f("L0_tok_b2")])[None]),
        "ln_w1": seq_tiles(f("L0_tok_ln1_w")), "ln_b1": seq_tiles(f("L0_tok_ln1_b")),
        "ln_w2": seq_tiles(f("L0_tok_ln2_w")), "ln_b2": seq_tiles(f("L0_tok_ln2_b")),
        "pos": seq_tiles(pos_encoding()),
        "qkv_t": halves(cat([f("L0_attn_qkv_w").T, f("L0_attn_qkv_b")[None]], 0)),
        "proj_t": halves(cat([f("L0_attn_proj_w").T, f("L0_attn_proj_b")[None]], 0)),
        "qk_weights": c(np.broadcast_to(np.stack([f("L0_attn_q_norm_w"), f("L0_attn_k_norm_w")]), (P, 2, HDIM))),
        "gamma_in": c(np.broadcast_to(f("L0_ffn_gamma_in"), (P, DIM))),
        "slots1": c(f("L0_ffn_slots1").reshape(P, DIM)),
        "gamma2": c(np.repeat(f("L0_ffn_gamma2"), S1, 0)),
        "b2": c(np.repeat(f("L0_ffn_b2").reshape(E1 * E2, DIM), MEAN, 0)),
        "w_slot2": c(f("L0_ffn_w_slot2").reshape(E1, 2, HALF, E2 * DIM).transpose(0, 2, 1, 3)),
        "w1": c(cat([f("L0_ffn_w1").reshape(E1, E2, 2, HALF, 2 * HID),
                     np.broadcast_to(f("L0_ffn_b1")[:, :, None, None, :], (E1, E2, 2, 1, 2 * HID))], 3
                    ).transpose(0, 1, 3, 2, 4)),
        "w2e": c(f("L0_ffn_w2").reshape(E1, E2, HID // P, P, DIM).transpose(0, 1, 3, 2, 4)),
    }
    return d


def kernel(**inputs):
    from concourse import bacc
    from concourse.bass_utils import run_bass_kernel_spmd

    nc = bacc.Bacc("TRN2", target_bir_lowering=False, num_devices=1)
    arrays = layouts(inputs)
    d = {n: nc.dram_tensor("in_" + n, a.shape, mybir.dt.from_np(a.dtype), kind="ExternalInput").ap()
         for n, a in arrays.items()}
    out = nc.dram_tensor("out", (P, TILES, DIM), F32, kind="ExternalOutput").ap()
    tower(nc, d, out)
    r = run_bass_kernel_spmd(nc, [{"in_" + n: a for n, a in arrays.items()}], core_ids=[0])
    got = r.results[0]["out"]
    return np.ascontiguousarray(got.transpose(1, 0, 2)).reshape(BATCH, SEQ, DIM)
```

```python
from contextlib import ExitStack

import numpy as np

import concourse.bass as bass
from concourse import mybir

ALU = mybir.AluOpType
ACT = mybir.ActivationFunctionType
AX = mybir.AxisListType
F32 = mybir.dt.float32
BF16 = mybir.dt.bfloat16
U32 = mybir.dt.uint32

P = 128
BATCH, SEQ, DIM = 8, 256, 192
HALF = DIM // 2
AUG = HALF + 1
TILES = BATCH * SEQ // P
TPS = SEQ // P
TOK_HID = 768
HC = TOK_HID // P
HEADS, HDIM = 12, 16
QUADS, QH = 3, 4
PARTS = 6
KS = PARTS * HDIM
KM = KS + 2 * QH
SUM = HDIM
GROUP = 64
GPS = SEQ // GROUP
NGROUPS = BATCH * GPS
E1, S1, E2 = 8, 16, 4
MEAN = 4
HID = 512
SLOTS = E1 * S1
W = 2
WIDE = 4
STEPS = BATCH // W
ROOT = float(DIM) ** 0.5
MASKED = -1.0e30
FRONT_OPERANDS = ("qkv_t", "proj_t", "ln_w1", "ln_b1", "ln_w2", "ln_b2", "pos", "qk_weights")
MOE_OPERANDS = ("gamma_in", "gamma2", "b2")
N_OPERANDS = len(FRONT_OPERANDS) + len(MOE_OPERANDS)
ds = bass.ds
EXP_LN = "natural_log_exp_and_others"


def pos_encoding():
    pos = np.arange(SEQ, dtype=np.float32)[:, None]
    i = np.arange(DIM, dtype=np.float32)[None, :]
    ang = pos / np.power(np.float32(10000.0), i / np.float32(DIM))
    return np.where((np.arange(DIM) % 2 == 0)[None, :], np.sin(ang), np.cos(ang)).astype(np.float32)


class Shared:

    def __init__(self):
        self.t = {}
        self.own, self.before = [], []
        self.own_scope, self.before_scope = ExitStack(), ExitStack()

    def next_stage(self):
        self.before_scope.close()
        self.before, self.before_scope = self.own, self.own_scope
        self.own, self.own_scope = [], ExitStack()

    def stage_semaphore(self, semaphore):
        s = self.own_scope.enter_context(semaphore)
        self.own.append(s)
        return s

    def clear_before(self, sp):
        for s in self.before:
            sp.sem_clear(s)


def fold_weights(nc, g):
    g.next_stage()
    with ExitStack() as ctx:
        sb = lambda name, shape, dt=F32: ctx.enter_context(nc.sbuf_tensor(name, shape, dt))
        sem = lambda name: g.stage_semaphore(nc.semaphore(name))
        wq_t = sb("wq_t", [P, HC, DIM + 1])
        wk_t = sb("wk_t", [P, HC, DIM + 1])
        wv_t = sb("wv_t", [P, HC, DIM + 1])
        w1_t = sb("w1_t", [P, HC, DIM + 1])
        wo = sb("wo", [P, HC, DIM])
        w2 = sb("w2", [P, HC, DIM])
        tail_bias = sb("tail_bias", [1, 2, DIM])
        last_row = sb("last_row", [1, AUG])
        slots_raw = sb("slots_raw", [P, DIM])
        slots_sq = sb("slots_sq", [P, DIM])
        slots_ss = sb("slots_ss", [P, 1])
        slots_ln = sb("slots_ln", [P, 1])
        slots_rn = sb("slots_rn", [P, 1])
        loaded_qk = sem("loaded_qk")
        loaded_v = sem("loaded_v")
        loaded_1 = sem("loaded_1")
        loaded_bias = sem("loaded_bias")
        loaded_slots = sem("loaded_slots")
        zeroed = sem("zeroed")
        row_set = sem("row_set")
        folded = sem("folded")
        slots_squared = sem("slots_squared")
        slots_logged = sem("slots_logged")
        slots_rooted = sem("slots_rooted")
        slots_normed = sem("slots_normed")
        slots_turned = sem("slots_turned")
        ident_zeroed = sem("ident_zeroed")
        masks_zeroed = sem("masks_zeroed")
        block = ctx.enter_context(nc.Block())

        @block.sync
        def _(sp):
            sp.dma_start(wq_t[:, :, :], g.d["wq_t"]).then_inc(loaded_qk, 16)
            sp.dma_start(wv_t[:, :, :], g.d["wv_t"]).then_inc(loaded_v, 16)
            sp.dma_start(w1_t[:, :, :], g.d["w1_t"]).then_inc(loaded_1, 16)
            sp.dma_start(tail_bias[:, :, :], g.d["tail_bias"]).then_inc(loaded_bias, 16)
            for name in FRONT_OPERANDS + MOE_OPERANDS:
                sp.dma_start(g.t[name], g.d[name]).then_inc(g.operands_loaded, 16)
            sp.wait_ge(g.operands_loaded, 16 * N_OPERANDS)

        @block.gpsimd
        def _(pool):
            pool.dma_start(g.ids[:, :], g.d["ids"]).then_inc(g.ids_loaded, 16)
            pool.wait_ge(g.ids_loaded, 16)
            for t in range(TILES):
                pool.indirect_dma_start(g.h[:, t, :], None, g.d["emb"],
                                        bass.IndirectOffsetOnAxis(ap=g.ids[:, t:t + 1], axis=0)
                                        ).then_inc(g.gathered, 16)
            nc.gpsimd.memset(g.ident[:, :], 0.0).then_inc(ident_zeroed, 1)
            nc.gpsimd.memset(g.average[:, :], 1.0 / MEAN).then_inc(masks_zeroed, 1)
            nc.gpsimd.memset(g.block_mask[:, :], 0.0).then_inc(masks_zeroed, 1)
            pool.wait_ge(ident_zeroed, 1)
            nc.gpsimd.affine_select(out=g.ident[:, :], in_=g.ident[:, :], compare_op=ALU.not_equal, fill=1.0,
                                    base=0, pattern=[[-1, P]], channel_multiplier=1).then_inc(g.ident_made, 1)
            pool.wait_ge(masks_zeroed, 2)
            nc.gpsimd.affine_select(out=g.average[:, :], in_=g.average[:, :], compare_op=ALU.is_ge, fill=0.0,
                                    base=0, pattern=[[-MEAN, P // MEAN]], channel_multiplier=1
                                    ).then_inc(masks_zeroed, 1)
            nc.gpsimd.affine_select(out=g.block_mask[:, :], in_=g.block_mask[:, :], compare_op=ALU.is_ge,
                                    fill=MASKED, base=0, pattern=[[-S1, E1], [0, S1]], channel_multiplier=1
                                    ).then_inc(masks_zeroed, 1)
            pool.wait_ge(masks_zeroed, 4)
            nc.gpsimd.affine_select(out=g.average[:, :], in_=g.average[:, :], compare_op=ALU.is_ge, fill=0.0,
                                    base=MEAN - 1, pattern=[[MEAN, P // MEAN]], channel_multiplier=-1
                                    ).then_inc(g.masks_made, 1)
            nc.gpsimd.affine_select(out=g.block_mask[:, :], in_=g.block_mask[:, :], compare_op=ALU.is_ge,
                                    fill=MASKED, base=S1 - 1, pattern=[[S1, E1], [0, S1]],
                                    channel_multiplier=-1).then_inc(g.masks_made, 1)

        @block.scalar
        def _(act):
            act.dma_start(wk_t[:, :, :], g.d["wk_t"]).then_inc(loaded_qk, 16)
            act.dma_start(wo[:, :, :], g.d["wo"]).then_inc(loaded_v, 16)
            act.dma_start(w2[:, :, :], g.d["w2"]).then_inc(loaded_1, 16)
            act.dma_start(slots_raw[:, :], g.d["slots1"]).then_inc(loaded_slots, 16)
            nc.scalar.preload_act_table_set(EXP_LN)
            act.wait_ge(loaded_slots, 16)
            nc.scalar.activation(slots_sq[:, :], slots_raw[:, :], ACT.Square,
                                 accum_out=slots_ss[:, :]).then_inc(slots_squared, 1)
            act.wait_ge(slots_squared, 1)
            act.wait_ge(g.consts_set, 1)
            nc.scalar.activation(slots_ln[:, :], slots_ss[:, :], ACT.Ln, bias=g.eps6[:, :]
                                 ).then_inc(slots_logged, 1)
            act.wait_ge(slots_logged, 1)
            nc.scalar.activation(slots_rn[:, :], slots_ln[:, :], ACT.Exp, scale=-0.5).then_inc(slots_rooted, 1)

        @block.tensor
        def _(pe):
            pe.wait_ge(loaded_qk, 32)
            for c in range(2):
                for j in range(HC):
                    last = nc.tensor.matmul(g.ps[c][0:AUG, 0:DIM + 1], wk_t[:, j, c * HALF:c * HALF + AUG],
                                            wq_t[:, j, :], start=(j == 0), stop=(j == HC - 1))
                last.then_inc(folded, 1)
            pe.wait_ge(zeroed, 1)
            pe.wait_ge(row_set, 1)
            pe.wait_ge(loaded_bias, 16)
            for n, (lhs, rhs, loaded) in enumerate(((wv_t, wo, loaded_v), (w1_t, w2, loaded_1))):
                pe.wait_ge(loaded, 32)
                for c in range(2):
                    bank = g.ps[2 + 2 * n + c]
                    for j in range(HC):
                        last = nc.tensor.matmul(bank[0:AUG, 0:DIM], lhs[:, j, c * HALF:c * HALF + AUG],
                                                rhs[:, j, :], start=(j == 0), stop=(c == 0 and j == HC - 1))
                    if c == 1:
                        last = nc.tensor.matmul(bank[0:AUG, 0:DIM], last_row[:, :], tail_bias[:, n, :],
                                                start=False, stop=True)
                    last.then_inc(folded, 1)
            pe.wait_ge(slots_normed, 1)
            pe.wait_ge(g.ident_made, 1)
            for c in range(2):
                last = nc.tensor.transpose(g.ps[6][0:HALF, c * P:(c + 1) * P],
                                           slots_raw[:, c * HALF:(c + 1) * HALF], g.ident[:, :])
            last.then_inc(slots_turned, 1)

        @block.vector
        def _(dve):
            nc.vector.memset(g.eps6[:, :], 1e-6)
            nc.vector.memset(g.eps5[:, :], 1e-5)
            nc.vector.memset(g.eps_norms[:, :], 1e-11 / DIM)
            nc.vector.memset(g.eps_dim[:, :], 1e-6 / DIM)
            nc.vector.memset(g.rms_eps[:, :], 1e-6).then_inc(g.consts_set, 1)
            nc.vector.memset(last_row[:, :], 0.0).then_inc(zeroed, 1)
            nc.vector.memset(g.mean_all[:, :], 1.0 / P).then_inc(g.consts_set, 1)
            dve.wait_ge(zeroed, 1)
            nc.vector.memset(last_row[:, HALF:AUG], 1.0).then_inc(row_set, 1)
            for s in range(WIDE):
                nc.vector.memset(g.xt[s][HALF:AUG, :, :], 1.0).then_inc(g.ones_set, 1)
            for n, fold in enumerate((g.qk_fold, g.vo_fold, g.mlp_fold)):
                for c in range(2):
                    dve.wait_ge(folded, 2 * n + c + 1)
                    nc.vector.tensor_copy(fold[:, c, :], g.ps[2 * n + c][0:AUG, 0:fold.shape[2]]
                                          ).then_inc(g.folds_ready, 1)
            dve.wait_ge(slots_rooted, 1)
            nc.vector.tensor_scalar(slots_raw[:, :], slots_raw[:, :], slots_rn[:, :], ROOT, ALU.mult, ALU.mult
                                    ).then_inc(slots_normed, 1)
            dve.wait_ge(slots_turned, 1)
            nc.vector.tensor_copy(g.phi_t[:, :, :], g.ps[6][0:HALF, 0:2 * P].rearrange("p (c n) -> p c n", c=2)
                                  ).then_inc(g.folds_ready, 1)


def token_mixer(nc, g):
    g.next_stage()
    with ExitStack() as ctx:
        def sb(name, shape, dt=F32):
            return [ctx.enter_context(nc.sbuf_tensor(f"{name}{s}", shape, dt)) for s in range(WIDE)]

        sem = lambda name: g.stage_semaphore(nc.semaphore(name))
        y = sb("y", [P, TPS, DIM])
        key_t = sb("key_t", [AUG, 2, SEQ])
        value = sb("value", [P, TPS, DIM])
        prob = sb("prob", [P, TPS, SEQ])
        prob_t = sb("prob_t", [P, TPS, SEQ])
        neg_max = sb("neg_max", [P, TPS])
        row_sum = sb("row_sum", [P, TPS])
        inv_sum = sb("inv_sum", [P, TPS])
        f_out = sb("f_out", [P, TPS, DIM])
        bn = sb("bn", [P, TPS, 6])
        one = lambda name, shape: ctx.enter_context(nc.sbuf_tensor(name, shape, F32))
        stat = one("stat", [P, WIDE, 2])
        mean_sq = one("mean_sq", [P, WIDE])
        neg_var = one("neg_var", [P, WIDE])
        log_var = one("log_var", [P, WIDE])
        rstd = one("rstd", [P, WIDE])
        tok = {n: sem("tok_" + n) for n in (
            "placed", "turned", "turned_kept", "keys", "keys_kept", "values", "values_kept", "scores",
            "maxed", "exped", "inverted", "probs_turned", "probs_kept", "mixed", "added", "stats1",
            "stats2", "squared", "stats3", "stats_summed", "stats_kept", "var_ready", "logged", "rooted",
            "weighted", "normed", "fed", "gelued", "weight_made", "preset",
            "picks_set")}

        def at(i, s, per=1, n=1):
            return (WIDE * i + s) * per + n

        def nth(i, s, which):
            return WIDE * (2 * i + which) + s + 1

        def norms(i, which):
            return 2 * i + which + 1

        STAT_BANK = g.ps[0]
        block = ctx.enter_context(nc.Block())

        def norm_stats_pe(pe, i, which):
            pe.wait_ge(tok["stats3"], norms(i, which))
            nc.tensor.matmul(STAT_BANK[:, 0:2 * WIDE], g.mean_all[:, :],
                             stat[:, :, :].rearrange("p s k -> p (s k)"), start=True, stop=True
                             ).then_inc(tok["stats_summed"], 1)

        @block.sync
        def _(sp):
            g.clear_before(sp)

        @block.gpsimd
        def _(pool):
            pool.wait_ge(g.operands_loaded, 16 * N_OPERANDS)
            nc.gpsimd.tensor_copy(g.ident_b[:, :], g.ident[:, :])
            nc.gpsimd.tensor_tensor(g.qk_weight[:, :], g.t["qk_weights"][:, 0, :], g.t["qk_weights"][:, 1, :],
                                    ALU.mult).then_inc(tok["weight_made"], 1)
            pool.wait_ge(tok["weight_made"], 1)
            nc.gpsimd.tensor_scalar(g.qk_weight[:, :], g.qk_weight[:, :], float(HDIM) ** -0.5, None, ALU.mult
                                    ).then_inc(tok["weight_made"], 1)
            for s in range(2):
                nc.gpsimd.memset(g.val[s][:, :, :, HDIM:], 0.0).then_inc(tok["preset"], 1)
            pool.wait_ge(tok["preset"], 2)
            for s in range(2):
                nc.gpsimd.memset(g.val[s][:, :, :, SUM:SUM + 1], 1.0).then_inc(tok["preset"], 1)
            pool.wait_ge(tok["preset"], 4)
            for s in range(2):
                nc.gpsimd.memset(g.k_t[s][KS:KM, :, :], 0.0).then_inc(tok["preset"], 1)
            pool.wait_ge(tok["preset"], 6)
            for r in range(2):
                for s in range(2):
                    rows = g.k_t[s][KS:KM, :, :].rearrange("p (q h) n -> p q h n", h=QH)
                    nc.gpsimd.affine_select(out=rows, in_=rows, compare_op=ALU.not_equal, fill=1.0,
                                            base=-QH * r, pattern=[[0, QUADS], [-1, QH], [0, SEQ]],
                                            channel_multiplier=1).then_inc(tok["picks_set"], 1)
                pool.wait_ge(tok["picks_set"], 2 + 2 * r)

        @block.tensor
        def _(pe):
            pe.wait_ge(g.consts_set, 2)
            with pe.Fori(0, BATCH // WIDE) as i:
                for s in range(WIDE):
                    pe.wait_ge(tok["placed"], at(i, s))
                    for c in range(2):
                        for t in range(TPS):
                            last = nc.tensor.transpose(
                                g.ps[2 * s][0:HALF, c * SEQ + t * P:c * SEQ + (t + 1) * P],
                                y[s][:, t, c * HALF:(c + 1) * HALF], g.ident[:, :])
                    last.then_inc(tok["turned"], 1)
                for s in range(WIDE):
                    pe.wait_ge(tok["turned_kept"], nth(i, s, 0))
                    for a in range(2):
                        for c in range(2):
                            k = HALF + c
                            last = nc.tensor.matmul(
                                g.ps[2 * s + 1][0:AUG, a * SEQ:(a + 1) * SEQ],
                                g.qk_fold[0:k, c, a * HALF:a * HALF + AUG], g.xt[s][0:k, c, :],
                                start=(c == 0), stop=(c == 1))
                    last.then_inc(tok["keys"], 1)
                for s in range(WIDE):
                    for t in range(TPS):
                        for c in range(2):
                            k = HALF + c
                            last = nc.tensor.matmul(
                                g.ps[2 * s][:, t * DIM:(t + 1) * DIM], g.xt[s][0:k, c, t * P:(t + 1) * P],
                                g.vo_fold[0:k, c, :], start=(c == 0), stop=(c == 1))
                    last.then_inc(tok["values"], 1)
                for s in range(WIDE):
                    pe.wait_ge(tok["keys_kept"], at(i, s))
                    for t in range(TPS):
                        for c in range(2):
                            k = HALF + c
                            last = nc.tensor.matmul(
                                g.ps[2 * s + 1][:, t * SEQ:(t + 1) * SEQ], g.xt[s][0:k, c, t * P:(t + 1) * P],
                                key_t[s][0:k, c, :], start=(c == 0), stop=(c == 1))
                    last.then_inc(tok["scores"], 1)
                for s in range(WIDE):
                    pe.wait_ge(tok["exped"], at(i, s, 2, 2))
                    pe.wait_ge(tok["values_kept"], at(i, s))
                    for m in range(TPS):
                        for t in range(TPS):
                            last = nc.tensor.transpose(
                                g.ps[2 * s][:, m * SEQ + t * P:m * SEQ + (t + 1) * P],
                                prob[s][:, t, m * P:(m + 1) * P], g.ident[:, :])
                    last.then_inc(tok["probs_turned"], 1)
                for s in range(WIDE):
                    pe.wait_ge(tok["probs_kept"], at(i, s))
                    for t in range(TPS):
                        for m in range(TPS):
                            last = nc.tensor.matmul(
                                g.ps[2 * s + 1][:, t * DIM:(t + 1) * DIM], prob_t[s][:, m, t * P:(t + 1) * P],
                                value[s][:, m, :], start=(m == 0), stop=(m == TPS - 1))
                    last.then_inc(tok["mixed"], 1)
                norm_stats_pe(pe, i, 0)
                for s in range(WIDE):
                    pe.wait_ge(tok["normed"], nth(i, s, 0))
                    for c in range(2):
                        for t in range(TPS):
                            last = nc.tensor.transpose(
                                g.ps[2 * s + 1][0:HALF, c * SEQ + t * P:c * SEQ + (t + 1) * P],
                                y[s][:, t, c * HALF:(c + 1) * HALF], g.ident[:, :])
                    last.then_inc(tok["turned"], 1)
                for s in range(WIDE):
                    pe.wait_ge(tok["turned_kept"], nth(i, s, 1))
                    for t in range(TPS):
                        for c in range(2):
                            k = HALF + c
                            last = nc.tensor.matmul(
                                g.ps[2 * s][:, t * DIM:(t + 1) * DIM], g.xt[s][0:k, c, t * P:(t + 1) * P],
                                g.mlp_fold[0:k, c, :], start=(c == 0), stop=(c == 1))
                    last.then_inc(tok["fed"], 1)
                norm_stats_pe(pe, i, 1)

        @block.scalar
        def _(act):
            act.wait_ge(g.consts_set, 2)

            def turned_copy(i, s, which, bank):
                act.wait_ge(tok["turned"], nth(i, s, which))
                nc.scalar.copy(g.xt[s][0:HALF, :, :], g.ps[bank][0:HALF, :].rearrange("p (c n) -> p c n", c=2)
                               ).then_inc(tok["turned_kept"], 1)

            def root(i, which):
                n = norms(i, which)
                act.wait_ge(tok["var_ready"], n)
                nc.scalar.activation(log_var[:, :], neg_var[:, :], ACT.Ln, bias=g.eps5[:, :], scale=-1.0
                                     ).then_inc(tok["logged"], 1)
                act.wait_ge(tok["logged"], n)
                nc.scalar.activation(rstd[:, :], log_var[:, :], ACT.Exp, scale=-0.5).then_inc(tok["rooted"], 1)

            nc.scalar.preload_act_table_set(EXP_LN)
            with act.Fori(0, BATCH // WIDE) as i:
                for s in range(WIDE):
                    turned_copy(i, s, 0, 2 * s)
                for s in range(WIDE):
                    act.wait_ge(tok["values"], at(i, s))
                    nc.scalar.copy(value[s][:, :, :],
                                   g.ps[2 * s][:, 0:TPS * DIM].rearrange("p (t n) -> p t n", t=TPS)
                                   ).then_inc(tok["values_kept"], 1)
                for s in range(WIDE):
                    act.wait_ge(tok["maxed"], at(i, s))
                    for t in range(TPS):
                        nc.scalar.activation(prob[s][:, t, :], g.ps[2 * s + 1][:, t * SEQ:(t + 1) * SEQ], ACT.Exp,
                                             bias=neg_max[s][:, t:t + 1], accum_out=row_sum[s][:, t:t + 1]
                                             ).then_inc(tok["exped"], 1)
                root(i, 0)
                nc.scalar.preload_act_table_set("gelu_and_others")
                for s in range(WIDE):
                    turned_copy(i, s, 1, 2 * s + 1)
                for s in range(WIDE):
                    act.wait_ge(tok["fed"], at(i, s))
                    nc.scalar.activation(f_out[s][:, :, :],
                                         g.ps[2 * s][:, 0:TPS * DIM].rearrange("p (t n) -> p t n", t=TPS),
                                         ACT.Gelu).then_inc(tok["gelued"], 1)
                nc.scalar.preload_act_table_set(EXP_LN)
                root(i, 1)

        @block.vector
        def _(dve):
            dve.wait_ge(g.gathered, 16 * TILES)
            dve.wait_ge(g.operands_loaded, 16 * N_OPERANDS)

            def added(i, which, s):
                return 3 * WIDE * i + (2 * WIDE + s + 1 if which else 2 * (s + 1))

            def sums(s, added):
                dve.wait_ge(tok["added"], added)
                for t in range(TPS):
                    nc.vector.bn_stats(bn[s][:, t, :], y[s][:, t, :]).then_inc(tok["stats1"], 1)

            def stats(i, which):
                for s in range(WIDE):
                    dve.wait_ge(tok["stats1"], 2 * nth(i, s, which))
                    nc.vector.nop(nofuse=True)
                    nc.vector.bn_aggr(stat[:, s, :], bn[s][:, :, :]).then_inc(tok["stats2"], 1)
                dve.wait_ge(tok["stats2"], WIDE * norms(i, which))
                nc.vector.tensor_tensor(mean_sq[:, :], stat[:, :, 0], stat[:, :, 0], ALU.mult
                                        ).then_inc(tok["squared"], 1)
                dve.wait_ge(tok["squared"], 2 * norms(i, which) - 1)
                nc.vector.tensor_tensor(stat[:, :, 1], stat[:, :, 1], mean_sq[:, :], ALU.add
                                        ).then_inc(tok["stats3"], 1)

            def norm(i, which, weight, bias, out):
                n = norms(i, which)
                dve.wait_ge(tok["stats_summed"], n)
                nc.vector.tensor_copy(stat[:, :, :], STAT_BANK[:, 0:2 * WIDE].rearrange("p (s k) -> p s k", k=2)
                                      ).then_inc(tok["stats_kept"], 1)
                dve.wait_ge(tok["stats_kept"], n)
                nc.vector.tensor_tensor(mean_sq[:, :], stat[:, :, 0], stat[:, :, 0], ALU.mult
                                        ).then_inc(tok["squared"], 1)
                dve.wait_ge(tok["squared"], 2 * n)
                nc.vector.tensor_tensor(neg_var[:, :], mean_sq[:, :], stat[:, :, 1], ALU.subtract
                                        ).then_inc(tok["var_ready"], 1)
                for s in range(WIDE + 1):
                    if s < WIDE:
                        nc.vector.scalar_tensor_tensor(out=y[s][:, :, :], in0=y[s][:, :, :],
                                                       scalar=stat[:, s, 0:1], in1=weight,
                                                       op0=ALU.subtract, op1=ALU.mult).then_inc(tok["weighted"], 1)
                    if s == 1:
                        dve.wait_ge(tok["rooted"], n)
                    if s:
                        dve.wait_ge(tok["weighted"], nth(i, s - 1, which))
                        nc.vector.scalar_tensor_tensor(out=out(s - 1), in0=y[s - 1][:, :, :],
                                                       scalar=rstd[:, s - 1:s], in1=bias, op0=ALU.mult, op1=ALU.add
                                                       ).then_inc(tok["normed"], 1)

            with dve.Fori(0, BATCH // WIDE) as i:
                dve.wait_ge(tok["normed"], 2 * WIDE * i)
                for s in range(WIDE):
                    nc.vector.tensor_tensor(y[s][:, :, :], g.h[:, ds(TPS * (WIDE * i + s), TPS), :], g.t["pos"],
                                            ALU.add).then_inc(tok["placed"], 1)
                for s in range(WIDE):
                    dve.wait_ge(tok["keys"], at(i, s))
                    nc.vector.tensor_copy(key_t[s][:, :, :],
                                          g.ps[2 * s + 1][0:AUG, :].rearrange("p (c n) -> p c n", c=2)
                                          ).then_inc(tok["keys_kept"], 1)
                for s in range(WIDE):
                    dve.wait_ge(tok["scores"], at(i, s))
                    nc.vector.tensor_reduce(neg_max[s][:, :],
                                            g.ps[2 * s + 1][:, :].rearrange("p (t n) -> p t n", t=TPS),
                                            AX.X, ALU.max, negate=True).then_inc(tok["maxed"], 1)
                for s in range(WIDE):
                    dve.wait_ge(tok["probs_turned"], at(i, s))
                    nc.vector.tensor_copy(prob_t[s][:, :, :],
                                          g.ps[2 * s][:, :].rearrange("p (m n) -> p m n", m=TPS)
                                          ).then_inc(tok["probs_kept"], 1)
                    nc.vector.reciprocal(inv_sum[s][:, :], row_sum[s][:, :]).then_inc(tok["inverted"], 1)
                for s in range(WIDE):
                    if s:
                        sums(s - 1, added(i, 0, s - 1))
                    dve.wait_ge(tok["mixed"], at(i, s))
                    dve.wait_ge(tok["inverted"], at(i, s))
                    for t in range(TPS):
                        nc.vector.scalar_tensor_tensor(
                            out=y[s][:, t, :], in0=g.ps[2 * s + 1][:, t * DIM:(t + 1) * DIM],
                            scalar=inv_sum[s][:, t:t + 1], in1=y[s][:, t, :], op0=ALU.mult, op1=ALU.add
                            ).then_inc(tok["added"], 1)
                sums(WIDE - 1, added(i, 0, WIDE - 1))
                stats(i, 0)
                norm(i, 0, g.t["ln_w1"], g.t["ln_b1"], lambda s: y[s][:, :, :])
                for s in range(WIDE):
                    dve.wait_ge(tok["gelued"], at(i, s))
                    nc.vector.tensor_tensor(y[s][:, :, :], y[s][:, :, :], f_out[s][:, :, :], ALU.add
                                            ).then_inc(tok["added"], 1)
                    if s:
                        sums(s - 1, added(i, 1, s - 1))
                sums(WIDE - 1, added(i, 1, WIDE - 1))
                stats(i, 1)
                norm(i, 1, g.t["ln_w2"], g.t["ln_b2"],
                     lambda s: g.h[:, ds(TPS * (WIDE * i + s), TPS), :])


def attention(nc, g):
    g.next_stage()
    QK = 2 * TPS * HEADS
    with ExitStack() as ctx:
        sb = lambda name, shape, dt=F32: ctx.enter_context(nc.sbuf_tensor(name, shape, dt))
        sem = lambda name: g.stage_semaphore(nc.semaphore("att_" + name))
        q_t, k_t, val, ident_b, weight = g.q_t, g.k_t, g.val, g.ident_b, g.qk_weight
        bn = sb("att_bn", [P, TPS, 6])
        mv = sb("att_mv", [P, TPS, 2])
        log_v = sb("att_log", [P, TPS])
        rstd = sb("att_rstd", [P, TPS])
        x = sb("att_x", [P, TPS, DIM])
        sq = sb("att_sq", [P, TPS, 2 * DIM])
        ss = sb("att_ss", [P, QK])
        log_s = sb("att_log_s", [P, QK])
        rms = sb("att_rms", [P, QK])
        qk = sb("att_qk", [P, QK, HDIM])
        rem = sb("att_rem", [P, QK, HDIM])
        stack = sb("att_stack", [P, QK, PARTS, HDIM], BF16)
        neg_max = sb("att_max", [P, QH, TPS])
        max_rem = sb("att_max_rem", [P, TPS, QH])
        max_bf = sb("att_max_bf", [P, TPS, 2, QH], BF16)
        prob = [sb(f"att_prob{u}", [P, 2, TPS, SEQ]) for u in range(2)]
        out_t = sb("att_out_t", [P, QUADS, SEQ])
        inv = sb("att_inv", [P, TPS, HEADS])
        mixed = sb("att_mixed", [P, TPS, HEADS, HDIM])
        x_t, mixed_t = g.xt[0:2], g.xt[2]
        S = {n: sem(n) for n in (
            "stats", "mean_var", "logged", "rooted", "normed", "x_turned", "x_kept", "qk_made", "v_made",
            "v_kept", "squared", "summed", "rms_logged", "rms_rooted", "scaled", "weighted", "part1",
            "rem1", "part2", "part3", "q_copied", "k_copied", "filled", "fill_kept_v", "fill_kept_s",
            "max_scored", "maxed", "max_hi", "max_rem", "max_lo", "max_turned", "max_kept",
            "scored", "exped", "mixed", "out_kept", "out_turned", "inverted", "divided", "mixed_turned",
            "mixed_kept", "projected", "added")}
        block = ctx.enter_context(nc.Block())
        O_BANKS = (4, 5)
        flat = lambda a, b, rows=P: g.psum[0:rows, a:b, :].rearrange("p b n -> p (b n)")

        def schedule(eng, prologue, body, finish):
            prologue()
            body(0, 0, first=True)
            with eng.Fori(0, (BATCH - 4) // 2) as i:
                body(2 * i + 1, 1)
                body(2 * i + 2, 0)
            body(BATCH - 3, 1, stat=False)
            body(BATCH - 2, 0, stat=False, make=False)
            body(BATCH - 1, 1, stat=False, make=False, fill=False)
            finish(BATCH - 1, 1)

        FRONT, FRONT_1 = (6, 7, 6), (4, 5, 4)

        def slots(which, slot):
            return stack[:, :, :, :].rearrange("p (t w h) a d -> p t w h a d", t=TPS, w=2)[:, :, which, :, slot, :]


        @block.sync
        def _(sp):
            g.clear_before(sp)

        @block.tensor
        def _(pe):
            def turn_x(n, banks=FRONT):
                if banks is FRONT and not (isinstance(n, int) and n == 0):
                    pe.wait_ge(S["scaled"], 2 * n)
                    pe.wait_ge(S["fill_kept_v"], QUADS * (n - 1))
                pe.wait_ge(S["normed"], 2 * n + 2)
                for c in range(2):
                    for t in range(TPS):
                        last = nc.tensor.transpose(
                            g.ps[banks[0]][0:HALF, c * SEQ + t * P:c * SEQ + (t + 1) * P],
                            x[:, t, c * HALF:(c + 1) * HALF], g.ident[:, :])
                last.then_inc(S["x_turned"], 1)

            def make_qk(n, s, t, banks=FRONT):
                if t == 0:
                    pe.wait_ge(S["x_kept"], n + 1)
                    if banks is FRONT and not (isinstance(n, int) and n == 0):
                        pe.wait_ge(S["fill_kept_s"], QUADS * (n - 1))
                for c in range(2):
                    k = HALF + c
                    last = nc.tensor.matmul(g.ps[banks[1 + t]][:, 0:2 * DIM], x_t[s][0:k, c, t * P:(t + 1) * P],
                                            g.t["qkv_t"][0:k, c, 0:2 * DIM], start=(c == 0), stop=(c == 1))
                last.then_inc(S["qk_made"], 1)

            def make_v(n, s, scaled):
                pe.wait_ge(S["scaled"], 2 * scaled)
                for t in range(TPS):
                    for c in range(2):
                        k = HALF + c
                        last = nc.tensor.matmul(g.ps[7][:, t * DIM:(t + 1) * DIM],
                                                x_t[s][0:k, c, t * P:(t + 1) * P],
                                                g.t["qkv_t"][0:k, c, 2 * DIM:3 * DIM],
                                                start=(c == 0), stop=(c == 1))
                last.then_inc(S["v_made"], 1)

            def fill_quad(n, quad):
                if quad == 0:
                    pe.wait_ge(S["q_copied"], 3 * n + 3)
                    pe.wait_ge(S["part3"], 2 * n + 2)
                for which, kept in ((0, "fill_kept_v"), (1, "fill_kept_s")):
                    if quad:
                        pe.wait_ge(S[kept], QUADS * n + quad)
                    elif which:
                        pe.wait_ge(S["k_copied"], 3 * n + 3)
                        pe.wait_ge(S["v_kept"], n + 1)
                    bank = g.ps[6 + which].bitcast(BF16)
                    for h in range(QH):
                        for t in range(TPS):
                            row = (t * 2 + which) * HEADS + quad * QH + h
                            last = nc.tensor.transpose(
                                bank[0:KS, h * SEQ + t * P:h * SEQ + (t + 1) * P],
                                stack[:, row, :, :].rearrange("p a b -> p (a b)"), ident_b[:, :])
                    last.then_inc(S["filled"], 1)

            def prologue():
                turn_x(0)
                for t in range(TPS):
                    make_qk(0, 0, t)
                turn_x(1, FRONT_1)
                for t in range(TPS):
                    make_qk(1, 1, t, FRONT_1)
                make_v(0, 0, 1)
                for quad in range(QUADS):
                    fill_quad(0, quad)
                max_scores(0, 0, 0, 0)

            def max_scores(n, s, q, u):
                count = QUADS * n + q
                if u == 0:
                    pe.wait_ge(S["fill_kept_v"], QUADS * n + q + 1)
                    pe.wait_ge(S["fill_kept_s"], QUADS * n + q + 1)
                pe.wait_ge(S["maxed"], 2 * count + u)
                for hh in range(2):
                    h = QH * q + 2 * u + hh
                    for t in range(TPS):
                        last = nc.tensor.matmul(g.ps[hh][:, t * SEQ:(t + 1) * SEQ],
                                                q_t[s][0:KS, h, t * P:(t + 1) * P], k_t[s][0:KS, h, :],
                                                start=True, stop=True)
                last.then_inc(S["max_scored"], 1)

            def turn_max(n, q):
                count = QUADS * n + q
                pe.wait_ge(S["max_lo"], count + 1)
                pe.wait_ge(S["exped"], 2 * count)
                for t in range(TPS):
                    last = nc.tensor.transpose(g.ps[2].bitcast(BF16)[KS:KM, t * P:(t + 1) * P],
                                               max_bf[:, t, :, :].rearrange("p a b -> p (a b)"), ident_b[:, :])
                last.then_inc(S["max_turned"], 1)

            def scores(n, s, q, u):
                count = 2 * (QUADS * n + q) + u
                if u == 0:
                    pe.wait_ge(S["max_kept"], QUADS * n + q + 1)
                pe.wait_ge(S["exped"], count)
                for hh in range(2):
                    h = QH * q + 2 * u + hh
                    for m in range(TPS):
                        last = nc.tensor.matmul(g.ps[2 + hh][:, m * SEQ:(m + 1) * SEQ],
                                                k_t[s][:, h, m * P:(m + 1) * P], q_t[s][:, h, :],
                                                start=True, stop=True)
                last.then_inc(S["scored"], 1)

            def mix(n, s, q):
                pe.wait_ge(S["exped"], 2 * (QUADS * n + q) + 2)
                if q == 0:
                    pe.wait_ge(S["mixed_kept"], n)
                if q == 2:
                    pe.wait_ge(S["added"], n)
                bank = g.ps[O_BANKS[q // 2]]
                for m in range(TPS):
                    for j in range(QH):
                        last = nc.tensor.matmul(
                            bank[32 * j:32 * j + 32, (q % 2) * SEQ:(q % 2 + 1) * SEQ],
                            val[s][:, m, QH * q + j, :], prob[j // 2][:, j % 2, m, :],
                            start=(m == 0), stop=(m == TPS - 1))
                last.then_inc(S["mixed"], 1)

            def turn_out(n):
                pe.wait_ge(S["out_kept"], n + 1)
                for t in range(TPS):
                    for q in range(QUADS):
                        last = nc.tensor.transpose(g.ps[O_BANKS[t]][:, q * P:(q + 1) * P],
                                                   out_t[:, q, t * P:(t + 1) * P], g.ident[:, :])
                last.then_inc(S["out_turned"], 1)

            def turn_mixed(n):
                pe.wait_ge(S["divided"], n + 1)
                flat_mixed = mixed[:, :, :, :].rearrange("p t h d -> p t (h d)")
                for c in range(2):
                    for t in range(TPS):
                        last = nc.tensor.transpose(
                            g.ps[4][0:HALF, c * SEQ + t * P:c * SEQ + (t + 1) * P],
                            flat_mixed[:, t, c * HALF:(c + 1) * HALF], g.ident[:, :])
                last.then_inc(S["mixed_turned"], 1)

            def project(n):
                pe.wait_ge(S["mixed_kept"], n + 1)
                for t in range(TPS):
                    for c in range(2):
                        k = HALF + c
                        last = nc.tensor.matmul(g.ps[5][:, t * DIM:(t + 1) * DIM],
                                                mixed_t[0:k, c, t * P:(t + 1) * P],
                                                g.t["proj_t"][0:k, c, :], start=(c == 0), stop=(c == 1))
                last.then_inc(S["projected"], 1)

            def body(n, s, first=False, stat=True, make=True, fill=True):
                for q in range(QUADS):
                    pn, ps_, pq = (n, s, q - 1) if q else (n - 1, 1 - s, QUADS - 1)
                    prev = q or not first
                    if prev:
                        scores(pn, ps_, pq, 0)
                    if q == 2 and fill:
                        fill_quad(n + 1, 0)
                    max_scores(n, s, q, 1)
                    if q == 0 and make:
                        turn_x(n + 2)
                    if q == 1 and not first:
                        turn_mixed(n - 1)
                    if prev:
                        scores(pn, ps_, pq, 1)
                    if q == 0 and make:
                        make_qk(n + 2, s, 0)
                    if q == 1 and not first:
                        project(n - 1)
                    if q == 2 and fill:
                        fill_quad(n + 1, 1)
                    if prev:
                        mix(pn, ps_, pq)
                    turn_max(n, q)
                    if q < QUADS - 1:
                        max_scores(n, s, q + 1, 0)
                    elif fill:
                        max_scores(n + 1, 1 - s, 0, 0)
                    if q == 0 and make:
                        make_qk(n + 2, s, 1)
                    if q == 0 and not first:
                        turn_out(n - 1)
                    if q == 1 and fill:
                        make_v(n + 1, 1 - s, n + 3 if make else BATCH)
                    if q == 2 and fill:
                        fill_quad(n + 1, 2)

            def finish(n, s):
                for u in range(2):
                    scores(n, s, QUADS - 1, u)
                mix(n, s, QUADS - 1)
                turn_out(n)
                turn_mixed(n)
                project(n)

            schedule(pe, prologue, body, finish)


        @block.scalar
        def _(act):
            act.wait_ge(g.consts_set, 2)

            def root_var(n):
                act.wait_ge(S["mean_var"], 2 * n + 2)
                nc.scalar.activation(log_v[:, :], mv[:, :, 1], ACT.Ln, bias=g.eps5[:, :]).then_inc(S["logged"], 1)
                act.wait_ge(S["logged"], n + 1)
                nc.scalar.activation(rstd[:, :], log_v[:, :], ACT.Exp, scale=-0.5).then_inc(S["rooted"], 1)

            def keep_x(n, s, banks=FRONT):
                act.wait_ge(S["x_turned"], n + 1)
                nc.scalar.copy(x_t[s][0:HALF, :, :], g.ps[banks[0]][0:HALF, :].rearrange("p (c n) -> p c n", c=2)
                               ).then_inc(S["x_kept"], 1)

            def square(n, t, banks=FRONT):
                act.wait_ge(S["summed"], n)
                act.wait_ge(S["qk_made"], 2 * n + t + 1)
                nc.scalar.activation(sq[:, t, :], g.ps[banks[1 + t]][:, 0:2 * DIM], ACT.Square).then_inc(S["squared"], 1)

            def root_rms(n):
                act.wait_ge(S["summed"], n + 1)
                nc.scalar.activation(log_s[:, :], ss[:, :], ACT.Ln, scale=1.0 / HDIM, bias=g.rms_eps[:, :]
                                     ).then_inc(S["rms_logged"], 1)
                act.wait_ge(S["rms_logged"], n + 1)
                nc.scalar.activation(rms[:, :], log_s[:, :], ACT.Exp, scale=-0.5).then_inc(S["rms_rooted"], 1)

            def repeat(n):
                act.wait_ge(S["part2"], 2 * n + 2)
                for to, of in ((3, 5), (4, 5), (1, 0)):
                    nc.scalar.copy(slots(1, to), slots(1, of)).then_inc(S["k_copied"], 1)

            def keep_v(n, s):
                act.wait_ge(S["v_made"], n + 1)
                nc.scalar.copy(val[s][:, :, :, 0:HDIM].rearrange("p t h d -> p (t h) d"),
                               g.ps[7][:, 0:TPS * DIM].rearrange("p (g d) -> p g d", d=HDIM)
                               ).then_inc(S["v_kept"], 1)

            def keep_fill(n, s, quad):
                act.wait_ge(S["filled"], 6 * n + 2 * quad + 2)
                nc.scalar.copy(k_t[s][0:KS, quad * QH:(quad + 1) * QH, :],
                               g.ps[7].bitcast(BF16)[0:KS, :].rearrange("p (h n) -> p h n", h=QH)
                               ).then_inc(S["fill_kept_s"], 1)

            def prologue():
                root_var(0)
                root_var(1)
                keep_x(0, 0)
                for t in range(TPS):
                    square(0, t)
                keep_x(1, 1, FRONT_1)
                root_rms(0)
                for t in range(TPS):
                    square(1, t, FRONT_1)
                repeat(0)
                keep_v(0, 0)
                root_rms(1)
                for quad in range(QUADS):
                    keep_fill(0, 0, quad)
                root_var(2)

            def expo(n, q, u):
                count = 2 * (QUADS * n + q) + u
                act.wait_ge(S["scored"], count + 1)
                act.wait_ge(S["mixed"], QUADS * n + q)
                nc.scalar.activation(prob[u][:, :, :, :].rearrange("p a b n -> p (a b n)"), flat(2, 4), ACT.Exp
                                     ).then_inc(S["exped"], 1)

            def keep_out(n):
                act.wait_ge(S["mixed"], QUADS * n + QUADS)
                nc.scalar.copy(out_t[:, :, :].rearrange("p q n -> p (q n)"), flat(4, 6)[:, 0:QUADS * SEQ]
                               ).then_inc(S["out_kept"], 1)

            def keep_mixed(n):
                act.wait_ge(S["mixed_turned"], n + 1)
                nc.scalar.copy(mixed_t[0:HALF, :, :], g.ps[4][0:HALF, :].rearrange("p (c n) -> p c n", c=2)
                               ).then_inc(S["mixed_kept"], 1)

            def body(n, s, first=False, stat=True, make=True, fill=True):
                for q in range(QUADS):
                    pn, pq = (n, q - 1) if q else (n - 1, QUADS - 1)
                    prev = q or not first
                    if prev:
                        expo(pn, pq, 0)
                    if q == 0 and make:
                        keep_x(n + 2, s)
                    if q == 1 and not first:
                        keep_mixed(n - 1)
                    if q == 1 and make:
                        root_rms(n + 2)
                    if q == 2 and fill:
                        keep_fill(n + 1, 1 - s, 0)
                    if q == 2 and stat:
                        root_var(n + 3)
                    if prev:
                        expo(pn, pq, 1)
                    if q == 0 and make:
                        square(n + 2, 0)
                    if q == 0 and not first:
                        keep_out(n - 1)
                    if q == 0 and make:
                        square(n + 2, 1)
                    if q == 1 and fill:
                        repeat(n + 1)
                        keep_v(n + 1, 1 - s)
                    if q == 2 and fill:
                        keep_fill(n + 1, 1 - s, 1)
                        keep_fill(n + 1, 1 - s, 2)

            def finish(n, s):
                for u in range(2):
                    expo(n, QUADS - 1, u)
                keep_out(n)
                keep_mixed(n)

            schedule(act, prologue, body, finish)


        @block.vector
        def _(dve):
            def norm_stats(n):
                dve.wait_ge(S["rooted"], n)
                for t in range(TPS):
                    nc.vector.nop(nofuse=True)
                    nc.vector.bn_stats(bn[:, t, :], g.h[:, ds(TPS * n + t, 1), :].rearrange("p a n -> p (a n)")
                                       ).then_inc(S["stats"], 1)
                dve.wait_ge(S["stats"], 2 * n + 2)
                nc.vector.nop(nofuse=True)
                for t in range(TPS):
                    nc.vector.bn_aggr(mv[:, t, :], bn[:, t, :]).then_inc(S["mean_var"], 1)

            def norm(n):
                dve.wait_ge(S["rooted"], n + 1)
                dve.wait_ge(S["x_turned"], n)
                for t in range(TPS):
                    nc.vector.tensor_scalar(x[:, t, :], g.h[:, ds(TPS * n + t, 1), :].rearrange("p a n -> p (a n)"),
                                            mv[:, t, 0:1], rstd[:, t:t + 1], ALU.subtract, ALU.mult
                                            ).then_inc(S["normed"], 1)

            def sum_squares(n):
                dve.wait_ge(S["squared"], 2 * n + 2)
                nc.vector.tensor_reduce(ss[:, :], sq[:, :, :].rearrange("p t (g d) -> p (t g) d", d=HDIM),
                                        AX.X, ALU.add).then_inc(S["summed"], 1)

            def scale(n, banks=FRONT):
                dve.wait_ge(S["rms_rooted"], n + 1)
                dve.wait_ge(S["part3"], 2 * n)
                for t in range(TPS):
                    r = rms[:, t * 24:(t + 1) * 24]
                    nc.vector.tensor_tensor(qk[:, t * 24:(t + 1) * 24, :],
                                            g.ps[banks[1 + t]][:, 0:2 * DIM].rearrange("p (g d) -> p g d", d=HDIM),
                                            r.unsqueeze(2).broadcast_to((P, 24, HDIM)), ALU.mult
                                            ).then_inc(S["scaled"], 1)

            def split(n):
                both = lambda v, which: v[:, :, :].rearrange("p (t w h) d -> p t w h d", t=TPS, w=2)[:, :, which]
                dve.wait_ge(S["weighted"], 2 * n + 2)
                dve.wait_ge(S["filled"], 6 * n)
                for which, slot in ((0, 0), (1, 5)):
                    nc.vector.tensor_copy(slots(which, slot), both(qk, which)).then_inc(S["part1"], 1)
                dve.wait_ge(S["part1"], 2 * n + 2)
                for which, slot in ((0, 0), (1, 5)):
                    nc.vector.tensor_tensor(both(rem, which), both(qk, which), slots(which, slot),
                                            ALU.subtract).then_inc(S["rem1"], 1)

            def split_rest(n):
                both = lambda v, which: v[:, :, :].rearrange("p (t w h) d -> p t w h d", t=TPS, w=2)[:, :, which]
                dve.wait_ge(S["rem1"], 2 * n + 2)
                for which, slot in ((0, 1), (1, 0)):
                    nc.vector.tensor_copy(slots(which, slot), both(rem, which)).then_inc(S["part2"], 1)
                dve.wait_ge(S["part2"], 2 * n + 2)
                for which, slot, part2 in ((0, 5, 1), (1, 2, 0)):
                    nc.vector.tensor_tensor(slots(which, slot), both(rem, which),
                                            slots(which, part2), ALU.subtract
                                            ).then_inc(S["part3"], 1)

            def repeat(n):
                dve.wait_ge(S["part2"], 2 * n + 2)
                for to, of in ((2, 0), (4, 0), (3, 1)):
                    nc.vector.tensor_copy(slots(0, to), slots(0, of)).then_inc(S["q_copied"], 1)

            def keep_fill(n, s, quad):
                dve.wait_ge(S["filled"], 6 * n + 2 * quad + 1)
                nc.vector.tensor_copy(q_t[s][0:KS, quad * QH:(quad + 1) * QH, :],
                                      g.ps[6].bitcast(BF16)[0:KS, :].rearrange("p (h n) -> p h n", h=QH)
                                      ).then_inc(S["fill_kept_v"], 1)

            def prologue():
                norm_stats(0)
                norm(0)
                norm_stats(1)
                norm(1)
                sum_squares(0)
                scale(0)
                split(0)
                split_rest(0)
                repeat(0)
                sum_squares(1)
                for quad in range(QUADS):
                    keep_fill(0, 0, quad)
                norm_stats(2)
                scale(1, FRONT_1)
                row_max(0, 0, 0)
                norm(2)
                split(1)

            def row_max(n, q, u):
                count = QUADS * n + q
                dve.wait_ge(S["max_scored"], 2 * count + u + 1)
                if u == 0:
                    dve.wait_ge(S["max_hi"], count)
                    dve.wait_ge(S["max_rem"], count)
                nc.vector.tensor_reduce(neg_max[:, 2 * u:2 * u + 2, :].rearrange("p a b -> p (a b)"),
                                        flat(0, 2).rearrange("p (g n) -> p g n", n=SEQ), AX.X, ALU.max,
                                        negate=True).then_inc(S["maxed"], 1)

            def split_max(n, q):
                count = QUADS * n + q
                by_tile = neg_max[:, :, :].rearrange("p h t -> p t h")
                dve.wait_ge(S["maxed"], 2 * count + 2)
                dve.wait_ge(S["max_turned"], count)
                nc.vector.tensor_copy(max_bf[:, :, 0, :], by_tile).then_inc(S["max_hi"], 1)
                dve.wait_ge(S["max_hi"], count + 1)
                dve.wait_ge(S["max_lo"], count)
                nc.vector.tensor_tensor(max_rem[:, :, :], by_tile, max_bf[:, :, 0, :], ALU.subtract
                                        ).then_inc(S["max_rem"], 1)
                dve.wait_ge(S["max_rem"], count + 1)
                nc.vector.tensor_copy(max_bf[:, :, 1, :], max_rem[:, :, :]).then_inc(S["max_lo"], 1)

            def keep_max(n, s, q):
                count = QUADS * n + q
                dve.wait_ge(S["max_turned"], count + 1)
                nc.vector.tensor_copy(q_t[s][KS:KM, QH * q:QH * (q + 1), :],
                                      g.ps[2].bitcast(BF16)[KS:KM, 0:SEQ].unsqueeze(1).broadcast_to((2 * QH, QH, SEQ))
                                      ).then_inc(S["max_kept"], 1)

            def divide(n):
                by_head = g.psum[:, 4:6, 0:QUADS * P].rearrange("p t (h c) -> p t h c", c=32)
                dve.wait_ge(S["out_turned"], n + 1)
                dve.wait_ge(S["divided"], n)
                nc.vector.reciprocal(inv[:, :, :], by_head[:, :, :, SUM]).then_inc(S["inverted"], 1)
                dve.wait_ge(S["inverted"], n + 1)
                dve.wait_ge(S["mixed_turned"], n)
                nc.vector.tensor_tensor(mixed[:, :, :, :], by_head[:, :, :, 0:HDIM],
                                        inv[:, :, :].unsqueeze(3).broadcast_to((P, TPS, HEADS, HDIM)), ALU.mult
                                        ).then_inc(S["divided"], 1)

            def add(n):
                dve.wait_ge(S["projected"], n + 1)
                state = g.h[:, ds(TPS * n, TPS), :]
                nc.vector.tensor_tensor(state, state,
                                        g.ps[5][:, 0:TPS * DIM].rearrange("p (t d) -> p t d", t=TPS), ALU.add
                                        ).then_inc(S["added"], 1)

            def body(n, s, first=False, stat=True, make=True, fill=True):
                for q in range(QUADS):
                    if q == 2 and fill:
                        keep_fill(n + 1, 1 - s, 0)
                    row_max(n, q, 1)
                    split_max(n, q)
                    if q == 0 and fill:
                        split_rest(n + 1)
                    if q == 1 and make:
                        scale(n + 2)
                    if q == 1 and fill:
                        repeat(n + 1)
                    if q == 2 and fill:
                        keep_fill(n + 1, 1 - s, 1)
                    keep_max(n, s, q)
                    if q < QUADS - 1:
                        row_max(n, q + 1, 0)
                    elif fill:
                        row_max(n + 1, 0, 0)
                    if q == 0 and not first:
                        divide(n - 1)
                    if q == 0 and make:
                        sum_squares(n + 2)
                    if q == 1 and not first:
                        add(n - 1)
                    if q == 1 and stat:
                        norm_stats(n + 3)
                    if q == 2 and fill:
                        keep_fill(n + 1, 1 - s, 2)
                    if q == 2 and stat:
                        norm(n + 3)
                    if q == 2 and make:
                        split(n + 2)

            def finish(n, s):
                divide(n)
                add(n)

            schedule(dve, prologue, body, finish)


        @block.gpsimd
        def _(pool):
            def weigh(n):
                for t in range(TPS):
                    pool.wait_ge(S["scaled"], 2 * n + t + 1)
                    q_part = qk[:, 2 * t * HEADS:(2 * t + 1) * HEADS, :]
                    nc.gpsimd.tensor_tensor(q_part, q_part,
                                            weight[:, :].unsqueeze(1).broadcast_to((P, HEADS, HDIM)), ALU.mult
                                            ).then_inc(S["weighted"], 1)

            def prologue():
                weigh(0)
                weigh(1)

            def body(n, s, first=False, stat=True, make=True, fill=True):
                if make:
                    weigh(n + 2)

            schedule(pool, prologue, body, lambda n, s: None)


def first_slots(nc, g):
    g.next_stage()
    with ExitStack() as ctx:
        def sb(name, shape, dt=F32):
            return [ctx.enter_context(nc.sbuf_tensor(f"fs_{name}{s}", shape, dt)) for s in range(WIDE)]

        sem = lambda name: g.stage_semaphore(nc.semaphore("fs_" + name))
        bn = sb("bn", [P, TPS, 6])
        one = lambda name, shape: ctx.enter_context(nc.sbuf_tensor("fs_" + name, shape, F32))
        mv = one("mv", [P, WIDE * TPS, 2])
        log_v = one("log_v", [P, WIDE * TPS])
        factor = one("factor", [P, WIDE * TPS])
        x = sb("x", [P, TPS, DIM])
        x_t = sb("x_t", [HALF, 2, SEQ])
        neg_slot = sb("neg_slot", [P, GPS])
        neg_tok = sb("neg_tok", [P, TPS])
        disp_t = sb("disp_t", [P, SEQ])
        disp_sum = sb("disp_sum", [P, GPS])
        comb = sb("comb", [P, TPS, P])
        comb_sum = sb("comb_sum", [P, TPS])
        comb_inv = sb("comb_inv", [P, TPS])
        disp = sb("disp", [P, GPS, P])
        square = sb("square", [P, DIM])
        slot_ss = sb("slot_ss", [P, GPS])
        eps_part = sb("eps_part", [P, GPS])
        slot_var = sb("slot_var", [P, GPS])
        slot_log = sb("slot_log", [P, GPS])
        slot_fac = sb("slot_fac", [P, GPS])
        yn = sb("yn", [P, GPS, DIM])
        mean_rows = sb("mean_rows", [P, DIM])
        S = {n: sem(n) for n in (
            "stats", "mean_var", "logged", "rooted", "centred", "weighted", "turned", "kept", "logits",
            "slot_maxed", "tok_maxed", "disp_exped", "comb_exped", "inverted", "combined", "disp_turned",
            "comb_turned", "disp_kept", "comb_kept", "slots_made", "squared", "eps_made", "var_made",
            "slot_logged", "slot_rooted", "slots_normed", "stored", "means_made", "mean_rows_kept",
            "means_turned", "means_kept", "zeroed")}
        at = lambda i, s, per=1: (WIDE * i + s + 1) * per
        block = ctx.enter_context(nc.Block())

        @block.tensor
        def _(pe):
            pe.wait_ge(S["zeroed"], 2 * WIDE)
            with pe.Fori(0, BATCH // WIDE) as i:
                for s in range(WIDE):
                    pe.wait_ge(S["weighted"], at(i, s))
                    for c in range(2):
                        for t in range(TPS):
                            last = nc.tensor.transpose(
                                g.ps[2 * s][0:HALF, c * SEQ + t * P:c * SEQ + (t + 1) * P],
                                x[s][:, t, c * HALF:(c + 1) * HALF], g.ident[:, :])
                    last.then_inc(S["turned"], 1)
                for s in range(WIDE):
                    pe.wait_ge(S["kept"], at(i, s))
                    bank = g.ps[2 * s + 1]
                    for c in range(2):
                        nc.tensor.matmul(bank[:, 0:SEQ], g.phi_t[:, c, :], x_t[s][0:HALF, c, :],
                                         start=(c == 0), stop=(c == 1))
                    for t in range(TPS):
                        for c in range(2):
                            last = nc.tensor.matmul(bank[:, SEQ + t * P:SEQ + (t + 1) * P],
                                                    x_t[s][0:HALF, c, t * P:(t + 1) * P], g.phi_t[:, c, :],
                                                    start=(c == 0), stop=(c == 1))
                    last.then_inc(S["logits"], 1)
                for s in range(WIDE):
                    pe.wait_ge(S["disp_exped"], at(i, s, GPS))
                    for t in range(TPS):
                        last = nc.tensor.transpose(g.ps[2 * s][:, t * P:(t + 1) * P],
                                                   disp_t[s][:, t * P:(t + 1) * P], g.ident[:, :])
                    last.then_inc(S["disp_turned"], 1)
                for s in range(WIDE):
                    pe.wait_ge(S["combined"], at(i, s))
                    for t in range(TPS):
                        last = nc.tensor.transpose(g.ps[2 * s + 1][:, t * P:(t + 1) * P], comb[s][:, t, :],
                                                   g.ident[:, :])
                    last.then_inc(S["comb_turned"], 1)
                for s in range(WIDE):
                    pe.wait_ge(S["disp_kept"], at(i, s, 2))
                    pe.wait_ge(S["comb_kept"], at(i, s))
                    for gr in range(GPS):
                        t = gr // 2
                        last = nc.tensor.matmul(g.ps[2 * s + gr % 2][:, t * DIM:(t + 1) * DIM],
                                                disp[s][:, gr, :], x[s][:, t, :], start=True, stop=True)
                    last.then_inc(S["slots_made"], 1)
                for s in range(WIDE):
                    pe.wait_ge(S["slots_normed"], at(i, s, GPS))
                    for gr in range(GPS):
                        m0 = gr * (P // MEAN)
                        last = nc.tensor.matmul(g.ps[2 * s + 1][m0:m0 + P // MEAN, 0:DIM], g.average[:, :],
                                                yn[s][:, gr, :], start=True, stop=True)
                    last.then_inc(S["means_made"], 1)
                for s in range(WIDE):
                    pe.wait_ge(S["mean_rows_kept"], at(i, s))
                    for c in range(2):
                        last = nc.tensor.transpose(g.ps[2 * s][0:HALF, c * P:(c + 1) * P],
                                                   mean_rows[s][:, c * HALF:(c + 1) * HALF], g.ident[:, :])
                    last.then_inc(S["means_turned"], 1)

        @block.scalar
        def _(act):
            act.wait_ge(g.consts_set, 2)
            with act.Fori(0, BATCH // WIDE) as i:
                act.wait_ge(S["mean_var"], at(i, WIDE - 1, TPS))
                nc.scalar.activation(log_v[:, :], mv[:, :, 1], ACT.Ln, scale=1.0 + 1e-6 / DIM,
                                     bias=g.eps_norms[:, :]).then_inc(S["logged"], 1)
                act.wait_ge(S["logged"], i + 1)
                nc.scalar.activation(factor[:, :], log_v[:, :], ACT.Exp, scale=-0.5).then_inc(S["rooted"], 1)
                for s in range(WIDE):
                    act.wait_ge(S["turned"], at(i, s))
                    nc.scalar.copy(x_t[s][0:HALF, :, :], g.ps[2 * s][0:HALF, :].rearrange("p (c n) -> p c n", c=2)
                                   ).then_inc(S["kept"], 1)
                for s in range(WIDE):
                    act.wait_ge(S["slot_maxed"], at(i, s))
                    act.wait_ge(S["tok_maxed"], at(i, s))
                    for gr in range(GPS):
                        cols = slice(gr * GROUP, (gr + 1) * GROUP)
                        nc.scalar.activation(disp_t[s][:, cols], g.ps[2 * s + 1][:, cols], ACT.Exp,
                                             bias=neg_slot[s][:, gr:gr + 1], accum_out=disp_sum[s][:, gr:gr + 1]
                                             ).then_inc(S["disp_exped"], 1)
                    for t in range(TPS):
                        nc.scalar.activation(comb[s][:, t, :], g.ps[2 * s + 1][:, SEQ + t * P:SEQ + (t + 1) * P],
                                             ACT.Exp, bias=neg_tok[s][:, t:t + 1],
                                             accum_out=comb_sum[s][:, t:t + 1]).then_inc(S["comb_exped"], 1)
                for s in range(WIDE):
                    act.wait_ge(S["disp_turned"], at(i, s))
                    for half in range(2):
                        rows = slice(GROUP * half, GROUP * (half + 1))
                        nc.scalar.copy(disp[s][rows, half::2, :],
                                       g.ps[2 * s][rows, 0:SEQ].rearrange("p (t n) -> p t n", t=TPS)
                                       ).then_inc(S["disp_kept"], 1)
                def root_slots(s):
                    act.wait_ge(S["var_made"], at(i, s))
                    nc.scalar.activation(slot_log[s][:, :], slot_var[s][:, :], ACT.Ln, scale=1.0 / DIM
                                         ).then_inc(S["slot_logged"], 1)
                    act.wait_ge(S["slot_logged"], at(i, s))
                    nc.scalar.activation(slot_fac[s][:, :], slot_log[s][:, :], ACT.Exp, scale=-0.5
                                         ).then_inc(S["slot_rooted"], 1)

                for s in range(WIDE):
                    act.wait_ge(S["slots_made"], at(i, s))
                    for gr in range(GPS):
                        t = gr // 2
                        act.wait_ge(S["squared"], at(i, s, GPS) - GPS + gr)
                        nc.scalar.activation(square[s][:, :],
                                             g.ps[2 * s + gr % 2][:, t * DIM:(t + 1) * DIM], ACT.Square,
                                             accum_out=slot_ss[s][:, gr:gr + 1]).then_inc(S["squared"], 1)
                    if s:
                        root_slots(s - 1)
                root_slots(WIDE - 1)
                for s in range(WIDE):
                    act.wait_ge(S["means_made"], at(i, s))
                    nc.scalar.copy(mean_rows[s][:, :], g.ps[2 * s + 1][:, 0:DIM]).then_inc(S["mean_rows_kept"], 1)
                for s in range(WIDE):
                    nc.scalar.nop(nofuse=True)
                    nc.scalar.copy(g.yn[:, ds((WIDE * i + s) * GPS, GPS), :], yn[s][:, :, :]
                                   ).then_inc(S["stored"], 1)

        @block.vector
        def _(dve):
            with dve.Fori(0, BATCH // WIDE) as i:
                dve.wait_ge(S["rooted"], i)
                for s in range(WIDE):
                    for t in range(TPS):
                        nc.vector.nop(nofuse=True)
                        row = g.h[:, ds(TPS * (WIDE * i + s) + t, 1), :].rearrange("p a n -> p (a n)")
                        nc.vector.bn_stats(bn[s][:, t, :], row).then_inc(S["stats"], 1)
                for s in range(WIDE):
                    dve.wait_ge(S["stats"], at(i, s, TPS))
                    nc.vector.nop(nofuse=True)
                    for t in range(TPS):
                        nc.vector.bn_aggr(mv[:, s * TPS + t, :], bn[s][:, t, :]).then_inc(S["mean_var"], 1)
                dve.wait_ge(S["rooted"], i + 1)
                dve.wait_ge(S["slots_made"], WIDE * i)

                def weigh(s):
                    dve.wait_ge(S["centred"], at(i, s, TPS))
                    nc.vector.tensor_tensor(x[s][:, :, :], x[s][:, :, :],
                                            g.t["gamma_in"].unsqueeze(1).broadcast_to((P, TPS, DIM)), ALU.mult
                                            ).then_inc(S["weighted"], 1)

                for s in range(WIDE):
                    for t in range(TPS):
                        row = g.h[:, ds(TPS * (WIDE * i + s) + t, 1), :].rearrange("p a n -> p (a n)")
                        col = s * TPS + t
                        nc.vector.tensor_scalar(x[s][:, t, :], row, mv[:, col, 0:1], factor[:, col:col + 1],
                                                ALU.subtract, ALU.mult).then_inc(S["centred"], 1)
                    if s:
                        weigh(s - 1)
                weigh(WIDE - 1)
                for s in range(WIDE):
                    dve.wait_ge(S["logits"], at(i, s))
                    nc.vector.tensor_reduce(neg_slot[s][:, :],
                                            g.ps[2 * s + 1][:, 0:SEQ].rearrange("p (g n) -> p g n", g=GPS),
                                            AX.X, ALU.max, negate=True).then_inc(S["slot_maxed"], 1)
                    nc.vector.tensor_reduce(neg_tok[s][:, :],
                                            g.ps[2 * s + 1][:, SEQ:].rearrange("p (t n) -> p t n", t=TPS),
                                            AX.X, ALU.max, negate=True).then_inc(S["tok_maxed"], 1)
                for s in range(WIDE):
                    dve.wait_ge(S["comb_exped"], at(i, s, TPS))
                    nc.vector.reciprocal(comb_inv[s][:, :], comb_sum[s][:, :]).then_inc(S["inverted"], 1)
                    dve.wait_ge(S["inverted"], at(i, s))
                    nc.vector.tensor_tensor(comb[s][:, :, :], comb[s][:, :, :],
                                            comb_inv[s][:, :].unsqueeze(2).broadcast_to((P, TPS, P)), ALU.mult
                                            ).then_inc(S["combined"], 1)
                for s in range(WIDE):
                    dve.wait_ge(S["comb_turned"], at(i, s))
                    nc.vector.nop(nofuse=True)
                    nc.vector.tensor_copy(g.comb_t[:, ds((WIDE * i + s) * SEQ, SEQ)], g.ps[2 * s + 1][:, 0:SEQ]
                                          ).then_inc(S["comb_kept"], 1)
                def norm_slots(s):
                    dve.wait_ge(S["slot_rooted"], at(i, s))
                    for gr in range(GPS):
                        t = gr // 2
                        nc.vector.scalar_tensor_tensor(
                            out=yn[s][:, gr, :], in0=g.ps[2 * s + gr % 2][:, t * DIM:(t + 1) * DIM],
                            scalar=slot_fac[s][:, gr:gr + 1], in1=g.t["gamma2"], op0=ALU.mult, op1=ALU.mult
                            ).then_inc(S["slots_normed"], 1)

                dve.wait_ge(S["stored"], WIDE * i)
                for s in range(WIDE):
                    nc.vector.scalar_tensor_tensor(out=eps_part[s][:, :], in0=disp_sum[s][:, :], scalar=1e-6,
                                                   in1=disp_sum[s][:, :], op0=ALU.mult, op1=ALU.mult
                                                   ).then_inc(S["eps_made"], 1)
                for s in range(WIDE):
                    dve.wait_ge(S["eps_made"], at(i, s))
                    dve.wait_ge(S["squared"], at(i, s, GPS))
                    nc.vector.tensor_tensor(slot_var[s][:, :], slot_ss[s][:, :], eps_part[s][:, :], ALU.add
                                            ).then_inc(S["var_made"], 1)
                    if s:
                        norm_slots(s - 1)
                norm_slots(WIDE - 1)
                for s in range(WIDE):
                    dve.wait_ge(S["means_turned"], at(i, s))
                    nc.vector.nop(nofuse=True)
                    for c in range(2):
                        nc.vector.tensor_copy(
                            g.means_t[:, c, :, ds((WIDE * i + s) * GPS, GPS), :],
                            g.ps[2 * s][0:HALF, c * P:(c + 1) * P].rearrange("p (g k m) -> p k g m", g=GPS, k=E1)
                            ).then_inc(S["means_kept"], 1)

        @block.sync
        def _(sp):
            for s in range(W):
                load_slot2(sp, g, 0, s)
            for e in range(E2):
                load_expert(sp, g, 0, e)
            g.clear_before(sp)

        @block.gpsimd
        def _(pool):
            for s in range(WIDE):
                nc.gpsimd.memset(disp[s][0:GROUP, 1::2, :], 0.0).then_inc(S["zeroed"], 1)
                nc.gpsimd.memset(disp[s][GROUP:P, 0::2, :], 0.0).then_inc(S["zeroed"], 1)


def load_slot2(sp, g, i, s):
    sp.dma_start(g.w_slot2[s][:, :, :], g.d["w_slot2"][ds(W * i + s, 1)].rearrange("a p c n -> (a p) c n")
                 ).then_inc(g.w_slot2_loaded[s], 16)


def load_expert(sp, g, k, e):
    sp.dma_start(g.w1[e][:, :, :], g.d["w1"][ds(k, 1), e].rearrange("a p c n -> (a p) c n")
                 ).then_inc(g.w1_loaded[e], 16)
    sp.dma_start(g.w2[e][:, :, :], g.d["w2e"][ds(k, 1), e].rearrange("a p c n -> (a p) c n")
                 ).then_inc(g.w2_loaded[e], 16)


def second_slots(nc, g):
    g.next_stage()
    with ExitStack() as ctx:
        def sb(name, shape, dt=F32):
            return [ctx.enter_context(nc.sbuf_tensor(f"ss_{name}{s}", shape, dt)) for s in range(W)]

        sem = lambda name: g.stage_semaphore(nc.semaphore("ss_" + name))
        mean_k = sb("mean_k", [HALF, 2, P])
        square = sb("square", [P, DIM])
        ss = sb("ss", [P, E2])
        log_s = sb("log_s", [P, E2])
        factor = sb("factor", [P, E2])
        se = sb("se", [P, E2, DIM])
        weight, loaded = g.w_slot2, g.w_slot2_loaded
        S = {n: [sem(f"{n}{s}") for s in range(W)] for n in (
            "means", "made", "squared", "logged", "rooted", "normed", "turned", "kept_v", "kept_s")}
        block = ctx.enter_context(nc.Block())

        def pipeline(eng, early, late, fetch=lambda i, s: None):
            fetch(0, 0)
            fetch(0, 1)
            early(0, 0)
            with eng.Fori(0, E1 // W - 1) as i:
                fetch(i + 1, 0)
                early(i, 1)
                fetch(i + 1, 1)
                late(i, 0)
                early(i + 1, 0)
                late(i, 1)
            early(E1 // W - 1, 1)
            late(E1 // W - 1, 0)
            late(E1 // W - 1, 1)

        @block.sync
        def _(sp):
            with sp.Fori(1, E1 // W) as i:
                for s in range(W):
                    sp.wait_ge(S["made"][s], i)
                    load_slot2(sp, g, i, s)
            g.clear_before(sp)

        @block.tensor
        def _(pe):
            def make(i, s):
                pe.wait_ge(loaded[s], 16 * (i + 1))
                pe.wait_ge(S["means"][s], i + 1)
                pe.wait_ge(S["normed"][s], i)
                for b in range(2):
                    for c in range(2):
                        last = nc.tensor.matmul(g.ps[4 * s + b][:, 0:2 * DIM], mean_k[s][:, c, :],
                                                weight[s][:, c, b * 2 * DIM:(b + 1) * 2 * DIM],
                                                start=(c == 0), stop=(c == 1))
                last.then_inc(S["made"][s], 1)

            def turn(i, s):
                pe.wait_ge(S["normed"][s], i + 1)
                pe.wait_ge(S["kept_v"][s], i)
                pe.wait_ge(S["kept_s"][s], i)
                for c in range(2):
                    for e in range(E2):
                        last = nc.tensor.transpose(g.ps[4 * s + 2 + c][0:HALF, e * P:(e + 1) * P],
                                                   se[s][:, e, c * HALF:(c + 1) * HALF], g.ident[:, :])
                last.then_inc(S["turned"][s], 1)

            pipeline(pe, make, turn)

        def dest(i, s, c):
            return g.se2_t[:, c, :, ds((W * i + s) * E2 * MEAN, E2 * MEAN)].rearrange(
                "p g (e m) -> p e g m", e=E2)

        def source(s, c):
            return g.ps[4 * s + 2 + c][0:HALF, :].rearrange("p (e g m) -> p e g m", e=E2, m=MEAN)

        @block.scalar
        def _(act):

            def root(i, s):
                act.wait_ge(S["made"][s], i + 1)
                for e in range(E2):
                    act.wait_ge(S["squared"][s], E2 * i + e)
                    nc.scalar.activation(square[s][:, :],
                                         g.ps[4 * s + e // 2][:, (e % 2) * DIM:(e % 2 + 1) * DIM], ACT.Square,
                                         accum_out=ss[s][:, e:e + 1]).then_inc(S["squared"][s], 1)
                act.wait_ge(S["squared"][s], E2 * (i + 1))
                nc.scalar.activation(log_s[s][:, :], ss[s][:, :], ACT.Ln, scale=1.0 / DIM,
                                     bias=g.eps_dim[:, :]).then_inc(S["logged"][s], 1)
                act.wait_ge(S["logged"][s], i + 1)
                nc.scalar.activation(factor[s][:, :], log_s[s][:, :], ACT.Exp, scale=-0.5
                                     ).then_inc(S["rooted"][s], 1)

            def keep(i, s):
                act.wait_ge(S["turned"][s], i + 1)
                nc.scalar.nop(nofuse=True)
                nc.scalar.copy(dest(i, s, 1), source(s, 1)).then_inc(S["kept_s"][s], 1)

            pipeline(act, root, keep)

        @block.vector
        def _(dve):
            def norm(i, s):
                dve.wait_ge(S["rooted"][s], i + 1)
                nc.vector.tensor_tensor(
                    se[s][:, :, :].rearrange("p (b e) d -> p b e d", b=2),
                    g.psum[:, 4 * s:4 * s + 2, 0:2 * DIM].rearrange("p b (e d) -> p b e d", e=2),
                    factor[s][:, :].rearrange("p (b e) -> p b e", b=2).unsqueeze(3).broadcast_to(
                        (P, 2, 2, DIM)), ALU.mult).then_inc(S["normed"][s], 1)

            def keep(i, s):
                dve.wait_ge(S["turned"][s], i + 1)
                nc.vector.nop(nofuse=True)
                nc.vector.tensor_copy(dest(i, s, 0), source(s, 0)).then_inc(S["kept_v"][s], 1)

            def fetch(i, s):
                dve.wait_ge(S["made"][s], i)
                nc.vector.nop(nofuse=True)
                nc.vector.tensor_copy(mean_k[s][:, :, :].unsqueeze(2),
                                      g.means_t[:, :, ds(W * i + s, 1), :, :].rearrange("p c k g m -> p c k (g m)")
                                      ).then_inc(S["means"][s], 1)

            pipeline(dve, norm, keep, fetch)


def second_dispatch(nc, g):
    g.next_stage()
    with ExitStack() as ctx:
        def sb(name, shape, dt=F32):
            return [ctx.enter_context(nc.sbuf_tensor(f"sd_{name}{s}", shape, dt)) for s in range(W)]

        sem = lambda name: g.stage_semaphore(nc.semaphore("sd_" + name))
        yn = sb("yn", [P, GPS, DIM])
        yn_t = [w[:, :, 0:GPS * P] for w in g.w_slot2]
        logits = sb("logits", [P, GPS, P])
        neg_row = sb("neg_row", [P, GPS])
        neg_col = sb("neg_col", [P, GPS])
        sum_row = sb("sum_row", [P, GPS])
        sum_col = sb("sum_col", [P, GPS])
        inv_row = sb("inv_row", [P, GPS])
        inv_col = sb("inv_col", [P, GPS])
        comb = sb("comb", [P, GPS, P])
        disp_t = sb("disp_t", [P, GPS, P])
        disp = sb("disp", [P, GPS, P])
        S = {n: sem(n) for n in (
            "fetched", "yn_turned", "yn_kept_s", "yn_kept_v", "logits_made", "masked", "row_maxed",
            "row_exped", "row_inverted", "combined", "logits_turned", "col_maxed", "col_exped",
            "col_inverted", "dispatched", "disp_turned", "disp_kept", "weights_made", "weights_kept",
            "inputs_made", "inputs_kept_s", "inputs_kept_v")}
        at = lambda i, s, per=1: (W * i + s + 1) * per
        block = ctx.enter_context(nc.Block())
        cols4 = lambda bank: bank.rearrange("p (g n) -> p g n", g=GPS)

        @block.sync
        def _(sp):
            g.clear_before(sp)

        @block.gpsimd
        def _(pool):
            nc.gpsimd.memset(g.slots2_t[HALF:AUG, 1, :, :], 1.0).then_inc(g.input_ones, 1)

        @block.tensor
        def _(pe):
            with pe.Fori(0, STEPS) as i:
                for s in range(W):
                    pe.wait_ge(S["fetched"], W * (i + 1))
                    pe.wait_ge(S["disp_kept"], W * i)
                    pe.wait_ge(S["weights_kept"], W * i)
                    for c in range(2):
                        for gr in range(GPS):
                            last = nc.tensor.transpose(g.ps[4 * s + c][0:HALF, gr * P:(gr + 1) * P],
                                                       yn[s][:, gr, c * HALF:(c + 1) * HALF], g.ident[:, :])
                    last.then_inc(S["yn_turned"], 1)
                for s in range(W):
                    pe.wait_ge(S["yn_kept_s"], at(i, s))
                    pe.wait_ge(S["yn_kept_v"], at(i, s))
                    pe.wait_ge(S["inputs_kept_v"], W * i)
                    pe.wait_ge(S["inputs_kept_s"], W * i)
                    for gr in range(GPS):
                        for c in range(2):
                            last = nc.tensor.matmul(
                                g.ps[4 * s + 2][:, gr * P:(gr + 1) * P], yn_t[s][:, c, gr * P:(gr + 1) * P],
                                g.se2_t[:, c, ds((W * i + s) * GPS + gr, 1), :].rearrange("p a n -> p (a n)"),
                                start=(c == 0), stop=(c == 1))
                    last.then_inc(S["logits_made"], 1)
                for s in range(W):
                    pe.wait_ge(S["masked"], at(i, s))
                    for gr in range(GPS):
                        last = nc.tensor.transpose(g.ps[4 * s + 3][:, gr * P:(gr + 1) * P], logits[s][:, gr, :],
                                                   g.ident[:, :])
                    last.then_inc(S["logits_turned"], 1)
                for s in range(W):
                    pe.wait_ge(S["combined"], at(i, s))
                    for gr in range(GPS):
                        last = nc.tensor.matmul(
                            g.ps[4 * s + 1][:, gr * GROUP:(gr + 1) * GROUP], comb[s][:, gr, :],
                            g.comb_t[:, ds((W * i + s) * SEQ + gr * GROUP, GROUP)], start=True, stop=True)
                    last.then_inc(S["weights_made"], 1)
                for s in range(W):
                    pe.wait_ge(S["dispatched"], at(i, s))
                    for gr in range(GPS):
                        last = nc.tensor.transpose(g.ps[4 * s][:, gr * P:(gr + 1) * P], disp_t[s][:, gr, :],
                                                   g.ident[:, :])
                    last.then_inc(S["disp_turned"], 1)
                for s in range(W):
                    pe.wait_ge(S["disp_kept"], at(i, s))
                    for c in range(2):
                        for gr in range(GPS):
                            last = nc.tensor.matmul(g.ps[4 * s + 2 + c][0:HALF, gr * P:(gr + 1) * P],
                                                    yn[s][:, gr, c * HALF:(c + 1) * HALF], disp[s][:, gr, :],
                                                    start=True, stop=True)
                    last.then_inc(S["inputs_made"], 1)

        def inputs(i, s, c):
            out = g.slots2_t[0:HALF, c, :, ds((W * i + s) * GPS * MEAN, GPS * MEAN)].rearrange(
                "p k (g m) -> p k g m", m=MEAN)
            return out, g.ps[4 * s + 2 + c][0:HALF, :].rearrange("p (g k m) -> p k g m", g=GPS, m=MEAN)

        @block.scalar
        def _(act):
            with act.Fori(0, STEPS) as i:
                act.wait_ge(S["inputs_made"], W * i)
                nc.scalar.nop(nofuse=True)
                nc.scalar.copy(yn[0][:, :, :], g.yn[:, ds(W * i * GPS, GPS), :]).then_inc(S["fetched"], 1)
                for s in range(W):
                    act.wait_ge(S["yn_turned"], at(i, s))
                    nc.scalar.copy(yn_t[s][:, 0, :], g.ps[4 * s][0:HALF, :]).then_inc(S["yn_kept_s"], 1)
                for s in range(W):
                    act.wait_ge(S["row_maxed"], at(i, s))
                    for gr in range(GPS):
                        nc.scalar.activation(comb[s][:, gr, :], logits[s][:, gr, :], ACT.Exp,
                                             bias=neg_row[s][:, gr:gr + 1], accum_out=sum_row[s][:, gr:gr + 1]
                                             ).then_inc(S["row_exped"], 1)
                for s in range(W):
                    act.wait_ge(S["col_maxed"], at(i, s))
                    for gr in range(GPS):
                        nc.scalar.activation(disp_t[s][:, gr, :], g.ps[4 * s + 3][:, gr * P:(gr + 1) * P], ACT.Exp,
                                             bias=neg_col[s][:, gr:gr + 1], accum_out=sum_col[s][:, gr:gr + 1]
                                             ).then_inc(S["col_exped"], 1)
                for s in range(W):
                    act.wait_ge(S["disp_turned"], at(i, s))
                    nc.scalar.copy(disp[s][:, :, :], cols4(g.ps[4 * s])).then_inc(S["disp_kept"], 1)
                for s in range(W):
                    act.wait_ge(S["inputs_made"], at(i, s))
                    nc.scalar.nop(nofuse=True)
                    out, of = inputs(i, s, 1)
                    nc.scalar.copy(out, of).then_inc(S["inputs_kept_s"], 1)

        @block.vector
        def _(dve):
            with dve.Fori(0, STEPS) as i:
                dve.wait_ge(S["inputs_made"], W * i)
                nc.vector.nop(nofuse=True)
                nc.vector.tensor_copy(yn[1][:, :, :], g.yn[:, ds((W * i + 1) * GPS, GPS), :]
                                      ).then_inc(S["fetched"], 1)
                for s in range(W):
                    dve.wait_ge(S["yn_turned"], at(i, s))
                    nc.vector.tensor_copy(yn_t[s][:, 1, :], g.ps[4 * s + 1][0:HALF, :]
                                          ).then_inc(S["yn_kept_v"], 1)
                for s in range(W):
                    dve.wait_ge(S["logits_made"], at(i, s))
                    nc.vector.tensor_tensor(logits[s][:, :, :], cols4(g.ps[4 * s + 2]),
                                            g.block_mask[:, :].unsqueeze(1).broadcast_to((P, GPS, P)), ALU.add
                                            ).then_inc(S["masked"], 1)
                    dve.wait_ge(S["masked"], at(i, s))
                    nc.vector.tensor_reduce(neg_row[s][:, :], logits[s][:, :, :], AX.X, ALU.max, negate=True
                                            ).then_inc(S["row_maxed"], 1)
                for s in range(W):
                    dve.wait_ge(S["logits_turned"], at(i, s))
                    nc.vector.tensor_reduce(neg_col[s][:, :], cols4(g.ps[4 * s + 3]), AX.X, ALU.max, negate=True
                                            ).then_inc(S["col_maxed"], 1)
                for s in range(W):
                    dve.wait_ge(S["row_exped"], at(i, s, GPS))
                    nc.vector.reciprocal(inv_row[s][:, :], sum_row[s][:, :]).then_inc(S["row_inverted"], 1)
                    dve.wait_ge(S["row_inverted"], at(i, s))
                    nc.vector.tensor_tensor(comb[s][:, :, :], comb[s][:, :, :],
                                            inv_row[s][:, :].unsqueeze(2).broadcast_to((P, GPS, P)), ALU.mult
                                            ).then_inc(S["combined"], 1)
                for s in range(W):
                    dve.wait_ge(S["col_exped"], at(i, s, GPS))
                    nc.vector.reciprocal(inv_col[s][:, :], sum_col[s][:, :]).then_inc(S["col_inverted"], 1)
                    dve.wait_ge(S["col_inverted"], at(i, s))
                    nc.vector.tensor_tensor(disp_t[s][:, :, :], disp_t[s][:, :, :],
                                            inv_col[s][:, :].unsqueeze(2).broadcast_to((P, GPS, P)), ALU.mult
                                            ).then_inc(S["dispatched"], 1)
                for s in range(W):
                    dve.wait_ge(S["weights_made"], at(i, s))
                    nc.vector.nop(nofuse=True)
                    nc.vector.tensor_copy(g.mix_t[:, ds((W * i + s) * SEQ, SEQ)], g.ps[4 * s + 1][:, 0:SEQ]
                                          ).then_inc(S["weights_kept"], 1)
                for s in range(W):
                    dve.wait_ge(S["inputs_made"], at(i, s))
                    nc.vector.nop(nofuse=True)
                    out, of = inputs(i, s, 0)
                    nc.vector.tensor_copy(out, of).then_inc(S["inputs_kept_v"], 1)


def experts(nc, g):
    g.next_stage()
    HB = HID // P
    with ExitStack() as ctx:
        def sb(name, shape, dt=F32):
            return [ctx.enter_context(nc.sbuf_tensor(f"ex_{name}{u}", shape, dt)) for u in range(2)]

        sem = lambda name: g.stage_semaphore(nc.semaphore("ex_" + name))
        gelu = sb("gelu", [P, HID])
        act_t = sb("act_t", [P, HID])
        rows = sb("rows", [P, DIM])
        S = {n: sem(n) for n in ("gates", "values", "gelued", "acted", "made", "kept")}
        written = [sem(f"written{e}") for e in range(E2)]
        gathered = sem("gathered")
        block = ctx.enter_context(nc.Block())
        gate_bank, value_bank, out_bank = (lambda e: g.ps[4 * (e % 2)], lambda e: g.ps[4 * (e % 2) + 1],
                                           lambda e: g.ps[4 * (e % 2) + 2])

        @block.sync
        def _(sp):
            g.clear_before(sp)
            with sp.Fori(1, E1) as k:
                for e in range(E2):
                    sp.wait_ge(S["values"], E2 * (k - 1) + e + 1)
                    sp.wait_ge(S["made"], E2 * (k - 1) + e + 1)
                    load_expert(sp, g, k, e)

        @block.tensor
        def _(pe):
            pe.wait_ge(g.input_ones, 1)

            def hidden(k, e):
                n = E2 * k + e
                pe.wait_ge(g.w1_loaded[e], 16 * (k + 1))
                x = lambda c: g.slots2_t[0:HALF + c, c, ds(n, 1), :].rearrange("p a n -> p (a n)")
                for bank, first, done, free in ((gate_bank(e), HID, "gates", "gelued"),
                                                (value_bank(e), 0, "values", "acted")):
                    if e >= 2:
                        pe.wait_ge(S[free], n - 1)
                    else:
                        pe.wait_ge(S[free], E2 * k)
                    for j in range(HB):
                        for c in range(2):
                            last = nc.tensor.matmul(
                                bank[:, j * P:(j + 1) * P],
                                g.w1[e][0:HALF + c, c, first + j * P:first + (j + 1) * P], x(c),
                                start=(c == 0), stop=(c == 1))
                    last.then_inc(S[done], 1)

            def output(k, e):
                n = E2 * k + e
                pe.wait_ge(S["acted"], n + 1)
                pe.wait_ge(g.w2_loaded[e], 16 * (k + 1))
                if e >= 2:
                    pe.wait_ge(S["kept"], n - 1)
                else:
                    pe.wait_ge(S["kept"], E2 * k)
                for j in range(HB):
                    last = nc.tensor.matmul(out_bank(e)[:, 0:DIM], act_t[e % 2][:, j * P:(j + 1) * P],
                                            g.w2[e][:, j, :], start=(j == 0), stop=(j == HB - 1))
                last.then_inc(S["made"], 1)

            with pe.Fori(0, E1) as k:
                hidden(k, 0)
                for e in range(1, E2):
                    hidden(k, e)
                    output(k, e - 1)
                output(k, E2 - 1)

        @block.scalar
        def _(act):
            def gate(k, e):
                n = E2 * k + e
                act.wait_ge(S["gates"], n + 1)
                if e >= 2:
                    act.wait_ge(S["acted"], n - 1)
                else:
                    act.wait_ge(S["acted"], E2 * k)
                nc.scalar.activation(gelu[e % 2][:, :], gate_bank(e)[:, :], ACT.Gelu_apprx_tanh
                                     ).then_inc(S["gelued"], 1)

            def keep(k, e):
                n = E2 * k + e
                act.wait_ge(S["made"], n + 1)
                if e >= 2:
                    act.wait_ge(written[e - 2], 16 * (k + 1))
                else:
                    act.wait_ge(written[e + 2], 16 * k)
                nc.scalar.copy(rows[e % 2][:, :], out_bank(e)[:, 0:DIM]).then_inc(S["kept"], 1)
                act.wait_ge(S["kept"], n + 1)
                act.dma_start(g.scratch[ds(k, 1), e].rearrange("a p n -> (a p) n"), rows[e % 2][:, :]
                              ).then_inc(written[e], 16)

            with act.Fori(0, E1) as k:
                gate(k, 0)
                for e in range(1, E2):
                    gate(k, e)
                    keep(k, e - 1)
                keep(k, E2 - 1)

        @block.vector
        def _(dve):
            with dve.Fori(0, E1) as k:
                for e in range(E2):
                    n = E2 * k + e
                    dve.wait_ge(S["gelued"], n + 1)
                    dve.wait_ge(S["values"], n + 1)
                    if e >= 2:
                        dve.wait_ge(S["made"], n - 1)
                    else:
                        dve.wait_ge(S["made"], E2 * k)
                    nc.vector.tensor_tensor(act_t[e % 2][:, :], value_bank(e)[:, :], gelu[e % 2][:, :], ALU.mult
                                            ).then_inc(S["acted"], 1)

        @block.gpsimd
        def _(pool):
            for k in range(E1):
                for e in range(E2):
                    p0 = (k * E2 + e) * MEAN
                    pool.wait_ge(written[e], 16 * (k + 1))
                    pool.dma_start(g.yn[p0:p0 + MEAN, :, :],
                                   g.scratch[k, e].rearrange("(g m) d -> m g d", m=MEAN)).then_inc(gathered, 16)
            pool.wait_ge(gathered, 16 * E1 * E2)


def combine(nc, g):
    g.next_stage()
    with ExitStack() as ctx:
        def sb(name, shape, dt=F32):
            return [ctx.enter_context(nc.sbuf_tensor(f"co_{name}{s}", shape, dt)) for s in range(WIDE)]

        sem = lambda name: g.stage_semaphore(nc.semaphore("co_" + name))
        rows = sb("rows", [P, GPS, DIM])
        mix = sb("mix", [P, SEQ])
        final = sb("final", [P, TPS, DIM])
        S = {n: sem(n) for n in ("biased_even", "biased_odd", "fetched", "added")}
        mixed = [sem(f"mixed{s}") for s in range(WIDE)]
        stored = [sem(f"stored{s}") for s in range(WIDE)]
        at = lambda i, s: WIDE * i + s + 1
        block = ctx.enter_context(nc.Block())

        def add_bias(i, s):
            return (rows[s][:, :, :], g.yn[:, ds((WIDE * i + s) * GPS, GPS), :],
                    g.t["b2"].unsqueeze(1).broadcast_to((P, GPS, DIM)), ALU.add)

        @block.vector
        def _(dve):
            with dve.Fori(0, BATCH // WIDE) as i:
                for s in range(0, WIDE, 2):
                    dve.wait_ge(mixed[s], i)
                    nc.vector.tensor_tensor(*add_bias(i, s)).then_inc(S["biased_even"], 1)
                for s in range(WIDE):
                    dve.wait_ge(stored[s], 16 * i)
                    dve.wait_ge(mixed[s], i + 1)
                    nc.vector.tensor_tensor(final[s][:, :, :], g.h[:, ds((WIDE * i + s) * TPS, TPS), :],
                                            g.ps[s][:, 0:TPS * DIM].rearrange("p (t d) -> p t d", t=TPS), ALU.add
                                            ).then_inc(S["added"], 1)

        @block.gpsimd
        def _(pool):
            with pool.Fori(0, BATCH // WIDE) as i:
                for s in range(1, WIDE, 2):
                    pool.wait_ge(mixed[s], i)
                    nc.gpsimd.nop(nofuse=True)
                    nc.gpsimd.tensor_tensor(*add_bias(i, s)).then_inc(S["biased_odd"], 1)

        @block.scalar
        def _(act):
            with act.Fori(0, BATCH // WIDE) as i:
                for s in range(WIDE):
                    act.wait_ge(mixed[s], i)
                    nc.scalar.nop(nofuse=True)
                    nc.scalar.copy(mix[s][:, :], g.mix_t[:, ds((WIDE * i + s) * SEQ, SEQ)]
                                   ).then_inc(S["fetched"], 1)

        @block.tensor
        def _(pe):
            with pe.Fori(0, BATCH // WIDE) as i:
                for s in range(WIDE):
                    pe.wait_ge(S["biased_odd" if s % 2 else "biased_even"], WIDE // 2 * i + s // 2 + 1)
                    pe.wait_ge(S["fetched"], at(i, s))
                    pe.wait_ge(S["added"], WIDE * i)
                    for gr in range(GPS):
                        r0, t = GROUP * (gr % 2), gr // 2
                        last = nc.tensor.matmul(
                            g.ps[s][r0:r0 + GROUP, t * DIM:(t + 1) * DIM], mix[s][:, gr * GROUP:(gr + 1) * GROUP],
                            rows[s][:, gr, :], start=True, stop=True)
                    last.then_inc(mixed[s], 1)

        @block.sync
        def _(sp):
            g.clear_before(sp)
            with sp.Fori(0, BATCH // WIDE) as i:
                for s in range(WIDE):
                    sp.wait_ge(S["added"], at(i, s))
                    sp.dma_start(g.out[:, ds((WIDE * i + s) * TPS, TPS), :], final[s][:, :, :]
                                 ).then_inc(stored[s], 16)
            for s in range(WIDE):
                sp.wait_ge(stored[s], 16 * BATCH // WIDE)


def tower(nc, d, out):
    g = Shared()
    g.d, g.out = d, out
    with ExitStack() as ctx:
        sb = lambda name, shape, dt=F32: ctx.enter_context(nc.sbuf_tensor(name, shape, dt))
        sem = lambda name: ctx.enter_context(nc.semaphore(name))
        g.psum = ctx.enter_context(nc.psum_tensor("banks", [P, 8, 512], F32))
        g.ps = [g.psum[:, n, :] for n in range(8)]
        g.h = sb("h", [P, TILES, DIM])
        g.ident = sb("ident", [P, P])
        g.average = sb("average", [P, P // MEAN])
        g.block_mask = sb("block_mask", [P, P])
        g.eps5, g.eps6, g.rms_eps, g.eps_norms, g.eps_dim = (
            sb(name, [P, 1]) for name in ("eps5", "eps6", "rms_eps", "eps_norms", "eps_dim"))
        g.phi_t = sb("phi_t", [HALF, 2, P])
        g.w1 = [sb(f"w1_{e}", [AUG, 2, 2 * HID]) for e in range(E2)]
        g.w2 = [sb(f"w2_{e}", [P, HID // P, DIM]) for e in range(E2)]
        g.w1_loaded = [sem(f"w1_loaded{e}") for e in range(E2)]
        g.w2_loaded = [sem(f"w2_loaded{e}") for e in range(E2)]
        g.scratch = nc.dram_tensor("rows_scratch", (E1, E2, P, DIM), F32, kind="Internal").ap()
        g.ids_loaded, g.gathered, g.operands_loaded = sem("ids_loaded"), sem("gathered"), sem("operands_loaded")
        g.ident_made, g.masks_made, g.consts_set = sem("ident_made"), sem("masks_made"), sem("consts_set")
        g.folds_ready, g.ones_set, g.input_ones = sem("folds_ready"), sem("ones_set"), sem("input_ones")

        def operands(scope, names):
            for n in names:
                g.t[n] = scope.enter_context(nc.sbuf_tensor(n + "_sb", list(d[n].shape), F32))[
                    tuple(slice(None) for _ in d[n].shape)]

        operands(ctx, MOE_OPERANDS)
        with ExitStack() as front:
            fsb = lambda name, shape, dt=F32: front.enter_context(nc.sbuf_tensor(name, shape, dt))
            operands(front, FRONT_OPERANDS)
            g.ids = fsb("ids", [P, TILES], U32)
            g.mean_all = fsb("mean_all", [P, P])
            g.xt = [fsb(f"xt{s}", [AUG, 2, SEQ]) for s in range(WIDE)]
            g.qk_fold = fsb("qk_fold", [AUG, 2, DIM + 1])
            g.vo_fold = fsb("vo_fold", [AUG, 2, DIM])
            g.mlp_fold = fsb("mlp_fold", [AUG, 2, DIM])
            g.q_t = [fsb(f"q_t{s}", [KM, HEADS, SEQ], BF16) for s in range(2)]
            g.k_t = [fsb(f"k_t{s}", [KM, HEADS, SEQ], BF16) for s in range(2)]
            g.val = [fsb(f"val{s}", [P, TPS, HEADS, 32]) for s in range(2)]
            g.ident_b = fsb("ident_b", [P, P], BF16)
            g.qk_weight = fsb("qk_weight", [P, HDIM])
            fold_weights(nc, g)
            token_mixer(nc, g)
            attention(nc, g)
        g.yn = sb("yn_all", [P, NGROUPS, DIM])
        g.w_slot2 = [sb(f"w_slot2_{s}", [HALF, 2, E2 * DIM]) for s in range(W)]
        g.w_slot2_loaded = [sem(f"w_slot2_loaded{s}") for s in range(W)]
        g.comb_t = sb("comb_t", [P, BATCH * SEQ])
        g.means_t = sb("means_t", [HALF, 2, E1, NGROUPS, MEAN])
        first_slots(nc, g)
        g.slots2_t = sb("slots2_t", [AUG, 2, E1 * E2, NGROUPS * MEAN])
        g.mix_t = sb("mix_t", [P, BATCH * SEQ])
        with ExitStack() as second:
            g.se2_t = second.enter_context(nc.sbuf_tensor("se2_t", [HALF, 2, NGROUPS, P], F32))
            second_slots(nc, g)
            second_dispatch(nc, g)
        experts(nc, g)
        combine(nc, g)


def layouts(inputs):
    f = lambda n: np.asarray(inputs[n])
    cat, c = np.concatenate, np.ascontiguousarray

    def halves(w):
        return c(cat([w[:DIM].reshape(2, HALF, -1), np.stack([w[DIM:], w[DIM:]])], 1).transpose(1, 0, 2))

    def hidden(w, b):
        return c(cat([w, b[None]], 0).T.reshape(HC, P, DIM + 1).transpose(1, 0, 2))

    def hid_rows(w):
        return c(w.reshape(HC, P, DIM).transpose(1, 0, 2))

    def seq_tiles(w):
        return c(w.reshape(TPS, P, DIM).transpose(1, 0, 2))

    d = {
        "ids": c(f("x").reshape(TILES, P).T).view(np.uint32),
        "emb": c(f("L0_tok_emb")),
        "wq_t": hidden(f("L0_tok_Wq"), f("L0_tok_bq")),
        "wk_t": hidden(f("L0_tok_Wk"), f("L0_tok_bk")),
        "wv_t": hidden(f("L0_tok_Wv"), f("L0_tok_bv")),
        "w1_t": hidden(f("L0_tok_W1"), f("L0_tok_b1")),
        "wo": hid_rows(f("L0_tok_Wo")),
        "w2": hid_rows(f("L0_tok_W2")),
        "tail_bias": c(np.stack([f("L0_tok_bo"), f("L0_tok_b2")])[None]),
        "ln_w1": seq_tiles(f("L0_tok_ln1_w")), "ln_b1": seq_tiles(f("L0_tok_ln1_b")),
        "ln_w2": seq_tiles(f("L0_tok_ln2_w")), "ln_b2": seq_tiles(f("L0_tok_ln2_b")),
        "pos": seq_tiles(pos_encoding()),
        "qkv_t": halves(cat([f("L0_attn_qkv_w").T, f("L0_attn_qkv_b")[None]], 0)),
        "proj_t": halves(cat([f("L0_attn_proj_w").T, f("L0_attn_proj_b")[None]], 0)),
        "qk_weights": c(np.broadcast_to(np.stack([f("L0_attn_q_norm_w"), f("L0_attn_k_norm_w")]), (P, 2, HDIM))),
        "gamma_in": c(np.broadcast_to(f("L0_ffn_gamma_in"), (P, DIM))),
        "slots1": c(f("L0_ffn_slots1").reshape(P, DIM)),
        "gamma2": c(np.repeat(f("L0_ffn_gamma2"), S1, 0)),
        "b2": c(np.repeat(f("L0_ffn_b2").reshape(E1 * E2, DIM), MEAN, 0)),
        "w_slot2": c(f("L0_ffn_w_slot2").reshape(E1, 2, HALF, E2 * DIM).transpose(0, 2, 1, 3)),
        "w1": c(cat([f("L0_ffn_w1").reshape(E1, E2, 2, HALF, 2 * HID),
                     np.broadcast_to(f("L0_ffn_b1")[:, :, None, None, :], (E1, E2, 2, 1, 2 * HID))], 3
                    ).transpose(0, 1, 3, 2, 4)),
        "w2e": c(f("L0_ffn_w2").reshape(E1, E2, HID // P, P, DIM).transpose(0, 1, 3, 2, 4)),
    }
    return d


def kernel(**inputs):
    from concourse import bacc
    from concourse.bass_utils import run_bass_kernel_spmd

    nc = bacc.Bacc("TRN2", target_bir_lowering=False, num_devices=1)
    arrays = layouts(inputs)
    d = {n: nc.dram_tensor("in_" + n, a.shape, mybir.dt.from_np(a.dtype), kind="ExternalInput").ap()
         for n, a in arrays.items()}
    out = nc.dram_tensor("out", (P, TILES, DIM), F32, kind="ExternalOutput").ap()
    tower(nc, d, out)
    r = run_bass_kernel_spmd(nc, [{"in_" + n: a for n, a in arrays.items()}], core_ids=[0])
    got = r.results[0]["out"]
    return np.ascontiguousarray(got.transpose(1, 0, 2)).reshape(BATCH, SEQ, DIM)
```
